# Optimizing a Trainium2 kernel written in Bass

```python
import numpy as np
import jax
import jax.numpy as jnp

def _softmax(x, axis=-1):
    return jax.nn.softmax(x, axis=axis)

def _gelu(x):
    return jax.nn.gelu(x, approximate=True)

def _silu(x):
    return jax.nn.silu(x)

def _sigmoid(x):
    return jax.nn.sigmoid(x)

def _layernorm(x, axis=-1, eps=1e-05):
    m = jnp.mean(x, axis=axis, keepdims=True)
    v = jnp.var(x, axis=axis, keepdims=True)
    return (x - m) / jnp.sqrt(v + eps)

def _scatter_add(tgt, idx, src, axis=0):
    return tgt.at[idx].add(src)

def _segment_sum(src, seg, n):
    return jax.ops.segment_sum(src, seg, n)
kernel_name = 'mk_vit_tower_d2_tok_img768_r4_6fbaff'

def setup_inputs(seed: int=0):
    np.random.seed(seed)
    _w = jnp.asarray

    def _rec_inputs():
        import jax
        import jax.numpy as jnp
        _rk = jax.random.key(seed)
        x = -9.30917e-05 + 1.0002 * jax.random.normal(jax.random.fold_in(_rk, 1), (64, 3, 96, 96), jnp.float32)
        return x
    x = _rec_inputs()

    def _L0_tok_setup():
        import jax, jax.numpy as jnp
        import numpy as np
        PATCH = 16
        EPS = 1e-05

        def _shift(x, pad_spec):
            l, r, t, b = pad_spec
            H, W = (x.shape[2], x.shape[3])
            xp = jnp.pad(x, ((0, 0), (0, 0), (max(t, 0), max(b, 0)), (max(l, 0), max(r, 0))))
            h0 = -t if t < 0 else 0
            w0 = -l if l < 0 else 0
            return xp[:, :, h0:h0 + H, w0:w0 + W]
        key = jax.random.key(seed)
        k1, k2 = jax.random.split(key)
        B, C, H, Wd = (32, 3, 224, 224)
        patch_dim = PATCH * PATCH * 5 * C
        dim = 192
        x = jax.random.normal(k1, (B, C, H, Wd), dtype=jnp.float32)
        ln_gamma = jnp.ones((patch_dim,), dtype=jnp.float32)
        ln_beta = jnp.zeros((patch_dim,), dtype=jnp.float32)
        W = jax.random.normal(k2, (patch_dim, dim), dtype=jnp.float32) * patch_dim ** (-0.5)
        b = jnp.zeros((dim,), dtype=jnp.float32)
        return {'x': x, 'ln_gamma': ln_gamma, 'ln_beta': ln_beta, 'W': W, 'b': b}
    _L0_tok_all = _L0_tok_setup()
    _L0_tok_in = {k: v for k, v in _L0_tok_all.items() if k in ('ln_gamma', 'ln_beta', 'W', 'b')}
    del _L0_tok_all

    def _L0_attn_setup():
        import jax, jax.numpy as jnp
        import numpy as np
        import math
        D_MODEL = 192
        N_HEADS = 12
        B, L = (2, 512)
        ALPHA = 0.3
        key = jax.random.key(seed)
        ks = jax.random.split(key, 7)
        s = 0.02
        return {'x': jax.random.normal(ks[0], (B, L, D_MODEL), dtype=jnp.float32), 'Wqkv_w': jax.random.normal(ks[1], (D_MODEL, 3 * D_MODEL), dtype=jnp.float32) * s, 'Wqkv_b': jax.random.normal(ks[2], (3 * D_MODEL,), dtype=jnp.float32) * s, 'sel_w': jax.random.normal(ks[3], (D_MODEL, 2), dtype=jnp.float32) * s, 'sel_b': jax.random.normal(ks[4], (2,), dtype=jnp.float32) * s, 'out_w': jax.random.normal(ks[5], (D_MODEL, D_MODEL), dtype=jnp.float32) * s, 'out_b': jax.random.normal(ks[6], (D_MODEL,), dtype=jnp.float32) * s, 'temperature': jnp.ones((1,), dtype=jnp.float32) * (math.sqrt(D_MODEL) * ALPHA)}
    _L0_attn_all = _L0_attn_setup()
    _L0_attn_in = {k: v for k, v in _L0_attn_all.items() if k in ('Wqkv_w', 'Wqkv_b', 'sel_w', 'sel_b', 'out_w', 'out_b', 'temperature')}
    del _L0_attn_all

    def _L0_ffn_setup():
        import jax, jax.numpy as jnp
        import numpy as np
        B, N, D, E, K = (4, 1024, 192, 8, 2)
        H = 4 * D
        LN_EPS = 1e-05
        key = jax.random.key(seed)
        ks = jax.random.split(key, 9)
        s_d = 1.0 / np.sqrt(D)
        s_h = 1.0 / np.sqrt(H)
        return {'x': jax.random.normal(ks[0], (B, N, D), dtype=jnp.float32), 'router_w': jax.random.normal(ks[1], (D, E), dtype=jnp.float32) * s_d, 'router_b': jnp.zeros((E,), dtype=jnp.float32), 'w1': jax.random.normal(ks[2], (E, D, H), dtype=jnp.float32) * s_d, 'b1': jnp.zeros((E, H), dtype=jnp.float32), 'w2': jax.random.normal(ks[3], (E, H, D), dtype=jnp.float32) * s_h, 'b2': jnp.zeros((E, D), dtype=jnp.float32), 'gamma': jnp.ones((D,), dtype=jnp.float32), 'beta': jnp.zeros((D,), dtype=jnp.float32)}
    _L0_ffn_all = _L0_ffn_setup()
    _L0_ffn_in = {k: v for k, v in _L0_ffn_all.items() if k in ('router_w', 'router_b', 'w1', 'b1', 'w2', 'b2', 'gamma', 'beta')}
    del _L0_ffn_all

    def _L1_attn_setup():
        import jax, jax.numpy as jnp
        import numpy as np
        INIT_STD = 0.05
        key = jax.random.key(seed)
        k1, k2, k3 = jax.random.split(key, 3)
        b, p, d = (2, 512, 192)
        h, n = (12, 64)
        x = jax.random.normal(k1, (b, p, d), dtype=jnp.float32)
        w_qkv = INIT_STD * jax.random.normal(k2, (h, 3, d, n), dtype=jnp.float32)
        w_o = INIT_STD * jax.random.normal(k3, (h * n, d), dtype=jnp.float32)
        return {'x': x, 'w_qkv': w_qkv, 'w_o': w_o}
    _L1_attn_all = _L1_attn_setup()
    _L1_attn_in = {k: v for k, v in _L1_attn_all.items() if k in ('w_qkv', 'w_o')}
    del _L1_attn_all

    def _L1_ffn_setup():
        import jax, jax.numpy as jnp
        import numpy as np
        H = 192
        I = 96
        E = 16
        G = 4
        TOPK_GROUP = 2
        TOP_K = 4
        SCALE = 2.5
        N_SHARED = 2
        IS = I * N_SHARED
        B, S = (1, 512)

        def _route(x, router_w, router_b, corr_bias):
            logits = x.astype(jnp.float32) @ router_w.T + router_b
            scores = jax.nn.sigmoid(logits)
            sfc = scores + corr_bias[None, :]
            grp = sfc.reshape(-1, G, E // G)
            group_scores = jax.lax.top_k(grp, 2)[0].sum(-1)
            _, gidx = jax.lax.top_k(group_scores, TOPK_GROUP)
            gmask = jax.nn.one_hot(gidx, G, dtype=sfc.dtype).sum(axis=1)
            score_mask = jnp.repeat(gmask, E // G, axis=-1)
            sfc = jnp.where(score_mask > 0, sfc, 0.0)
            _, idx = jax.lax.top_k(sfc, TOP_K)
            w = jnp.take_along_axis(scores, idx, axis=1)
            w = w / (w.sum(-1, keepdims=True) + 1e-20)
            return (idx, w * SCALE)

        def _forward(x3, router_w, router_b, corr_bias, gWg, gbg, gWu, gbu, gWd, gbd, sWg, sbg, sWu, sbu, sWd, sbd):
            orig_shape = x3.shape
            x = x3.reshape(-1, H)
            idx, w = _route(x, router_w, router_b, corr_bias)
            c = (jax.nn.one_hot(idx, E, dtype=w.dtype) * w[..., None]).sum(1)
            h = jax.nn.silu(jnp.einsum('th,ehi->tei', x, gWg) + gbg) * (jnp.einsum('th,ehi->tei', x, gWu) + gbu)
            out_e = jnp.einsum('tei,eih->teh', h, gWd) + gbd
            moe_out = jnp.einsum('te,teh->th', c, out_e)
            hs = jax.nn.silu(x @ sWg + sbg) * (x @ sWu + sbu)
            shared = hs @ sWd + sbd
            return (moe_out + shared).reshape(orig_shape)
        key = jax.random.key(seed)
        ks = jax.random.split(key, 16)
        s = lambda k, shape, fan: jax.random.normal(k, shape, jnp.float32) * fan ** (-0.5)
        return {'hidden_states': jax.random.normal(ks[0], (B, S, H), jnp.float32), 'router_w': s(ks[1], (E, H), H), 'router_b': jnp.zeros((E,), jnp.float32), 'corr_bias': jnp.zeros((E,), jnp.float32), 'gWg': s(ks[2], (E, H, I), H), 'gbg': jnp.zeros((E, I), jnp.float32), 'gWu': s(ks[3], (E, H, I), H), 'gbu': jnp.zeros((E, I), jnp.float32), 'gWd': s(ks[4], (E, I, H), I), 'gbd': jnp.zeros((E, H), jnp.float32), 'sWg': s(ks[5], (H, IS), H), 'sbg': jnp.zeros((IS,), jnp.float32), 'sWu': s(ks[6], (H, IS), H), 'sbu': jnp.zeros((IS,), jnp.float32), 'sWd': s(ks[7], (IS, H), IS), 'sbd': jnp.zeros((H,), jnp.float32)}
    _L1_ffn_all = _L1_ffn_setup()
    _L1_ffn_in = {k: v for k, v in _L1_ffn_all.items() if k in ('router_w', 'router_b', 'corr_bias', 'gWg', 'gbg', 'gWu', 'gbu', 'gWd', 'gbd', 'sWg', 'sbg', 'sWu', 'sbu', 'sWd', 'sbd')}
    del _L1_ffn_all
    return {'x': x, 'L0_tok_ln_gamma': _L0_tok_in['ln_gamma'], 'L0_tok_ln_beta': _L0_tok_in['ln_beta'], 'L0_tok_W': _L0_tok_in['W'], 'L0_tok_b': _L0_tok_in['b'], 'L0_attn_Wqkv_w': _L0_attn_in['Wqkv_w'], 'L0_attn_Wqkv_b': _L0_attn_in['Wqkv_b'], 'L0_attn_sel_w': _L0_attn_in['sel_w'], 'L0_attn_sel_b': _L0_attn_in['sel_b'], 'L0_attn_out_w': _L0_attn_in['out_w'], 'L0_attn_out_b': _L0_attn_in['out_b'], 'L0_attn_temperature': _L0_attn_in['temperature'], 'L0_ffn_router_w': _L0_ffn_in['router_w'], 'L0_ffn_router_b': _L0_ffn_in['router_b'], 'L0_ffn_w1': _L0_ffn_in['w1'], 'L0_ffn_b1': _L0_ffn_in['b1'], 'L0_ffn_w2': _L0_ffn_in['w2'], 'L0_ffn_b2': _L0_ffn_in['b2'], 'L0_ffn_gamma': _L0_ffn_in['gamma'], 'L0_ffn_beta': _L0_ffn_in['beta'], 'L1_attn_w_qkv': _L1_attn_in['w_qkv'], 'L1_attn_w_o': _L1_attn_in['w_o'], 'L1_ffn_router_w': _L1_ffn_in['router_w'], 'L1_ffn_router_b': _L1_ffn_in['router_b'], 'L1_ffn_corr_bias': _L1_ffn_in['corr_bias'], 'L1_ffn_gWg': _L1_ffn_in['gWg'], 'L1_ffn_gbg': _L1_ffn_in['gbg'], 'L1_ffn_gWu': _L1_ffn_in['gWu'], 'L1_ffn_gbu': _L1_ffn_in['gbu'], 'L1_ffn_gWd': _L1_ffn_in['gWd'], 'L1_ffn_gbd': _L1_ffn_in['gbd'], 'L1_ffn_sWg': _L1_ffn_in['sWg'], 'L1_ffn_sbg': _L1_ffn_in['sbg'], 'L1_ffn_sWu': _L1_ffn_in['sWu'], 'L1_ffn_sbu': _L1_ffn_in['sbu'], 'L1_ffn_sWd': _L1_ffn_in['sWd'], 'L1_ffn_sbd': _L1_ffn_in['sbd']}

def reference(x, L0_tok_ln_gamma, L0_tok_ln_beta, L0_tok_W, L0_tok_b, L0_attn_Wqkv_w, L0_attn_Wqkv_b, L0_attn_sel_w, L0_attn_sel_b, L0_attn_out_w, L0_attn_out_b, L0_attn_temperature, L0_ffn_router_w, L0_ffn_router_b, L0_ffn_w1, L0_ffn_b1, L0_ffn_w2, L0_ffn_b2, L0_ffn_gamma, L0_ffn_beta, L1_attn_w_qkv, L1_attn_w_o, L1_ffn_router_w, L1_ffn_router_b, L1_ffn_corr_bias, L1_ffn_gWg, L1_ffn_gbg, L1_ffn_gWu, L1_ffn_gbu, L1_ffn_gWd, L1_ffn_gbd, L1_ffn_sWg, L1_ffn_sbg, L1_ffn_sWu, L1_ffn_sbu, L1_ffn_sWd, L1_ffn_sbd):
    import jax
    import jax.numpy as jnp

    def _L0_tok_ref(x, ln_gamma, ln_beta, W, b):
        import jax, jax.numpy as jnp
        import numpy as np
        PATCH = 16
        EPS = 1e-05

        def _shift(x, pad_spec):
            l, r, t, b = pad_spec
            H, W = (x.shape[2], x.shape[3])
            xp = jnp.pad(x, ((0, 0), (0, 0), (max(t, 0), max(b, 0)), (max(l, 0), max(r, 0))))
            h0 = -t if t < 0 else 0
            w0 = -l if l < 0 else 0
            return xp[:, :, h0:h0 + H, w0:w0 + W]
        shifts = [(1, -1, 0, 0), (-1, 1, 0, 0), (0, 0, 1, -1), (0, 0, -1, 1)]
        xs = jnp.concatenate([x] + [_shift(x, s) for s in shifts], axis=1)
        B, C5, H, Wd = xs.shape
        h, w = (H // PATCH, Wd // PATCH)
        t = xs.reshape(B, C5, h, PATCH, w, PATCH)
        t = t.transpose(0, 2, 4, 3, 5, 1)
        t = t.reshape(B, h * w, PATCH * PATCH * C5)
        mu = jnp.mean(t, axis=-1, keepdims=True)
        var = jnp.var(t, axis=-1, keepdims=True)
        tn = (t - mu) * jax.lax.rsqrt(var + EPS) * ln_gamma + ln_beta
        return jnp.einsum('bnp,pd->bnd', tn, W) + b

    def _L0_attn_ref(x, Wqkv_w, Wqkv_b, sel_w, sel_b, out_w, out_b, temperature):
        import jax, jax.numpy as jnp
        import numpy as np
        import math
        D_MODEL = 192
        N_HEADS = 12
        B, L = (2, 512)
        ALPHA = 0.3
        b, l, d = x.shape
        h = N_HEADS
        hd = d // h
        qkv = (x @ Wqkv_w + Wqkv_b).reshape(b, l, 3, h, hd)
        q, k_, v = (qkv[:, :, 0], qkv[:, :, 1], qkv[:, :, 2])
        scale = 1.0 / math.sqrt(hd)
        scores = jnp.einsum('bthd,bshd->bhts', q, k_ * scale)
        causal_mask = jnp.triu(jnp.full((l, l), -10000.0, dtype=scores.dtype), 1)
        attn = jax.nn.softmax(scores + causal_mask, axis=-1)
        ctx = jnp.einsum('bhts,bshd->bthd', attn, v).reshape(b, l, d)
        attn_output = ctx @ out_w + out_b
        selection = jax.nn.softmax((x @ sel_w + sel_b) / temperature, axis=-1)[..., 1:]
        k_sel = int(math.ceil(math.sqrt(l)))
        _, idx = jax.lax.top_k(selection[..., 0], k_sel)
        gated = attn_output * selection
        src = jnp.take_along_axis(gated, idx[..., None], axis=1)
        y = jax.vmap(lambda xb, ib, sb: xb.at[ib].add(sb))(x, idx, src)
        return y

    def _L0_ffn_ref(x, router_w, router_b, w1, b1, w2, b2, gamma, beta):
        import jax, jax.numpy as jnp
        import numpy as np
        B, N, D, E, K = (4, 1024, 192, 8, 2)
        H = 4 * D
        LN_EPS = 1e-05
        logits = jnp.einsum('bnd,de->bne', x, router_w) + router_b
        topv, topi = jax.lax.top_k(logits, K)
        w = jax.nn.softmax(topv.astype(jnp.float32), axis=-1).astype(x.dtype)
        onehot = (topi[..., None] == jnp.arange(E)).astype(x.dtype)
        we = jnp.einsum('bnk,bnke->bne', w, onehot)
        out = jnp.zeros_like(x)
        for e in range(E):
            h = jax.nn.gelu(jnp.einsum('bnd,dh->bnh', x, w1[e]) + b1[e], approximate=False)
            y_e = jnp.einsum('bnh,hd->bnd', h, w2[e]) + b2[e]
            out = out + y_e * we[..., e:e + 1]
        y = x + out
        mu = jnp.mean(y, axis=-1, keepdims=True)
        var = jnp.mean((y - mu) ** 2, axis=-1, keepdims=True)
        return (y - mu) * jax.lax.rsqrt(var + LN_EPS) * gamma + beta

    def _L1_attn_ref(x, w_qkv, w_o):
        import jax, jax.numpy as jnp
        import numpy as np
        INIT_STD = 0.05
        head_dim = w_qkv.shape[-1]
        qkv = jnp.einsum('bpv,havn->bhapn', x, w_qkv)
        q, k, v = (qkv[:, :, 0], qkv[:, :, 1], qkv[:, :, 2])
        scale = jnp.sqrt(jnp.asarray(head_dim, dtype=x.dtype))
        scores = jnp.einsum('bhqn,bhkn->bhqk', q, k) / scale
        attn = jax.nn.softmax(scores, axis=-1)
        out = jnp.einsum('bhqk,bhkn->bhqn', attn, v)
        b, h, p, n = out.shape
        out = out.transpose(0, 2, 1, 3).reshape(b, p, h * n)
        return jnp.einsum('bpi,ij->bpj', out, w_o)

    def _L1_ffn_ref(hidden_states, router_w, router_b, corr_bias, gWg, gbg, gWu, gbu, gWd, gbd, sWg, sbg, sWu, sbu, sWd, sbd):
        import jax, jax.numpy as jnp
        import numpy as np
        H = 192
        I = 96
        E = 16
        G = 4
        TOPK_GROUP = 2
        TOP_K = 4
        SCALE = 2.5
        N_SHARED = 2
        IS = I * N_SHARED
        B, S = (1, 512)

        def _route(x, router_w, router_b, corr_bias):
            logits = x.astype(jnp.float32) @ router_w.T + router_b
            scores = jax.nn.sigmoid(logits)
            sfc = scores + corr_bias[None, :]
            grp = sfc.reshape(-1, G, E // G)
            group_scores = jax.lax.top_k(grp, 2)[0].sum(-1)
            _, gidx = jax.lax.top_k(group_scores, TOPK_GROUP)
            gmask = jax.nn.one_hot(gidx, G, dtype=sfc.dtype).sum(axis=1)
            score_mask = jnp.repeat(gmask, E // G, axis=-1)
            sfc = jnp.where(score_mask > 0, sfc, 0.0)
            _, idx = jax.lax.top_k(sfc, TOP_K)
            w = jnp.take_along_axis(scores, idx, axis=1)
            w = w / (w.sum(-1, keepdims=True) + 1e-20)
            return (idx, w * SCALE)

        def _forward(x3, router_w, router_b, corr_bias, gWg, gbg, gWu, gbu, gWd, gbd, sWg, sbg, sWu, sbu, sWd, sbd):
            orig_shape = x3.shape
            x = x3.reshape(-1, H)
            idx, w = _route(x, router_w, router_b, corr_bias)
            c = (jax.nn.one_hot(idx, E, dtype=w.dtype) * w[..., None]).sum(1)
            h = jax.nn.silu(jnp.einsum('th,ehi->tei', x, gWg) + gbg) * (jnp.einsum('th,ehi->tei', x, gWu) + gbu)
            out_e = jnp.einsum('tei,eih->teh', h, gWd) + gbd
            moe_out = jnp.einsum('te,teh->th', c, out_e)
            hs = jax.nn.silu(x @ sWg + sbg) * (x @ sWu + sbu)
            shared = hs @ sWd + sbd
            return (moe_out + shared).reshape(orig_shape)
        return _forward(hidden_states, router_w, router_b, corr_bias, gWg, gbg, gWu, gbu, gWd, gbd, sWg, sbg, sWu, sbu, sWd, sbd)
    h = _L0_tok_ref(x, L0_tok_ln_gamma, L0_tok_ln_beta, L0_tok_W, L0_tok_b)
    h = h + _L0_attn_ref(_layernorm(h, axis=-1), L0_attn_Wqkv_w, L0_attn_Wqkv_b, L0_attn_sel_w, L0_attn_sel_b, L0_attn_out_w, L0_attn_out_b, L0_attn_temperature)
    h = h + _L0_ffn_ref(_layernorm(h, axis=-1), L0_ffn_router_w, L0_ffn_router_b, L0_ffn_w1, L0_ffn_b1, L0_ffn_w2, L0_ffn_b2, L0_ffn_gamma, L0_ffn_beta)
    h = h + _L1_attn_ref(_layernorm(h, axis=-1), L1_attn_w_qkv, L1_attn_w_o)
    h = h + _L1_ffn_ref(_layernorm(h, axis=-1), L1_ffn_router_w, L1_ffn_router_b, L1_ffn_corr_bias, L1_ffn_gWg, L1_ffn_gbg, L1_ffn_gWu, L1_ffn_gbu, L1_ffn_gWd, L1_ffn_gbd, L1_ffn_sWg, L1_ffn_sbg, L1_ffn_sWu, L1_ffn_sbu, L1_ffn_sWd, L1_ffn_sbd)
    return h

_drawn_inputs = setup_inputs


def setup_inputs(seed=0):
    import zlib

    import numpy as np

    out = dict(_drawn_inputs(seed))
    spreads = {'L0_tok_ln_gamma': (1.0, 0.2),
     'L0_tok_ln_beta': (0.0, 0.1),
     'L0_tok_b': (0.0, 0.1),
     'L0_ffn_router_b': (0.0, 0.1),
     'L0_ffn_b1': (0.0, 0.1),
     'L0_ffn_b2': (0.0, 0.1),
     'L0_ffn_gamma': (1.0, 0.2),
     'L0_ffn_beta': (0.0, 0.1),
     'L1_ffn_router_b': (0.0, 0.1),
     'L1_ffn_corr_bias': (0.0, 0.1),
     'L1_ffn_gbg': (0.0, 0.314),
     'L1_ffn_gbu': (0.0, 0.335),
     'L1_ffn_gbd': (0.0, 0.1),
     'L1_ffn_sbg': (0.0, 0.46),
     'L1_ffn_sbu': (0.0, 0.403),
     'L1_ffn_sbd': (0.0, 0.268)}
    factors = {'L0_attn_Wqkv_w': 6.705,
     'L0_attn_Wqkv_b': 8.0,
     'L0_attn_sel_w': 4.854,
     'L0_attn_sel_b': 31.193,
     'L0_attn_out_w': 5.03,
     'L0_attn_out_b': 6.073}
    for name, (base, spread) in spreads.items():
        noise = np.random.default_rng([zlib.crc32(name.encode()), seed]).standard_normal(out[name].shape)
        drawn = base * np.exp(spread * noise) if base else spread * noise
        out[name] = jnp.asarray(drawn.astype(out[name].dtype))
    for name, factor in factors.items():
        out[name] = (out[name] * factor).astype(out[name].dtype)
    return out
```

```python
import numpy as np
import concourse.bass as bass
from concourse import mybir
from contextlib import ExitStack


N_IMG, C_IN, SIDE, PATCH = 64, 3, 96, 16
GRID = SIDE // PATCH
TOK = GRID * GRID
IPG = 3
R = IPG * TOK
NG = 2 * -(-N_IMG // (2 * IPG))
NP = NG // 2
D = 192
HW = D // 2
HALO = PATCH + 2
FEAT = C_IN * HALO * HALO
KP = 7 * HALO
KB = -(-FEAT // KP)
NS = 5
SHIFTS = ((0, 0), (0, -1), (0, 1), (-1, 0), (1, 0))
FULL = PATCH * PATCH * NS * C_IN
EPS = 1e-5
H0, D0 = 12, 16
HH = H0 // 2
KSEL = 6
QG = IPG * KSEL
E0, F0 = 8, 4 * D
FB0 = F0 // 128
H1, D1 = 12, 64
A1 = H1 * D1
MB1 = A1 // 128
E1, F1 = 16, 96
EX = E1 + 2
G1 = 4
GE = E1 // G1
K1 = 4
SCALE1 = 2.5
PH = 2 * R


def vit_tower(nc, x, tok_w, tok_g, tok_be, tok_b, tok_cnt,
              wqkv, bqk, bv, sel_w, sel_b, temp, wo, bo,
              rt_w, rt_b, w1, b1, w2, b2, gam, bet,
              wqkv1, wo1,
              rt1_w, rt1_b, corr, w_gate, b_gate, w_up, b_up, w_down, b_down, sb_down,
              ident_c, cmask_c, bmask_c, later_c, earlier_c, rtab_c, hmask_c, tri0_c, tri1_c, trig_c, out):
    fp32 = mybir.dt.float32
    ALU = mybir.AluOpType
    ACT = mybir.ActivationFunctionType
    AX = mybir.AxisListType.X

    with ExitStack() as ctx:
        def sb(name, shape):
            return ctx.enter_context(nc.sbuf_tensor(name, shape, fp32))

        def sem(name):
            return ctx.enter_context(nc.semaphore(name))

        def sem2(name):
            return [sem(f"{name}_{s}") for s in range(2)]

        ps = ctx.enter_context(nc.psum_tensor("ps", [128, 8, 512], fp32))
        bank = [ps[:, n, :] for n in range(8)]

        ident = sb("ident", [128, 128])
        ones = sb("ones", [128, 128])
        h = sb("h", [128, NG, D])
        mean = sb("mean", [128, NG])
        var = sb("var", [128, NG])
        dif = sb("dif", [128, NG])
        dif2 = sb("dif2", [128, NG])
        var2 = sb("var2", [128, NG])
        rstd = sb("rstd", [128, NG])
        sdev = sb("sdev", [128, NG])
        eps_t = sb("eps_t", [128, 1])
        warm = sb("warm", [1, 5])
        xn = [sb(f"xn{s}", [128, D]) for s in range(2)]
        xT = sb("xT", [128, 2, PH])
        st6 = sb("st6", [128, NG, 6])

        arena1 = sb("arena1", [128, KB * NS * D])
        tw = arena1[:, :].rearrange("p (k s d) -> p k s d", k=KB, s=NS)
        tg = sb("tg", [128, KB, NS])
        tbe = sb("tbe", [128, KB, NS])
        arena3 = sb("arena3", [128, KB * (D + 1) + 4 * KB * R])
        weff = arena3[:, 0:KB * (D + 1)].rearrange("p (k d) -> p k d", k=KB)
        cnt = sb("cnt", [128, KB, 1])
        tb_row = sb("tb_row", [1, D])
        bw_row = sb("bw_row", [1, D])
        csum = sb("csum", [128, D])
        bw = sb("bw", [128, D])
        patches = arena3[:, KB * (D + 1):].rearrange("p (n k r) -> p n k r", n=4, k=KB)
        xp = [patches[:, s, :, :] for s in range(2)]
        xsq = [patches[:, 2 + s, :, :] for s in range(2)]
        sums = sb("sums", [128, NG, 2])
        mu = sb("mu", [128, NG])
        nmu = sb("nmu", [128, NG])
        m2 = sb("m2", [128, NG])
        tmp = [sb(f"tmp{s}", [128, D]) for s in range(2)]

        cmask = sb("cmask", [128, R])
        bmask = sb("bmask", [128, R])
        later = sb("later", [128, R])
        earlier = sb("earlier", [128, R])
        rtab = sb("rtab", [128, R])
        hmask = sb("hmask", [128, R])
        hmaskq = sb("hmaskq", [128, R])
        wqkv_t = sb("wqkv_t", [128, 2, 3 * D])
        wo_t = sb("wo_t", [128, 2, D])
        bqk_t = sb("bqk_t", [128, 4])
        bv_t = sb("bv_t", [128, D])
        bo_t = sb("bo_t", [128, D])
        selw_t = sb("selw_t", [128, 2, 2])
        selb_t = sb("selb_t", [128, 2])
        temp_t = sb("temp_t", [128, 1])
        itemp = sb("itemp", [128, 1])
        dselb = sb("dselb", [128, 1])
        bz = sb("bz", [128, 1])
        dselw = sb("dselw", [128, 2, 1])
        wz = sb("wz", [128, 2, R])

        def slots(name, shape):
            return [sb(f"{name}{s}", shape) for s in range(2)]

        kT = sb("kT", [128, 2, PH])
        zr = slots("zr", [128, R])
        zc = slots("zc", [128, 1])
        junk = slots("junk", [128, 3, R])
        rka = slots("rka", [128, 1])
        rkb = slots("rkb", [128, 1])
        psel = slots("psel", [128, R])
        pselT = slots("pselT", [128, R])
        xs = slots("xs", [128, 2, QG])
        qb = slots("qb", [128, 2, R])
        v0 = slots("v0", [128, D])
        nmx = slots("nmx", [128, H1])
        den = slots("den", [128, H1])
        rden = slots("rden", [128, H1])
        p0 = slots("p0", [128, 2, R])
        pn = slots("pn", [128, 2, R])
        pt0 = slots("pt0", [128, 2, R])
        om = slots("om", [128, 2, R])
        ct0 = slots("ct0", [128, 2, QG])
        at0 = slots("at0", [128, D])
        ez = slots("ez", [128, 1])
        ez1 = slots("ez1", [128, 1])
        sig = slots("sig", [128, 1])
        y0 = slots("y0", [128, D])

        arena2 = sb("arena2", [128, 15648])
        taken = [0]

        def part(shape):
            n = int(np.prod(shape))
            v = arena2[:, taken[0]:taken[0] + n]
            taken[0] += n
            names = "abcd"[:len(shape)]
            return v.rearrange(f"p ({' '.join(names)}) -> p {' '.join(names)}",
                               **{c: m for c, m in zip(names, shape)}) if len(shape) > 1 else v

        acc = part([NG, D])
        xTall = part([2, NG * R])
        w1_t = [part([2, F0]) for _ in range(2)]
        w2_t = [part([FB0, D]) for _ in range(2)]
        hT = part([FB0, PH])
        b1_t = [sb(f"b1_t{s}", [128, FB0]) for s in range(2)]
        b2_t = sb("b2_t", [128, D])
        rtw_t = sb("rtw_t", [128, 2, E0])
        rtb_t = sb("rtb_t", [128, E0])
        gam_t = sb("gam_t", [128, D])
        bet_t = sb("bet_t", [128, D])
        tri0 = sb("tri0", [128, E0 * 2 * E0])
        lg = sb("lg", [128, NG, E0])
        cmp0 = arena1[:, 0:NG * E0 * 2 * E0].rearrange("p (g w) -> p g w", g=NG)
        rank0 = sb("rank0", [128, NG, E0])
        eq = [sb(f"eq{k}", [128, NG, E0]) for k in range(2)]
        eql = [sb(f"eql{k}", [128, NG, E0]) for k in range(2)]
        top = [sb(f"top{k}", [128, NG]) for k in range(2)]
        gap = sb("gap", [128, NG])
        egap = sb("egap", [128, NG])
        egap1 = sb("egap1", [128, NG])
        gw = [sb(f"gw{k}", [128, NG]) for k in range(2)]
        we = sb("we", [128, NG, E0])
        wes = slots("wes", [128, E0])
        weT = slots("weT", [128, R])
        y1 = slots("y1", [128, D])
        z1 = slots("z1", [128, D])
        z2 = slots("z2", [128, D])
        z3 = slots("z3", [128, D])

        taken[0] = 0
        qT = [part([MB1, PH]) for _ in range(2)]
        k1T = part([MB1, PH])
        v1 = [part([A1]) for _ in range(2)]
        sm = [part([H1, R]) for _ in range(2)]
        p1 = [part([H1, R]) for _ in range(2)]
        pt1 = sm
        cx = [part([A1]) for _ in range(2)]
        cT = [part([MB1, R]) for _ in range(2)]
        qscale = sb("qscale", [128, 2])
        w1qkv = arena3[:, 0:6 * A1].rearrange("p (k n) -> p k n", k=2)
        wo1_t = sb("wo1_t", [128, MB1, D])
        s_w4 = sem("s_w4")
        s_qs = sem("s_qs")
        s_qkp = [sem(f"s_qkp{n}") for n in range(MB1)]
        s_qk = [sem(f"s_qk{n}") for n in range(MB1)]
        s_sm = sem2("s_sm")
        s_pt1p = [[sem(f"s_pt1p{s}{b}") for b in range(3)] for s in range(2)]
        s_pt1 = [[sem(f"s_pt1_{s}{b}") for b in range(3)] for s in range(2)]
        s_cTp = sem2("s_cTp")
        s_cT = sem2("s_cT")
        wg_t = arena1[:, 0:2 * EX * F1].rearrange("p (k n) -> p k n", k=2)
        wu_t = arena1[:, 2 * EX * F1:4 * EX * F1].rearrange("p (k n) -> p k n", k=2)
        wd_t = sb("wd_t", [128, EX, D])
        bd_t = sb("bd_t", [128, D])
        bg_t = sb("bg_t", [128, EX])
        bu_t = sb("bu_t", [128, EX])
        rt1w_t = sb("rt1w_t", [128, 2, E1])
        taken[0] = 0
        rt1b_t = sb("rt1b_t", [128, E1])
        corr_t = sb("corr_t", [128, E1])
        cmp1 = part([NG, 2 * E1 * E1])
        lg1 = part([NG, E1])
        sc1 = part([NG, E1])
        sfc = part([NG, E1])
        psum1 = part([NG * G1, 6])
        gtop = part([NG, G1])
        gcmp = part([NG, G1 * 2 * G1])
        grank = part([NG, G1])
        skept = part([NG, E1])
        tri1 = part([E1 * 2 * E1])
        trig = part([G1 * 2 * G1])
        taken[0] = 0
        hid = [part([PH]) for _ in range(3)]
        sg = [part([PH]) for _ in range(2)]
        acc5 = [part([D]) for _ in range(2)]
        o5 = [part([D]) for _ in range(2)]
        oh = [part([D]) for _ in range(2)]
        c1 = sb("c1", [128, NG, E1 + 1])
        wsum = sb("wsum", [128, NG])
        wsum1 = sb("wsum1", [128, NG])
        wrec = sb("wrec", [128, NG])
        cs = slots("cs", [128, E1 + 1])
        s_wgu = sem("s_wgu")
        s_w5 = sem("s_w5")
        s_c1 = sem("s_c1")
        s_r5 = sem("s_r5")
        s_sc = sem("s_sc")
        s_gp = sem("s_gp")
        s_sg = sem("s_sg")
        s_hid = sem("s_hid")
        s_dn = sem("s_dn")
        s_ac5 = sem("s_ac5")
        s_sh = sem("s_sh")
        s_o5 = sem("s_o5")
        s_oh = sem("s_oh")
        s_w3 = sem("s_w3")
        s_we = [sem(f"s_we{n}") for n in range(2)]
        s_zacc = sem("s_zacc")
        s_xTa = sem("s_xTa")
        s_lgp = sem("s_lgp")
        s_lg = sem("s_lg")
        s_rt = sem("s_rt")
        s_eg = sem("s_eg")
        s_hp = [sem(f"s_hp{n}") for n in range(3)]
        s_hT = [sem(f"s_hT{n}") for n in range(3)]
        s_yp = sem2("s_yp")
        s_acc = sem2("s_acc")
        s_wes = sem("s_wes")
        s_weTp = sem("s_weTp")
        s_weT = sem("s_weT")
        s_b2p = sem("s_b2p")
        s_y1 = sem("s_y1")
        s_y2 = sem("s_y2")
        s_z1 = sem("s_z1")
        s_z2 = sem("s_z2")
        s_z3 = sem("s_z3")
        s_w0 = sem("s_w0")
        s_sw = sem("s_sw")
        s_xn = sem2("s_xn")
        s_xTp = sem2("s_xTp")
        s_xT = sem2("s_xT")
        s_zp = sem("s_zp")
        s_zr = sem("s_zr")
        s_zc = sem("s_zc")
        s_rk = sem("s_rk")
        s_psel = sem("s_psel")
        s_ptp0 = sem("s_ptp0")
        s_pselT = sem("s_pselT")
        s_xsp = sem("s_xsp")
        s_xs = sem("s_xs")
        s_qp = sem("s_qp")
        s_qb = sem2("s_qb")
        s_kp = sem("s_kp")
        s_kT = sem("s_kT")
        s_vp = sem2("s_vp")
        s_v = sem2("s_v")
        s_sp = sem2("s_sp")
        s_mx = sem("s_mx")
        s_exp = sem2("s_exp")
        s_rd = sem("s_rd")
        s_pn = sem("s_pn")
        s_ptp = sem2("s_ptp")
        s_pt = sem2("s_pt")
        s_op = sem2("s_op")
        s_om = sem("s_om")
        s_ct = sem2("s_ct")
        s_ap = sem2("s_ap")
        s_at = sem("s_at")
        s_up = sem("s_up")
        s_ez = sem("s_ez")
        s_ez1 = sem("s_ez1")
        s_sig = sem("s_sig")
        s_y0 = sem("s_y0")

        s_const = sem("s_const")
        s_tokw = sem("s_tokw")
        s_ones = sem("s_ones")
        s_eps = sem("s_eps")
        s_weff = sem("s_weff")
        s_cnt = sem("s_cnt")
        s_bwrow_p = sem("s_bwrow_p")
        s_bwrow = sem("s_bwrow")
        s_bw_p = sem("s_bw_p")
        s_bw = sem("s_bw")
        s_x = sem2("s_x")
        s_xsq = sem2("s_xsq")
        s_emb = sem2("s_emb")
        s_raw = sem2("s_raw")
        s_mu = sem("s_mu")
        s_e1 = sem("s_e1")
        s_h = sem2("s_h")
        s_bn = sem2("s_bn")
        s_st = sem("s_st")
        s_sd = sem("s_sd")
        s_rstd = sem("s_rstd")
        s_out = sem("s_out")
        s_outs = sem2("s_outs")

        R5_END = 19
        RT_GAP, RT_END = 11, 17

        block = ctx.enter_context(nc.Block())

        def grp(t, g, n=D):
            return t[0:R, :, :].rearrange("p g d -> p (g d)")[:, bass.ds(g * n, n)]

        def col(t, g):
            return t[0:R, bass.ds(g, 1)]

        def head_at(n):
            b, j = divmod(n, 3)
            return 2 * (b // 2 * 3 + j) + b % 2

        def row_stats(dve, time):
            st = 7 * (time - 1)
            a = st6[0:R, :, :]
            for s in range(2):
                dve.wait_ge(s_bn[s], NP * time)
            dve.tensor_tensor(mean[0:R, :], a[:, :, 1], a[:, :, 4], ALU.add).then_inc(s_st, 1)
            dve.tensor_tensor(dif[0:R, :], a[:, :, 1], a[:, :, 4], ALU.subtract).then_inc(s_st, 1)
            dve.tensor_tensor(var2[0:R, :], a[:, :, 2], a[:, :, 5], ALU.add).then_inc(s_st, 1)
            dve.wait_ge(s_st, st + 2)
            dve.scalar_tensor_tensor(dif2[0:R, :], dif[0:R, :], 0.25, dif[0:R, :], ALU.mult, ALU.mult).then_inc(s_st, 1)
            dve.tensor_scalar(mean[0:R, :], mean[0:R, :], 0.5, None, ALU.mult).then_inc(s_st, 1)
            dve.wait_ge(s_st, st + 4)
            dve.scalar_tensor_tensor(var[0:R, :], var2[0:R, :], 1.0 / D, dif2[0:R, :], ALU.mult, ALU.add).then_inc(s_st, 1)
            dve.wait_ge(s_sd, time + 1)
            dve.reciprocal(rstd[0:R, :], sdev[0:R, :]).then_inc(s_st, 1)
            dve.wait_ge(s_st, st + 7)

        def use_tables(act, func, n):
            act.activation(warm[0:1, n:n + 1], eps_t[0:1, :], func)

        def row_sdev(act, time):
            act.wait_ge(s_st, 7 * (time - 1) + 6)
            act.activation(sdev[0:R, :], var[0:R, :], ACT.Sqrt, bias=eps_t[0:R, :]).then_inc(s_sd, 1)

        def load_expert(sp, e, n):
            sp.dma_start(w1_t[n][0:HW, :, :].rearrange("p k f -> p (k f)"),
                         w1[bass.ds(e, 1)].rearrange("a p k f -> p (a k f)")).then_inc(s_we[n], 16)
            sp.dma_start(w2_t[n].rearrange("p k f -> p (k f)"),
                         w2[bass.ds(e, 1)].rearrange("a p k f -> p (a k f)")).then_inc(s_we[n], 16)
            sp.dma_start(b1_t[n][:, :], b1[bass.ds(e, 1)].rearrange("a p k -> p (a k)")).then_inc(s_we[n], 16)

        @block.sync
        def _(sp):
            for t, d in ((ident[:, :], ident_c),):
                sp.dma_start(t, d).then_inc(s_const, 16)
            for t, d in ((arena1[0:KP, :], tok_w), (tg[0:KP, :, :], tok_g), (tbe[0:KP, :, :], tok_be),
                         (tb_row[:, :], tok_b), (cnt[0:KP, :, :], tok_cnt)):
                sp.dma_start(t, d).then_inc(s_tokw, 16)
            with sp.Fori(0, NP) as i:
                for s in range(2):
                    sp.wait_ge(s_emb[s], i)
                    sp.wait_ge(s_xsq[s], i)
                    sp.dma_start(xp[s][0:KP, :, :].rearrange("p k r -> p (k r)"),
                                 x[bass.ds(2 * i + s, 1), :, :].rearrange("a p f -> p (a f)")).then_inc(s_x[s], 16)
            for t, d in ((wqkv_t[0:HW, :, :], wqkv), (wo_t[0:HW, :, :], wo), (bqk_t[0:HW, :], bqk),
                         (bv_t[0:R, :], bv), (bo_t[0:R, :], bo), (selw_t[0:HW, :, :], sel_w),
                         (selb_t[0:R, :], sel_b), (temp_t[0:R, :], temp), (cmask[0:R, :], cmask_c),
                         (later[0:R, :], later_c), (earlier[0:R, :], earlier_c), (rtab[0:R, :], rtab_c),
                         (hmask[0:HW, :], hmask_c)):
                sp.dma_start(t, d).then_inc(s_w0, 16)
            for t, d in ((rtw_t[0:HW, :, :], rt_w), (rtb_t[0:R, :], rt_b), (b2_t[0:E0, :], b2), (gam_t[0:R, :], gam),
                         (bet_t[0:R, :], bet), (tri0[0:R, :], tri0_c)):
                sp.dma_start(t, d).then_inc(s_w3, 16)
            for n in range(2):
                load_expert(sp, n, n)
            with sp.Fori(1, E0 // 2) as ie:
                for n in range(2):
                    sp.wait_ge(s_hT[2], (2 * ie + n - 1) * NP)
                    sp.wait_ge(s_yp[1], (2 * ie + n - 1) * NP)
                    load_expert(sp, 2 * ie + n, n)
            for s in range(2):
                sp.wait_ge(s_emb[s], NP)
            for t, d in ((w1qkv[0:HW, :, :], wqkv1), (wo1_t[:, :, :], wo1), (bmask[0:R, :], bmask_c)):
                sp.dma_start(t, d).then_inc(s_w4, 16)
            sp.wait_ge(s_rt, RT_END)
            sp.dma_start(wg_t[0:HW, :, :], w_gate).then_inc(s_wgu, 16)
            sp.dma_start(wu_t[0:HW, :, :], w_up).then_inc(s_wgu, 16)
            for t, d in ((wd_t[0:F1, :, :], w_down), (bd_t[0:E1, :], b_down), (bd_t[E1:E1 + 1, :], sb_down),
                         (bg_t[0:F1, :], b_gate), (bu_t[0:F1, :], b_up), (rt1w_t[0:HW, :, :], rt1_w),
                         (rt1b_t[0:R, :], rt1_b), (corr_t[0:R, :], corr)):
                sp.dma_start(t, d).then_inc(s_w5, 16)
            for s in range(2):
                sp.wait_ge(s_h[s], 4 * NP)
            sp.dma_start(tri1[0:R, :], tri1_c).then_inc(s_w5, 16)
            sp.dma_start(trig[0:R, :], trig_c).then_inc(s_w5, 16)
            with sp.Fori(0, NP) as i:
                for s in range(2):
                    sp.wait_ge(s_oh, 2 * i + s + 1)
                    sp.dma_start(out[bass.ds(2 * i + s, 1)].rearrange("a r d -> (a r) d"), oh[s][0:R, :]
                                 ).then_inc(s_outs[s], 16)
            for s in range(2):
                sp.wait_ge(s_outs[s], 16 * NP)
        @block.gpsimd
        def _(pool):
            pool.memset(ones[:, :], 1.0).then_inc(s_ones, 1)
            pool.memset(eps_t[:, :], EPS).then_inc(s_eps, 1)
            pool.wait_ge(s_tokw, 5 * 16)
            pool.tensor_copy(weff[0:KP, :, D:D + 1], cnt[0:KP, :, :]).then_inc(s_cnt, 1)
            pool.memset(acc[0:R, :, :], 0.0).then_inc(s_zacc, 1)
            with pool.Fori(0, NP) as i:
                for s in range(2):
                    pool.wait_ge(s_ones, 1)
                    pool.wait_ge(s_xT[s], i + 1 + NP)
                    pool.tensor_copy(xTall[0:HW, :, bass.ds((2 * i + s) * R, R)], xT[0:HW, :, s * R:(s + 1) * R]
                                     ).then_inc(s_xTa, 1)
            with pool.Fori(0, NP) as i:
                for s in range(2):
                    pool.wait_ge(s_ones, 1)
                    pool.wait_ge(s_rt, RT_END)
                    pool.wait_ge(s_weTp, 2 * i)
                    pool.tensor_copy(wes[s][0:R, :], grp(we, 2 * i + s, E0)).then_inc(s_wes, 1)
            pool.memset(c1[0:R, :, :], 1.0).then_inc(s_c1, 1)
            with pool.Fori(0, NP) as i:
                for s in range(2):
                    pool.wait_ge(s_ones, 1)
                    pool.wait_ge(s_r5, R5_END)
                    pool.wait_ge(s_ac5, E1 * 2 * i)
                    pool.wait_ge(s_weTp, 2 * i + 2 * NP)
                    pool.tensor_copy(cs[s][0:R, :], grp(c1, 2 * i + s, E1 + 1)).then_inc(s_wes, 1)

        @block.scalar
        def _(act):
            act.wait_ge(s_eps, 1)
            use_tables(act, ACT.Square, 0)
            with act.Fori(0, NP) as i:
                for s in range(2):
                    act.wait_ge(s_x[s], 16 * i + 16)
                    act.wait_ge(s_emb[s], i)
                    act.activation(xsq[s][0:KP, :, :], xp[s][0:KP, :, :], ACT.Square).then_inc(s_xsq[s], 1)
            act.wait_ge(s_eps, 1)
            act.wait_ge(s_mu, 3)
            act.activation(sdev[0:R, :], var[0:R, :], ACT.Sqrt, bias=eps_t[0:R, :]).then_inc(s_sd, 1)
            row_sdev(act, 1)

            use_tables(act, ACT.Exp, 1)
            act.wait_ge(s_w0, 13 * 16)
            with act.Fori(0, NP) as i:
                for s in range(2):
                    act.wait_ge(s_xTp[s], i + 1)
                    act.wait_ge(s_vp[s], i)
                    act.copy(xT[0:HW, :, s * R:(s + 1) * R],
                             bank[4 * s][0:HW, 0:PH].rearrange("p (k r) -> p k r", k=2)).then_inc(s_xT[s], 1)
                act.wait_ge(s_kp, i + 1)
                for s in range(2):
                    act.wait_ge(s_sp[s], i)
                for hh in range(2):
                    act.activation(kT[0:HW, hh, :], bank[0][0:HW, hh * PH:(hh + 1) * PH], ACT.Identity,
                                   bias=bqk_t[0:HW, 2 + hh:3 + hh]).then_inc(s_kT, 1)
                for s in range(2):
                    act.wait_ge(s_zc, 2 * i + s + 1)
                    act.wait_ge(s_ez1, 2 * i)
                    act.activation(ez[s][0:R, :], zc[s][0:R, :], ACT.Exp, scale=-1.0).then_inc(s_ez, 1)
                for s in range(2):
                    act.wait_ge(s_ptp0, 2 * i + s + 1)
                    act.wait_ge(s_up, 2 * i)
                    act.copy(pselT[s][0:QG, :], bank[4 * s + 3][0:QG, 0:R]).then_inc(s_pselT, 1)
                for s in range(2):
                    act.wait_ge(s_mx, 2 * i + s + 1)
                    act.wait_ge(s_pn, 2 * i)
                    for hh in range(2):
                        ex = act.activation(p0[s][0:R, hh, :], bank[4 * s + 2][0:R, D + hh * R:D + (hh + 1) * R], ACT.Exp,
                                            bias=nmx[s][0:R, hh:hh + 1], accum_out=den[s][0:R, hh:hh + 1])
                    ex.then_inc(s_exp[s], 1)
                for s in range(2):
                    act.wait_ge(s_ptp[s], i + 1)
                    act.wait_ge(s_op[s], i)
                    act.copy(pt0[s][0:R, :, :], bank[4 * s + 3][0:R, 0:PH].rearrange("p (k r) -> p k r", k=2)
                             ).then_inc(s_pt[s], 1)
            row_sdev(act, 2)

            with act.Fori(0, NP) as i:
                for s in range(2):
                    act.wait_ge(s_xTp[s], i + 1 + NP)
                    act.wait_ge(s_xTa, 2 * i)
                    act.wait_ge(s_lgp, 2 * i)
                    act.copy(xT[0:HW, :, s * R:(s + 1) * R],
                             bank[4 * s][0:HW, 0:PH].rearrange("p (k r) -> p k r", k=2)).then_inc(s_xT[s], 1)
            act.wait_ge(s_rt, RT_GAP)
            act.activation(egap[0:R, :], gap[0:R, :], ACT.Exp).then_inc(s_eg, 1)
            use_tables(act, ACT.Gelu, 2)
            with act.Fori(0, E0 // 2) as ie:
                for n in range(2):
                    act.wait_ge(s_we[n], 48 * ie + 48)
                    with act.Fori(0, NP) as i:
                        for b in range(3):
                            act.wait_ge(s_yp[1], (2 * ie + n) * NP + i)
                            act.wait_ge(s_hp[b], (2 * ie + n) * NP + i + 1)
                            for m in (2 * b, 2 * b + 1):
                                g = act.activation(hT[:, m, :], bank[b][:, (m % 2) * PH:(m % 2 + 1) * PH], ACT.Gelu,
                                                   bias=b1_t[n][:, m:m + 1])
                            g.then_inc(s_hT[b], 1)
            with act.Fori(0, NP) as i:
                for s in range(2):
                    act.wait_ge(s_weTp, 2 * i + s + 1)
                    act.wait_ge(s_b2p, 2 * i)
                    act.copy(weT[s][0:E0, :], bank[4 * s][0:E0, 0:R]).then_inc(s_weT, 1)
            row_sdev(act, 3)
            row_sdev(act, 4)

            act.wait_ge(s_w4, 3 * 16)
            act.wait_ge(s_qs, 4)
            use_tables(act, ACT.Exp, 3)

            def front1(i):
                for s in range(2):
                    act.wait_ge(s_xTp[1], i + 1 + 2 * NP)
                    act.copy(xT[0:HW, :, s * R:(s + 1) * R],
                             bank[4][0:HW, s * PH:(s + 1) * PH].rearrange("p (k r) -> p k r", k=2)).then_inc(s_xT[s], 1)
                for n in range(3):
                    act.wait_ge(s_qkp[n], i + 1)
                    for c in range(2):
                        q = act.activation(qT[c][:, 2 * n:2 * n + 2, :],
                                           bank[5 + n][:, 0:2 * PH].rearrange("p (m r) -> p m r", m=2),
                                           ACT.Copy, scale=qscale[:, c:c + 1])
                    q.then_inc(s_qk[n], 1)

            def attend1(i, more):
                for s in range(2):
                    act.wait_ge(s_vp[s], i + 1 + NP)
                    act.copy(v1[s][0:R, :].rearrange("p (b f) -> p b f", b=2), ps[0:R, 5:7, 0:A1 // 2]).then_inc(s_v[s], 1)
                for s in range(2):
                    if s == 1 and more:
                        front1(i + 1)
                    act.wait_ge(s_mx, 2 * i + s + 1 + 2 * NP)
                    for n in range(H1):
                        ex = act.activation(p1[s][0:R, head_at(n), :], sm[s][0:R, n, :], ACT.Exp, bias=nmx[s][0:R, n:n + 1],
                                            accum_out=den[s][0:R, head_at(n):head_at(n) + 1])
                    ex.then_inc(s_exp[s], 1)
                for s in range(2):
                    act.wait_ge(s_cTp[s], i + 1)
                    act.copy(cT[s].rearrange("p (b m) r -> p b (m r)", b=2), ps[:, 2:4, 0:3 * R]).then_inc(s_cT[s], 1)

            front1(0)
            with act.Fori(0, NP - 1) as i:
                attend1(i, True)
            attend1(NP - 1, False)
            row_sdev(act, 5)

            with act.Fori(0, NP) as i:
                for s in range(2):
                    act.wait_ge(s_xTp[1], i + 1 + 3 * NP)
                    act.wait_ge(s_lgp, 2 * i + 2 * NP)
                    act.copy(xT[0:HW, :, s * R:(s + 1) * R],
                             bank[4][0:HW, s * PH:(s + 1) * PH].rearrange("p (k r) -> p k r", k=2)).then_inc(s_xT[s], 1)
            for s in range(2):
                act.wait_ge(s_lg, 4 * NP)
            act.activation(sc1[0:R, :, :], lg1[0:R, :, :], ACT.Sigmoid).then_inc(s_sc, 1)
            use_tables(act, ACT.Silu, 4)
            act.wait_ge(s_w5, 10 * 16)
            with act.Fori(0, NP) as i:
                for s in range(2):
                    act.wait_ge(s_xTp[1], i + 1 + 4 * NP)
                    act.wait_ge(s_gp, EX * i)
                    act.copy(xT[0:HW, :, s * R:(s + 1) * R],
                             bank[7][0:HW, s * PH:(s + 1) * PH].rearrange("p (k r) -> p k r", k=2)).then_inc(s_xT[s], 1)
                for s in range(2):
                    act.wait_ge(s_weTp, 2 * i + 2 + 2 * NP)
                    act.wait_ge(s_sh, i)
                    act.copy(weT[s][0:E1 + 1, :], bank[7][0:E1 + 1, s * R:(s + 1) * R]).then_inc(s_weT, 1)
                for e in range(EX):
                    act.wait_ge(s_gp, EX * i + e + 1)
                    act.wait_ge(s_hid, EX * i + max(e - 1, 0))
                    act.activation(sg[e % 2][0:F1, :], bank[e % 2][0:F1, 0:PH], ACT.Silu, bias=bg_t[0:F1, e:e + 1]
                                   ).then_inc(s_sg, 1)

        @block.vector
        def _(dve):
            dve.wait_ge(s_tokw, 5 * 16)
            for k in range(KB):
                dve.tensor_scalar(weff[0:KP, k, 0:D], tw[0:KP, k, 0, :], tg[0:KP, k, 0:1], None,
                                  ALU.mult).then_inc(s_weff, 1)
            for j in range(1, NS):
                for k in range(KB):
                    dve.wait_ge(s_weff, KB * (j - 1) + k + 1)
                    dve.scalar_tensor_tensor(weff[0:KP, k, 0:D], tw[0:KP, k, j, :], tg[0:KP, k, j:j + 1],
                                             weff[0:KP, k, 0:D], ALU.mult, ALU.add).then_inc(s_weff, 1)
            dve.wait_ge(s_bwrow_p, 1)
            dve.tensor_copy(bw_row[:, :], bank[0][0:1, 0:D]).then_inc(s_bwrow, 1)
            dve.wait_ge(s_bw_p, 1)
            dve.tensor_copy(csum[0:R, :], bank[1][0:R, 0:D]).then_inc(s_bw, 1)
            dve.tensor_copy(bw[0:R, :], bank[1][0:R, D:2 * D]).then_inc(s_bw, 1)
            with dve.Fori(0, NP) as i:
                for s in range(2):
                    dve.wait_ge(s_emb[s], i + 1)
                    dve.tensor_copy(grp(h, 2 * i + s), bank[2 + s][0:R, 0:D])
                    dve.tensor_copy(grp(sums, 2 * i + s, 2), bank[2 + s][0:R, D:D + 2]).then_inc(s_raw[s], 1)
            for s in range(2):
                dve.wait_ge(s_raw[s], NP)
            dve.tensor_scalar(mu[0:R, :], sums[0:R, :, 0], 1.0 / FULL, None, ALU.mult).then_inc(s_mu, 1)
            dve.wait_ge(s_mu, 1)
            dve.scalar_tensor_tensor(m2[0:R, :], mu[0:R, :], -1.0, mu[0:R, :], ALU.mult, ALU.mult).then_inc(s_mu, 1)
            dve.tensor_scalar(nmu[0:R, :], mu[0:R, :], -1.0, None, ALU.mult)
            dve.wait_ge(s_mu, 2)
            dve.scalar_tensor_tensor(var[0:R, :], sums[0:R, :, 1], 1.0 / FULL, m2[0:R, :], ALU.mult,
                                     ALU.add).then_inc(s_mu, 1)
            dve.wait_ge(s_sd, 1)
            dve.reciprocal(rstd[0:R, :], sdev[0:R, :]).then_inc(s_rstd, 1)
            dve.wait_ge(s_rstd, 1)
            dve.wait_ge(s_bw, 2)
            with dve.Fori(0, NP) as i:
                for s in range(2):
                    dve.scalar_tensor_tensor(tmp[s][0:R, :], csum[0:R, :], col(nmu, 2 * i + s), grp(h, 2 * i + s),
                                             ALU.mult, ALU.add).then_inc(s_e1, 1)
                for s in range(2):
                    dve.wait_ge(s_e1, 2 * i + s + 1)
                    dve.scalar_tensor_tensor(grp(h, 2 * i + s), tmp[s][0:R, :], col(rstd, 2 * i + s), bw[0:R, :],
                                             ALU.mult, ALU.add).then_inc(s_h[s], 1)
                for s in range(2):
                    dve.wait_ge(s_bw, 2)
                    dve.wait_ge(s_h[s], i + 1)
                    dve.bn_stats(grp(st6, 2 * i + s, 6), grp(h, 2 * i + s)).then_inc(s_bn[s], 1)
            row_stats(dve, 1)

            dve.wait_ge(s_w0, 13 * 16)
            dve.reciprocal(itemp[0:R, :], temp_t[0:R, :]).then_inc(s_sw, 1)
            dve.tensor_tensor(dselb[0:R, :], selb_t[0:R, 1:2], selb_t[0:R, 0:1], ALU.subtract).then_inc(s_sw, 1)
            dve.tensor_tensor(dselw[0:HW, :, :], selw_t[0:HW, :, 1:2], selw_t[0:HW, :, 0:1], ALU.subtract).then_inc(s_sw, 1)
            dve.tensor_scalar(hmaskq[0:HW, :], hmask[0:HW, :], float(D0) ** -0.5, None, ALU.mult)
            dve.wait_ge(s_sw, 3)
            dve.tensor_scalar(bz[0:R, :], dselb[0:R, :], itemp[0:R, :], None, ALU.mult).then_inc(s_sw, 1)
            dve.tensor_scalar(wz[0:HW, :, :], dselw[0:HW, :, :].broadcast_to([HW, 2, R]), itemp[0:HW, :], None,
                              ALU.mult).then_inc(s_sw, 1)
            dve.wait_ge(s_sw, 5)
            with dve.Fori(0, NP) as i:
                for s in range(2):
                    dve.wait_ge(s_xsp, 2 * i)
                    dve.tensor_scalar(xn[s][0:R, :], grp(h, 2 * i + s), col(mean, 2 * i + s), col(rstd, 2 * i + s),
                                      ALU.subtract, ALU.mult).then_inc(s_xn[s], 1)
                for s in range(2):
                    dve.wait_ge(s_zp, 2 * i + s + 1)
                    dve.tensor_scalar(zr[s][0:R, :], bank[4 * s + 1][0:R, 0:R], bz[0:R, :], None,
                                      ALU.add).then_inc(s_zr, 1)
                for s in range(2):
                    dve.wait_ge(s_zr, 2 * i + s + 1)
                    dve.wait_ge(s_ez, 2 * i)
                    dve.scalar_tensor_tensor(junk[s][0:R, 0, :], zr[s][0:R, :], 1.0, ident[0:R, 0:R], ALU.mult, ALU.mult,
                                             accum_out=zc[s][0:R, :]).then_inc(s_zc, 1)
                for s in range(2):
                    dve.wait_ge(s_zc, 2 * i + s + 1)
                    dve.scalar_tensor_tensor(junk[s][0:R, 1, :], zr[s][0:R, :], zc[s][0:R, :], later[0:R, :], ALU.is_gt,
                                             ALU.mult, accum_out=rka[s][0:R, :]).then_inc(s_rk, 1)
                    dve.scalar_tensor_tensor(junk[s][0:R, 2, :], zr[s][0:R, :], zc[s][0:R, :], earlier[0:R, :], ALU.is_ge,
                                             ALU.mult, accum_out=rkb[s][0:R, :]).then_inc(s_rk, 1)
                for s in range(2):
                    dve.wait_ge(s_rk, 4 * i + 2 * s + 2)
                    dve.wait_ge(s_sp[s], i)
                    dve.tensor_scalar(psel[s][0:R, :], rtab[0:R, :], rka[s][0:R, :], rkb[s][0:R, :], ALU.subtract,
                                      ALU.is_equal).then_inc(s_psel, 1)
                for s in range(2):
                    dve.wait_ge(s_vp[s], i + 1)
                    dve.tensor_tensor(v0[s][0:R, :], bank[4 * s + 2][0:R, 0:D], bv_t[0:R, :], ALU.add).then_inc(s_v[s], 1)
                for s in range(2):
                    dve.wait_ge(s_xsp, 2 * i + s + 1)
                    dve.tensor_copy(xs[s][0:HW, :, :], bank[4 * s + 1][0:HW, R:R + 2 * QG].rearrange("p (k q) -> p k q", k=2)
                                    ).then_inc(s_xs, 1)
                for s in range(2):
                    dve.wait_ge(s_qp, 2 * i + s + 1)
                    for hh in range(2):
                        q = bank[4 * s + 1][0:HW, 256 + hh * QG:256 + (hh + 1) * QG]
                        dve.scalar_tensor_tensor(qb[s][0:HW, hh, :].rearrange("p (j q) -> p j q", j=HH),
                                                 q.unsqueeze(1).broadcast_to([HW, HH, QG]), bqk_t[0:HW, hh:hh + 1],
                                                 hmaskq[0:HW, :].rearrange("p (j q) -> p j q", j=HH),
                                                 ALU.add, ALU.mult).then_inc(s_qb[s], 1)
                for s in range(2):
                    dve.wait_ge(s_sp[s], i + 1)
                    dve.tensor_reduce(nmx[s][0:R, 0:2], bank[4 * s + 2][0:R, D:D + PH].rearrange("p (k r) -> p k r", k=2),
                                      AX, ALU.max, negate=True).then_inc(s_mx, 1)
                for s in range(2):
                    dve.wait_ge(s_ez, 2 * i + s + 1)
                    dve.tensor_scalar(ez1[s][0:R, :], ez[s][0:R, :], 1.0, None, ALU.add).then_inc(s_ez1, 1)
                for s in range(2):
                    dve.wait_ge(s_ez1, 2 * i + s + 1)
                    dve.reciprocal(sig[s][0:R, :], ez1[s][0:R, :]).then_inc(s_sig, 1)
                for s in range(2):
                    dve.wait_ge(s_exp[s], i + 1)
                    dve.reciprocal(rden[s][0:R, 0:2], den[s][0:R, 0:2]).then_inc(s_rd, 1)
                for s in range(2):
                    dve.wait_ge(s_rd, 2 * i + s + 1)
                    dve.wait_ge(s_ptp[s], i)
                    dve.tensor_tensor(pn[s][0:R, :, :], p0[s][0:R, :, :],
                                      rden[s][0:R, 0:2].unsqueeze(2).broadcast_to([R, 2, R]), ALU.mult).then_inc(s_pn, 1)
                for s in range(2):
                    dve.wait_ge(s_op[s], i + 1)
                    dve.tensor_tensor(om[s][0:HW, :, :], bank[4 * s + 3][0:HW, 0:PH].rearrange("p (k r) -> p k r", k=2),
                                      hmask[0:HW, :].unsqueeze(1).broadcast_to([HW, 2, R]), ALU.mult).then_inc(s_om, 1)
                for s in range(2):
                    dve.wait_ge(s_om, 2 * i + s + 1)
                    dve.tensor_reduce(ct0[s][0:HW, :, :], om[s][0:HW, :, :].rearrange("p k (j q) -> p k q j", j=HH), AX,
                                      ALU.add).then_inc(s_ct[s], 1)
                for s in range(2):
                    dve.wait_ge(s_ap[s], i + 1)
                    dve.tensor_tensor(at0[s][0:QG, :], bank[4 * s + 3][0:QG, 0:D], bo_t[0:QG, :], ALU.add).then_inc(s_at, 1)
                for s in range(2):
                    dve.wait_ge(s_sig, 2 * i + s + 1)
                    dve.wait_ge(s_up, 2 * i + s + 1)
                    dve.scalar_tensor_tensor(y0[s][0:R, :], bank[4 * s + 3][0:R, D:2 * D], sig[s][0:R, :], xn[s][0:R, :],
                                             ALU.mult, ALU.add).then_inc(s_y0, 1)
                for s in range(2):
                    dve.wait_ge(s_y0, 2 * i + s + 1)
                    dve.tensor_tensor(grp(h, 2 * i + s), grp(h, 2 * i + s), y0[s][0:R, :], ALU.add).then_inc(s_h[s], 1)
                for s in range(2):
                    dve.wait_ge(s_bw, 2)
                    dve.wait_ge(s_h[s], i + 1 + NP)
                    dve.bn_stats(grp(st6, 2 * i + s, 6), grp(h, 2 * i + s)).then_inc(s_bn[s], 1)
            row_stats(dve, 2)

            dve.wait_ge(s_w3, 6 * 16)
            with dve.Fori(0, NP) as i:
                for s in range(2):
                    dve.wait_ge(s_xTp[s], i + NP)
                    dve.tensor_scalar(xn[s][0:R, :], grp(h, 2 * i + s), col(mean, 2 * i + s), col(rstd, 2 * i + s),
                                      ALU.subtract, ALU.mult).then_inc(s_xn[s], 1)
                for s in range(2):
                    dve.wait_ge(s_lgp, 2 * i + s + 1)
                    dve.tensor_tensor(grp(lg, 2 * i + s, E0), bank[4 * s + 1][0:R, 0:E0], rtb_t[0:R, :],
                                      ALU.add).then_inc(s_lg, 1)
            for s in range(2):
                dve.wait_ge(s_lg, 2 * NP)
            c4 = cmp0[0:R, :, :].rearrange("p g (e w j) -> p g e w j", e=E0, w=2)
            one = lg[0:R, :, :].unsqueeze(3).broadcast_to([R, NG, E0, E0])
            other = lg[0:R, :, :].unsqueeze(2).broadcast_to([R, NG, E0, E0])
            dve.tensor_tensor(c4[:, :, :, 0, :], other, one, ALU.is_gt).then_inc(s_rt, 1)
            dve.tensor_tensor(c4[:, :, :, 1, :], other, one, ALU.is_ge).then_inc(s_rt, 1)
            dve.wait_ge(s_rt, 2)
            dve.tensor_tensor(cmp0[0:R, :, :], cmp0[0:R, :, :],
                              tri0[0:R, :].unsqueeze(1).broadcast_to([R, NG, E0 * 2 * E0]), ALU.mult).then_inc(s_rt, 1)
            dve.wait_ge(s_rt, 3)
            dve.tensor_reduce(rank0[0:R, :, :], cmp0[0:R, :, :].rearrange("p g (e w) -> p g e w", e=E0), AX,
                              ALU.add).then_inc(s_rt, 1)
            dve.wait_ge(s_rt, 4)
            for k in range(2):
                dve.tensor_scalar(eq[k][0:R, :, :], rank0[0:R, :, :], float(k), None, ALU.is_equal).then_inc(s_rt, 1)
            dve.wait_ge(s_rt, 6)
            for k in range(2):
                dve.tensor_tensor(eql[k][0:R, :, :], eq[k][0:R, :, :], lg[0:R, :, :], ALU.mult).then_inc(s_rt, 1)
            dve.wait_ge(s_rt, 8)
            for k in range(2):
                dve.tensor_reduce(top[k][0:R, :], eql[k][0:R, :, :], AX, ALU.add).then_inc(s_rt, 1)
            dve.wait_ge(s_rt, 10)
            dve.tensor_tensor(gap[0:R, :], top[1][0:R, :], top[0][0:R, :], ALU.subtract).then_inc(s_rt, 1)
            dve.wait_ge(s_eg, 1)
            dve.tensor_scalar(egap1[0:R, :], egap[0:R, :], 1.0, None, ALU.add).then_inc(s_rt, 1)
            dve.wait_ge(s_rt, 12)
            dve.reciprocal(gw[0][0:R, :], egap1[0:R, :]).then_inc(s_rt, 1)
            dve.wait_ge(s_rt, 13)
            dve.tensor_tensor(gw[1][0:R, :], egap[0:R, :], gw[0][0:R, :], ALU.mult).then_inc(s_rt, 1)
            dve.wait_ge(s_rt, 14)
            for k in range(2):
                dve.tensor_tensor(eql[k][0:R, :, :], eq[k][0:R, :, :],
                                  gw[k][0:R, :].unsqueeze(2).broadcast_to([R, NG, E0]), ALU.mult).then_inc(s_rt, 1)
            dve.wait_ge(s_rt, 16)
            dve.tensor_tensor(we[0:R, :, :], eql[0][0:R, :, :], eql[1][0:R, :, :], ALU.add).then_inc(s_rt, 1)
            dve.wait_ge(s_rt, RT_END)
            dve.wait_ge(s_zacc, 1)
            with dve.Fori(0, E0 // 2) as ie:
                for n in range(2):
                    with dve.Fori(0, NP) as i:
                        for s in range(2):
                            dve.wait_ge(s_acc[s], (2 * ie + n) * NP + i)
                            dve.wait_ge(s_yp[s], (2 * ie + n) * NP + i + 1)
                            dve.scalar_tensor_tensor(
                                grp(acc, 2 * i + s), bank[3 + s][0:R, 0:D],
                                we[0:R, :, :].rearrange("p g e -> p (g e)")[:, bass.ds((2 * i + s) * E0 + 2 * ie + n, 1)],
                                grp(acc, 2 * i + s), ALU.mult, ALU.add).then_inc(s_acc[s], 1)
            with dve.Fori(0, NP) as i:
                for s in range(2):
                    dve.wait_ge(s_y1, 2 * i)
                    dve.tensor_scalar(xn[s][0:R, :], grp(h, 2 * i + s), col(mean, 2 * i + s), col(rstd, 2 * i + s),
                                      ALU.subtract, ALU.mult).then_inc(s_xn[s], 1)
                for s in range(2):
                    dve.wait_ge(s_xn[s], i + 1 + 2 * NP)
                    dve.wait_ge(s_b2p, 2 * i + s + 1)
                    dve.tensor_tensor(y1[s][0:R, :], bank[4 * s + 1][0:R, 0:D], xn[s][0:R, :], ALU.add).then_inc(s_y1, 1)
                for s in range(2):
                    dve.wait_ge(s_acc[s], E0 * NP)
                    dve.wait_ge(s_y1, 2 * i + s + 1)
                    dve.tensor_tensor(grp(acc, 2 * i + s), grp(acc, 2 * i + s), y1[s][0:R, :], ALU.add).then_inc(s_y2, 1)
                for s in range(2):
                    dve.wait_ge(s_bw, 2)
                    dve.wait_ge(s_y2, 2 * i + s + 1)
                    dve.bn_stats(grp(st6, 2 * i + s, 6), grp(acc, 2 * i + s)).then_inc(s_bn[s], 1)
            row_stats(dve, 3)
            with dve.Fori(0, NP) as i:
                for s in range(2):
                    dve.wait_ge(s_z2, 2 * i)
                    dve.tensor_scalar(z1[s][0:R, :], grp(acc, 2 * i + s), col(mean, 2 * i + s), col(rstd, 2 * i + s),
                                      ALU.subtract, ALU.mult).then_inc(s_z1, 1)
                for s in range(2):
                    dve.wait_ge(s_z1, 2 * i + s + 1)
                    dve.tensor_tensor(z2[s][0:R, :], z1[s][0:R, :], gam_t[0:R, :], ALU.mult).then_inc(s_z2, 1)
                for s in range(2):
                    dve.wait_ge(s_z2, 2 * i + s + 1)
                    dve.tensor_tensor(z3[s][0:R, :], z2[s][0:R, :], bet_t[0:R, :], ALU.add).then_inc(s_z3, 1)
                for s in range(2):
                    dve.wait_ge(s_z3, 2 * i + s + 1)
                    dve.tensor_tensor(grp(h, 2 * i + s), grp(h, 2 * i + s), z3[s][0:R, :], ALU.add).then_inc(s_h[s], 1)
                for s in range(2):
                    dve.wait_ge(s_bw, 2)
                    dve.wait_ge(s_h[s], i + 1 + 2 * NP)
                    dve.bn_stats(grp(st6, 2 * i + s, 6), grp(h, 2 * i + s)).then_inc(s_bn[s], 1)
            row_stats(dve, 4)

            for c in range(2):
                for half in range(2):
                    dve.memset(qscale[half * D1:(half + 1) * D1, c:c + 1], float(D1) ** -0.5 if c == half else 0.0
                                ).then_inc(s_qs, 1)
            dve.wait_ge(s_w4, 3 * 16)

            def rows1(i):
                for s in range(2):
                    dve.wait_ge(s_xTp[s], i + 2 * NP)
                    dve.tensor_scalar(xn[s][0:R, :], grp(h, 2 * i + s), col(mean, 2 * i + s), col(rstd, 2 * i + s),
                                      ALU.subtract, ALU.mult).then_inc(s_xn[s], 1)

            def keys1(i):
                for n in range(3, 6):
                    dve.wait_ge(s_qkp[n], i + 1)
                    dve.tensor_copy(k1T[:, 2 * n - 6:2 * n - 4, :],
                                    bank[2 + n][:, 0:2 * PH].rearrange("p (m r) -> p m r", m=2)).then_inc(s_qk[n], 1)

            def attend1(i, more):
                if more:
                    rows1(i + 1)
                for s in range(2):
                    dve.wait_ge(s_sp[s], i + 1 + NP)
                    dve.tensor_tensor(sm[s][0:R, :, :].rearrange("p (b j) r -> p b j r", b=4),
                                      ps[0:R, 0:4, 0:3 * R].rearrange("p b (j r) -> p b j r", j=3),
                                      bmask[0:R, :].unsqueeze(1).unsqueeze(1).broadcast_to([R, 4, 3, R]),
                                      ALU.add).then_inc(s_sm[s], 1)
                    dve.wait_ge(s_sm[s], i + 1)
                    dve.tensor_reduce(nmx[s][0:R, :], sm[s][0:R, :, :], AX, ALU.max, negate=True).then_inc(s_mx, 1)
                if more:
                    keys1(i + 1)
                for s in range(2):
                    dve.wait_ge(s_exp[s], i + 1 + NP)
                    dve.reciprocal(rden[s][0:R, :], den[s][0:R, :]).then_inc(s_rd, 1)
                    for b in range(3):
                        dve.wait_ge(s_pt1p[s][b], i + 1)
                        dve.tensor_copy(pt1[s][0:R, 4 * b:4 * b + 4, :],
                                        bank[5 + b][0:R, 0:4 * R].rearrange("p (n r) -> p n r", n=4)).then_inc(s_pt1[s][b], 1)
                    dve.wait_ge(s_rd, 2 * i + s + 1 + 2 * NP)
                    dve.wait_ge(s_op[s], i + 1 + NP)
                    dve.tensor_tensor(cx[s][0:R, :].rearrange("p (b j d) -> p b j d", b=2, j=H1 // 2),
                                      ps[0:R, 0:2, 0:A1 // 2].rearrange("p b (j d) -> p b j d", j=H1 // 2),
                                      rden[s][0:R, :].rearrange("p (b j) -> p b j", b=2).unsqueeze(3)
                                      .broadcast_to([R, 2, H1 // 2, D1]), ALU.mult).then_inc(s_ct[s], 1)
                for s in range(2):
                    dve.wait_ge(s_bw, 2)
                    dve.wait_ge(s_ap[s], i + 1 + NP)
                    dve.tensor_tensor(grp(h, 2 * i + s), bank[4][0:R, s * D:(s + 1) * D], grp(h, 2 * i + s),
                                      ALU.add).then_inc(s_h[s], 1)
                for s in range(2):
                    dve.wait_ge(s_bw, 2)
                    dve.wait_ge(s_h[s], i + 1 + 3 * NP)
                    dve.bn_stats(grp(st6, 2 * i + s, 6), grp(h, 2 * i + s)).then_inc(s_bn[s], 1)

            rows1(0)
            keys1(0)
            with dve.Fori(0, NP - 1) as i:
                attend1(i, True)
            attend1(NP - 1, False)
            row_stats(dve, 5)

            dve.wait_ge(s_w5, 10 * 16)
            with dve.Fori(0, NP) as i:
                for s in range(2):
                    dve.wait_ge(s_xTp[s], i + 3 * NP)
                    dve.tensor_scalar(xn[s][0:R, :], grp(h, 2 * i + s), col(mean, 2 * i + s), col(rstd, 2 * i + s),
                                      ALU.subtract, ALU.mult).then_inc(s_xn[s], 1)
                for s in range(2):
                    dve.wait_ge(s_lgp, 2 * i + s + 1 + 2 * NP)
                    dve.tensor_tensor(grp(lg1, 2 * i + s, E1), bank[5 + s][0:R, 0:E1], rt1b_t[0:R, :],
                                      ALU.add).then_inc(s_lg, 1)
            dve.wait_ge(s_sc, 1)
            dve.tensor_tensor(sfc[0:R, :, :], sc1[0:R, :, :], corr_t[0:R, :].unsqueeze(1).broadcast_to([R, NG, E1]),
                              ALU.add).then_inc(s_r5, 1)
            dve.wait_ge(s_r5, 1)
            s4 = sfc[0:R, :, :].rearrange("p g (c e) -> p (g c) e", e=GE)
            for d, o in ((1, 0), (2, 3), (3, 5)):
                dve.tensor_tensor(psum1[0:R, :, o:o + GE - d], s4[:, :, 0:GE - d], s4[:, :, d:GE], ALU.add).then_inc(s_r5, 1)
            dve.wait_ge(s_r5, 4)
            dve.tensor_reduce(gtop[0:R, :, :], psum1[0:R, :, :].rearrange("p (g c) e -> p g c e", g=NG), AX,
                              ALU.max).then_inc(s_r5, 1)

            def ranks(val, cmp, tri, rank, n, at):
                c = cmp[0:R, :, :].rearrange("p g (e w j) -> p g e w j", e=n, w=2)
                mine = val[0:R, :, :].unsqueeze(3).broadcast_to([R, NG, n, n])
                other = val[0:R, :, :].unsqueeze(2).broadcast_to([R, NG, n, n])
                dve.wait_ge(s_r5, at)
                dve.tensor_tensor(c[:, :, :, 0, :], other, mine, ALU.is_gt).then_inc(s_r5, 1)
                dve.tensor_tensor(c[:, :, :, 1, :], other, mine, ALU.is_ge).then_inc(s_r5, 1)
                dve.wait_ge(s_r5, at + 2)
                dve.tensor_tensor(cmp[0:R, :, :], cmp[0:R, :, :], tri[0:R, :].unsqueeze(1).broadcast_to([R, NG, 2 * n * n]),
                                  ALU.mult).then_inc(s_r5, 1)
                dve.wait_ge(s_r5, at + 3)
                dve.tensor_reduce(rank[0:R, :, :], cmp[0:R, :, :].rearrange("p g (e w) -> p g e w", e=n), AX,
                                  ALU.add).then_inc(s_r5, 1)
                dve.wait_ge(s_r5, at + 4)

            ranks(gtop, gcmp, trig, grank, G1, 5)
            dve.scalar_tensor_tensor(skept[0:R, :, :].rearrange("p g (c e) -> p (g c) e", e=GE),
                                     grank[0:R, :, :].rearrange("p g c -> p (g c)").unsqueeze(2).broadcast_to([R, NG * G1, GE]),
                                     2.0, s4, ALU.is_lt, ALU.mult).then_inc(s_r5, 1)
            ranks(skept, cmp1, tri1, lg1, E1, 10)
            dve.wait_ge(s_c1, 1)
            dve.scalar_tensor_tensor(sfc[0:R, :, :], lg1[0:R, :, :], float(K1), sc1[0:R, :, :], ALU.is_lt,
                                     ALU.mult).then_inc(s_r5, 1)
            dve.wait_ge(s_r5, 15)
            dve.tensor_reduce(wsum[0:R, :], sfc[0:R, :, :], AX, ALU.add).then_inc(s_r5, 1)
            dve.wait_ge(s_r5, 16)
            dve.tensor_scalar(wsum1[0:R, :], wsum[0:R, :], 1e-20, None, ALU.add).then_inc(s_r5, 1)
            dve.wait_ge(s_r5, 17)
            dve.reciprocal(wrec[0:R, :], wsum1[0:R, :]).then_inc(s_r5, 1)
            dve.wait_ge(s_r5, 18)
            dve.scalar_tensor_tensor(c1[0:R, :, 0:E1], sfc[0:R, :, :], SCALE1,
                                     wrec[0:R, :].unsqueeze(2).broadcast_to([R, NG, E1]), ALU.mult, ALU.mult).then_inc(s_r5, 1)
            dve.wait_ge(s_r5, R5_END)

            def weigh(i, e):
                dve.wait_ge(s_dn, E1 * i + e + 1)
                for s in range(2):
                    y = bank[4 + e % 2][0:R, s * D:(s + 1) * D]
                    if e == 0:
                        dve.wait_ge(s_wes, 2 * i + s + 1 + 2 * NP)
                        dve.wait_ge(s_o5, 2 * i)
                        dve.tensor_scalar(acc5[s][0:R, :], y, cs[s][0:R, 0:1], None, ALU.mult).then_inc(s_ac5, 1)
                    else:
                        dve.wait_ge(s_ac5, 2 * E1 * i + 2 * e - 1 + s)
                        dve.scalar_tensor_tensor(acc5[s][0:R, :], y, cs[s][0:R, e:e + 1], acc5[s][0:R, :], ALU.mult,
                                                 ALU.add).then_inc(s_ac5, 1)

            with dve.Fori(0, NP) as i:
                for s in range(2):
                    dve.wait_ge(s_xTp[s], i + 4 * NP)
                    dve.tensor_scalar(xn[s][0:R, :], grp(h, 2 * i + s), col(mean, 2 * i + s), col(rstd, 2 * i + s),
                                      ALU.subtract, ALU.mult).then_inc(s_xn[s], 1)
                for e in range(EX):
                    dve.wait_ge(s_sg, EX * i + e + 1)
                    dve.wait_ge(s_dn, E1 * i + min(max(e - 2, 0), E1))
                    if e < 3:
                        dve.wait_ge(s_sh, i)
                    dve.scalar_tensor_tensor(hid[e % 3][0:F1, :], bank[2 + e % 2][0:F1, 0:PH], bu_t[0:F1, e:e + 1],
                                             sg[e % 2][0:F1, :], ALU.add, ALU.mult).then_inc(s_hid, 1)
                    if 1 <= e <= E1:
                        weigh(i, e - 1)
                for s in range(2):
                    dve.wait_ge(s_ac5, 2 * E1 * i + 2 * E1 - 1 + s)
                    dve.wait_ge(s_sh, i + 1)
                    dve.tensor_tensor(o5[s][0:R, :], bank[6][0:R, s * D:(s + 1) * D], acc5[s][0:R, :], ALU.add).then_inc(s_o5, 1)
                for s in range(2):
                    dve.wait_ge(s_o5, 2 * i + s + 1)
                    dve.wait_ge(s_outs[s], 16 * i)
                    dve.tensor_tensor(oh[s][0:R, :], o5[s][0:R, :], grp(h, 2 * i + s), ALU.add).then_inc(s_oh, 1)

        @block.tensor
        def _(pe):
            pe.wait_ge(s_tokw, 5 * 16)
            pe.wait_ge(s_ones, 1)
            pe.matmul(bank[0][0:1, 0:D], ones[0:1, 0:1], tb_row[:, :], start=True, stop=False)
            for k in range(KB):
                for j in range(NS):
                    row = pe.matmul(bank[0][0:1, 0:D], tbe[0:KP, k, j:j + 1], tw[0:KP, k, j, :],
                                    start=False, stop=(k == KB - 1 and j == NS - 1))
            row.then_inc(s_bwrow_p, 1)
            pe.wait_ge(s_weff, KB * NS)
            pe.wait_ge(s_cnt, 1)
            for k in range(KB):
                pe.matmul(bank[1][0:R, 0:D], ones[0:KP, 0:R], weff[0:KP, k, 0:D], start=(k == 0), stop=(k == KB - 1))
            pe.wait_ge(s_bwrow, 1)
            pe.matmul(bank[1][0:R, D:2 * D], ones[0:1, 0:R], bw_row[:, :], start=True, stop=True).then_inc(s_bw_p, 1)
            with pe.Fori(0, NP) as i:
                for s in range(2):
                    pe.wait_ge(s_x[s], 16 * i + 16)
                    pe.wait_ge(s_raw[s], i)
                    for k in range(KB):
                        pe.matmul(bank[2 + s][0:R, 0:D + 1], xp[s][0:KP, k, :], weff[0:KP, k, :],
                                  start=(k == 0), stop=(k == KB - 1))
                    pe.wait_ge(s_xsq[s], i + 1)
                    for k in range(KB):
                        mm = pe.matmul(bank[2 + s][0:R, D + 1:D + 2], xsq[s][0:KP, k, :], weff[0:KP, k, D:D + 1],
                                       start=(k == 0), stop=(k == KB - 1))
                    mm.then_inc(s_emb[s], 1)
            for s in range(2):
                pe.wait_ge(s_raw[s], NP)

            pe.wait_ge(s_const, 16)
            pe.wait_ge(s_w0, 13 * 16)
            pe.wait_ge(s_sw, 5)
            with pe.Fori(0, NP) as i:
                for s in range(2):
                    pe.wait_ge(s_kT, 2 * i)
                    pe.wait_ge(s_xn[s], i + 1)
                    for k in range(2):
                        tr = pe.transpose(bank[4 * s][0:HW, k * R:(k + 1) * R], xn[s][0:R, k * HW:(k + 1) * HW],
                                          ident[0:R, 0:R])
                    tr.then_inc(s_xTp[s], 1)
                for s in range(2):
                    pe.wait_ge(s_xT[s], i + 1)
                    for k in range(2):
                        mm = pe.matmul(bank[4 * s + 1][0:R, 0:R], wz[0:HW, k, :], xT[0:HW, k, s * R:(s + 1) * R],
                                       start=(k == 0), stop=(k == 1))
                    mm.then_inc(s_zp, 1)
                for hh in range(2):
                    for k in range(2):
                        mm = pe.matmul(bank[0][0:HW, hh * PH:(hh + 1) * PH],
                                       wqkv_t[0:HW, k, D + hh * HW:D + (hh + 1) * HW], xT[0:HW, k, :],
                                       start=(k == 0), stop=(k == 1))
                mm.then_inc(s_kp, 1)
                for s in range(2):
                    pe.wait_ge(s_exp[s], i)
                    for k in range(2):
                        mm = pe.matmul(bank[4 * s + 2][0:R, 0:D], xT[0:HW, k, s * R:(s + 1) * R],
                                       wqkv_t[0:HW, k, 2 * D:3 * D], start=(k == 0), stop=(k == 1))
                    mm.then_inc(s_vp[s], 1)
                for s in range(2):
                    pe.wait_ge(s_psel, 2 * i + s + 1)
                    pe.wait_ge(s_y0, 2 * i)
                    pe.transpose(bank[4 * s + 3][0:QG, 0:R], psel[s][0:R, 0:QG], ident[0:R, 0:R]).then_inc(s_ptp0, 1)
                    for k in range(2):
                        mm = pe.matmul(bank[4 * s + 1][0:HW, R + k * QG:R + (k + 1) * QG], xn[s][0:R, k * HW:(k + 1) * HW],
                                       psel[s][0:R, 0:QG], start=True, stop=True)
                    mm.then_inc(s_xsp, 1)
                for s in range(2):
                    pe.wait_ge(s_xs, 2 * i + s + 1)
                    for hh in range(2):
                        for k in range(2):
                            mm = pe.matmul(bank[4 * s + 1][0:HW, 256 + hh * QG:256 + (hh + 1) * QG],
                                           wqkv_t[0:HW, k, hh * HW:(hh + 1) * HW], xs[s][0:HW, k, :],
                                           start=(k == 0), stop=(k == 1))
                    mm.then_inc(s_qp, 1)
                for s in range(2):
                    pe.wait_ge(s_kT, 2 * i + 2)
                    pe.wait_ge(s_v[s], i + 1)
                    pe.wait_ge(s_qb[s], 2 * i + 2)
                    for hh in range(2):
                        o = bank[4 * s + 2][0:R, D + hh * R:D + (hh + 1) * R]
                        pe.matmul(o, psel[s][0:R, :], cmask[0:R, :], start=True, stop=False)
                        mm = pe.matmul(o, qb[s][0:HW, hh, :], kT[0:HW, hh, s * R:(s + 1) * R], start=False, stop=True)
                    mm.then_inc(s_sp[s], 1)
                for s in range(2):
                    pe.wait_ge(s_pselT, 2 * i + s + 1)
                    pe.wait_ge(s_pn, 2 * i + s + 1)
                    for hh in range(2):
                        tr = pe.transpose(bank[4 * s + 3][0:R, hh * R:(hh + 1) * R], pn[s][0:R, hh, :], ident[0:R, 0:R])
                    tr.then_inc(s_ptp[s], 1)
                for s in range(2):
                    pe.wait_ge(s_pt[s], i + 1)
                    for hh in range(2):
                        mm = pe.matmul(bank[4 * s + 3][0:HW, hh * R:(hh + 1) * R], v0[s][0:R, hh * HW:(hh + 1) * HW],
                                       pt0[s][0:R, hh, :], start=True, stop=True)
                    mm.then_inc(s_op[s], 1)
                for s in range(2):
                    pe.wait_ge(s_ct[s], i + 1)
                    for hh in range(2):
                        mm = pe.matmul(bank[4 * s + 3][0:QG, 0:D], ct0[s][0:HW, hh, :], wo_t[0:HW, hh, :],
                                       start=(hh == 0), stop=(hh == 1))
                    mm.then_inc(s_ap[s], 1)
                for s in range(2):
                    pe.wait_ge(s_at, 2 * i + s + 1)
                    pe.matmul(bank[4 * s + 3][0:R, D:2 * D], pselT[s][0:QG, :], at0[s][0:QG, :], start=True,
                              stop=True).then_inc(s_up, 1)
            for s in range(2):
                pe.wait_ge(s_y0, 2 * NP)

            pe.wait_ge(s_w3, 6 * 16)
            with pe.Fori(0, NP) as i:
                for s in range(2):
                    pe.wait_ge(s_xT[s], i + NP)
                    pe.wait_ge(s_xn[s], i + 1 + NP)
                    for k in range(2):
                        tr = pe.transpose(bank[4 * s][0:HW, k * R:(k + 1) * R], xn[s][0:R, k * HW:(k + 1) * HW],
                                          ident[0:R, 0:R])
                    tr.then_inc(s_xTp[s], 1)
                for s in range(2):
                    pe.wait_ge(s_lg, 2 * i)
                    pe.wait_ge(s_xT[s], i + 1 + NP)
                    for k in range(2):
                        mm = pe.matmul(bank[4 * s + 1][0:R, 0:E0], xT[0:HW, k, s * R:(s + 1) * R], rtw_t[0:HW, k, :],
                                       start=(k == 0), stop=(k == 1))
                    mm.then_inc(s_lgp, 1)
            for s in range(2):
                pe.wait_ge(s_xTa, 2 * NP)
                pe.wait_ge(s_lg, 2 * NP)
            with pe.Fori(0, E0 // 2) as ie:
                for n in range(2):
                    with pe.Fori(0, NP) as i:
                        pe.wait_ge(s_we[n], 48 * ie + 48)
                        for b in range(3):
                            pe.wait_ge(s_hT[b], (2 * ie + n) * NP + i)
                            for m in (2 * b, 2 * b + 1):
                                for k in range(2):
                                    mm = pe.matmul(bank[b][:, (m % 2) * PH:(m % 2 + 1) * PH],
                                                   w1_t[n][0:HW, k, m * 128:(m + 1) * 128],
                                                   xTall[0:HW, k, bass.ds(i * PH, PH)], start=(k == 0), stop=(k == 1))
                            mm.then_inc(s_hp[b], 1)
                        for s in range(2):
                            pe.wait_ge(s_acc[s], (2 * ie + n) * NP + i)
                        for m in range(FB0):
                            if m % 2 == 0:
                                pe.wait_ge(s_hT[m // 2], (2 * ie + n) * NP + i + 1)
                            for s in range(2):
                                mm = pe.matmul(bank[3 + s][0:R, 0:D], hT[:, m, s * R:(s + 1) * R], w2_t[n][:, m, :],
                                               start=(m == 0), stop=(m == FB0 - 1))
                                if m == FB0 - 1:
                                    mm.then_inc(s_yp[s], 1)
            for s in range(2):
                pe.wait_ge(s_acc[s], E0 * NP)
            with pe.Fori(0, NP) as i:
                for s in range(2):
                    pe.wait_ge(s_weT, 2 * i)
                    pe.wait_ge(s_wes, 2 * i + s + 1)
                    pe.transpose(bank[4 * s][0:E0, 0:R], wes[s][0:R, :], ident[0:R, 0:R]).then_inc(s_weTp, 1)
                for s in range(2):
                    pe.wait_ge(s_y1, 2 * i)
                    pe.wait_ge(s_weT, 2 * i + s + 1)
                    pe.matmul(bank[4 * s + 1][0:R, 0:D], weT[s][0:E0, :], b2_t[0:E0, :], start=True,
                              stop=True).then_inc(s_b2p, 1)

            pe.wait_ge(s_w4, 3 * 16)
            pe.wait_ge(s_y1, 2 * NP)

            def front1(i):
                for s in range(2):
                    pe.wait_ge(s_h[s], i - 1 + 3 * NP)
                    pe.wait_ge(s_xn[s], i + 1 + 3 * NP)
                    for k in range(2):
                        tr = pe.transpose(bank[4][0:HW, s * PH + k * R:s * PH + (k + 1) * R], xn[s][0:R, k * HW:(k + 1) * HW],
                                          ident[0:R, 0:R])
                    tr.then_inc(s_xTp[s], 1)
                for s in range(2):
                    pe.wait_ge(s_xT[s], i + 1 + 2 * NP)
                for n in range(6):
                    if n >= 3:
                        pe.wait_ge(s_qk[n - 3], i + 1)
                    for m in (2 * n, 2 * n + 1):
                        for k in range(2):
                            mm = pe.matmul(bank[5 + n % 3][:, (m % 2) * PH:(m % 2 + 1) * PH],
                                           w1qkv[0:HW, k, m * 128:(m + 1) * 128], xT[0:HW, k, :],
                                           start=(k == 0), stop=(k == 1))
                    mm.then_inc(s_qkp[n], 1)

            def attend1(i, more):
                for s in range(2):
                    if s == 0:
                        for n in range(3, 6):
                            pe.wait_ge(s_qk[n], i + 1)
                        for b in range(3):
                            pe.wait_ge(s_pt1[1][b], i)
                    else:
                        pe.wait_ge(s_v[0], i + 1 + NP)
                    for b in range(2):
                        for k in range(2):
                            mm = pe.matmul(bank[5 + b][0:R, 0:A1 // 2], xT[0:HW, k, s * R:(s + 1) * R],
                                           w1qkv[0:HW, k, 2 * A1 + b * A1 // 2:2 * A1 + (b + 1) * A1 // 2],
                                           start=(k == 0), stop=(k == 1))
                    mm.then_inc(s_vp[s], 1)
                    if s == 0:
                        pe.wait_ge(s_ct[1], i + NP)
                        pe.wait_ge(s_cT[1], i)
                    else:
                        pe.wait_ge(s_sm[0], i + 1)
                    for n in range(H1):
                        hd = head_at(n)
                        mm = pe.matmul(bank[n // 3][0:R, (n % 3) * R:(n % 3 + 1) * R], qT[hd % 2][:, hd // 2, s * R:(s + 1) * R],
                                       k1T[:, hd // 2, s * R:(s + 1) * R], start=True, stop=True)
                    mm.then_inc(s_sp[s], 1)
                pe.wait_ge(s_v[1], i + 1 + NP)
                if more:
                    front1(i + 1)
                    for n in range(3, 6):
                        pe.wait_ge(s_qk[n], i + 2)
                for s in range(2):
                    pe.wait_ge(s_exp[s], i + 1 + NP)
                    for b in range(3):
                        if s == 1:
                            pe.wait_ge(s_pt1[0][b], i + 1)
                        for n in range(4):
                            tr = pe.transpose(bank[5 + b][0:R, n * R:(n + 1) * R], p1[s][0:R, 4 * b + n, :], ident[0:R, 0:R])
                        tr.then_inc(s_pt1p[s][b], 1)
                    if s == 0:
                        pe.wait_ge(s_sm[1], i + 1)
                    else:
                        pe.wait_ge(s_ct[0], i + 1 + NP)
                    for n in range(H1):
                        if n % 4 == 0:
                            pe.wait_ge(s_pt1[s][n // 4], i + 1)
                        mm = pe.matmul(bank[n // 6][0:R, (n % 6) * D1:(n % 6 + 1) * D1], pt1[s][0:R, n, :],
                                       v1[s][0:R, n * D1:(n + 1) * D1], start=True, stop=True)
                    mm.then_inc(s_op[s], 1)
                for s in range(2):
                    pe.wait_ge(s_ct[s], i + 1 + NP)
                    if s == 1:
                        pe.wait_ge(s_cT[0], i + 1)
                    for m in range(MB1):
                        tr = pe.transpose(bank[2 + m // 3][:, (m % 3) * R:(m % 3 + 1) * R], cx[s][0:R, m * 128:(m + 1) * 128],
                                          ident[0:R, 0:R])
                    tr.then_inc(s_cTp[s], 1)
                for s in range(2):
                    pe.wait_ge(s_cT[s], i + 1)
                    if s == 1:
                        pe.wait_ge(s_h[0], i + 1 + 3 * NP)
                    for m in range(MB1):
                        mm = pe.matmul(bank[4][0:R, s * D:(s + 1) * D], cT[s][:, m, :], wo1_t[:, m, :],
                                       start=(m == 0), stop=(m == MB1 - 1))
                    mm.then_inc(s_ap[s], 1)

            front1(0)
            with pe.Fori(0, NP - 1) as i:
                attend1(i, True)
            attend1(NP - 1, False)
            for s in range(2):
                pe.wait_ge(s_h[s], 4 * NP)

            pe.wait_ge(s_w5, 10 * 16)
            pe.wait_ge(s_wgu, 2 * 16)
            with pe.Fori(0, NP) as i:
                for s in range(2):
                    pe.wait_ge(s_xT[1], i + 3 * NP)
                    pe.wait_ge(s_xn[s], i + 1 + 4 * NP)
                    for k in range(2):
                        tr = pe.transpose(bank[4][0:HW, s * PH + k * R:s * PH + (k + 1) * R], xn[s][0:R, k * HW:(k + 1) * HW],
                                          ident[0:R, 0:R])
                    tr.then_inc(s_xTp[s], 1)
                for s in range(2):
                    pe.wait_ge(s_lg, 2 * i + 2 * NP)
                    pe.wait_ge(s_xT[s], i + 1 + 3 * NP)
                    for k in range(2):
                        mm = pe.matmul(bank[5 + s][0:R, 0:E1], xT[0:HW, k, s * R:(s + 1) * R], rt1w_t[0:HW, k, :],
                                       start=(k == 0), stop=(k == 1))
                    mm.then_inc(s_lgp, 1)
            pe.wait_ge(s_xT[1], 4 * NP)
            pe.wait_ge(s_lg, 4 * NP)

            def down(i, e):
                pe.wait_ge(s_hid, EX * i + e + 1)
                pe.wait_ge(s_ac5, 2 * E1 * i + 2 * max(e - 1, 0))
                for s in range(2):
                    mm = pe.matmul(bank[4 + e % 2][0:R, s * D:(s + 1) * D], hid[e % 3][0:F1, s * R:(s + 1) * R],
                                   wd_t[0:F1, e, :], start=True, stop=True)
                mm.then_inc(s_dn, 1)

            with pe.Fori(0, NP) as i:
                for s in range(2):
                    pe.wait_ge(s_weT, 2 * i + 2 * NP)
                    pe.wait_ge(s_xn[s], i + 1 + 5 * NP)
                    for k in range(2):
                        tr = pe.transpose(bank[7][0:HW, s * PH + k * R:s * PH + (k + 1) * R], xn[s][0:R, k * HW:(k + 1) * HW],
                                          ident[0:R, 0:R])
                    tr.then_inc(s_xTp[s], 1)
                for s in range(2):
                    pe.wait_ge(s_xT[1], i + 1 + 4 * NP)
                    pe.wait_ge(s_wes, 2 * i + s + 1 + 2 * NP)
                    pe.transpose(bank[7][0:E1 + 1, s * R:(s + 1) * R], cs[s][0:R, :], ident[0:R, 0:R]).then_inc(s_weTp, 1)
                for e in range(EX):
                    pe.wait_ge(s_hid, EX * i + max(e - 1, 0))
                    for w, b in ((wg_t, 0), (wu_t, 2)):
                        for k in range(2):
                            mm = pe.matmul(bank[b + e % 2][0:F1, 0:PH], w[0:HW, k, e * F1:(e + 1) * F1], xT[0:HW, k, :],
                                           start=(k == 0), stop=(k == 1))
                    mm.then_inc(s_gp, 1)
                    if 1 <= e <= E1:
                        down(i, e - 1)
                pe.wait_ge(s_hid, EX * i + EX)
                pe.wait_ge(s_weT, 2 * i + 2 + 2 * NP)
                pe.wait_ge(s_o5, 2 * i)
                for s in range(2):
                    o = bank[6][0:R, s * D:(s + 1) * D]
                    pe.matmul(o, weT[s][0:E1 + 1, :], bd_t[0:E1 + 1, :], start=True, stop=False)
                    for e in (E1, E1 + 1):
                        mm = pe.matmul(o, hid[e % 3][0:F1, s * R:(s + 1) * R], wd_t[0:F1, e, :], start=False,
                                       stop=(e == E1 + 1))
                mm.then_inc(s_sh, 1)


def _parts(a):
    a = np.pad(a, [(0, KB * KP - FEAT)] + [(0, 0)] * (a.ndim - 1))
    return np.ascontiguousarray(a.reshape(KB, KP, *a.shape[1:]).swapaxes(0, 1))


def _patches(x):
    xh = np.zeros((NG * IPG, C_IN, SIDE + 2, SIDE + 2), np.float32)
    xh[:N_IMG, :, 1:-1, 1:-1] = x
    f = np.empty((C_IN, HALO, HALO, NG * IPG, GRID, GRID), np.float32)
    for a in range(HALO):
        for b in range(HALO):
            f[:, a, b] = xh[:, :, a:a + SIDE:PATCH, b:b + SIDE:PATCH].swapaxes(0, 1)
    f = _parts(f.reshape(FEAT, NG, R))
    return np.ascontiguousarray(f.transpose(2, 0, 1, 3)).reshape(NG, KP, KB * R)


def _shifted(w):
    w = np.asarray(w).reshape(PATCH, PATCH, NS, C_IN, -1)
    o = np.zeros((C_IN, HALO, HALO, NS, w.shape[-1]), np.float32)
    for j, (dy, dx) in enumerate(SHIFTS):
        o[:, 1 + dy:1 + dy + PATCH, 1 + dx:1 + dx + PATCH, j] = w[:, :, j].transpose(2, 0, 1, 3)
    return _parts(o.reshape(FEAT, NS, -1))


def _halves(w):
    w = np.asarray(w)
    return np.ascontiguousarray(w.reshape(2, HW, -1).swapaxes(0, 1))


def _tables():
    tok = np.arange(R)
    same = tok[:, None] // TOK == tok[None, :] // TOK
    later = (same & (tok[None, :] > tok[:, None])).astype(np.float32)
    earlier = (same & (tok[None, :] < tok[:, None])).astype(np.float32)
    bmask = np.where(same, 0.0, -1e30).astype(np.float32)
    cmask = np.where(same, np.where(later > 0, -10000.0, 0.0), -1e30).astype(np.float32)
    slot = np.tile(np.arange(QG), HH)
    rtab = np.where(tok[:, None] // TOK == slot[None, :] // KSEL, slot[None, :] % KSEL, -1).astype(np.float32)
    head = np.repeat(np.arange(HH), QG)
    hmask = (np.arange(HW)[:, None] // D0 == head[None, :]).astype(np.float32)

    def tri(n):
        j, e = np.arange(n)[None, :], np.arange(n)[:, None]
        t = np.stack([(j > e), (j < e)], 1).astype(np.float32).reshape(1, n * 2 * n)
        return np.ascontiguousarray(np.broadcast_to(t, (R, n * 2 * n)))
    return dict(ident=np.eye(128, dtype=np.float32), cmask=cmask, bmask=bmask, later=later, earlier=earlier,
                rtab=rtab, hmask=hmask, tri0=tri(E0), tri1=tri(E1), trig=tri(G1))


def kernel(**inputs):
    import concourse.bacc as _bacc
    from concourse.bass_utils import run_bass_kernel_spmd as _run

    a = {k: np.asarray(v) for k, v in inputs.items()}
    count = np.zeros((C_IN, HALO, HALO), np.float32)
    for dy, dx in SHIFTS:
        count[:, 1 + dy:1 + dy + PATCH, 1 + dx:1 + dx + PATCH] += 1
    t = _tables()
    rep = lambda v: np.ascontiguousarray(np.broadcast_to(np.asarray(v).reshape(1, -1), (R, np.asarray(v).size)))
    wqkv1 = a["L1_attn_w_qkv"].transpose(2, 1, 0, 3).reshape(D, 3 * A1)
    arrays = dict(
        x=_patches(a["x"]), tok_w=_shifted(a["L0_tok_W"]).reshape(KP, KB * NS * D),
        tok_g=_shifted(a["L0_tok_ln_gamma"])[..., 0], tok_be=_shifted(a["L0_tok_ln_beta"])[..., 0],
        tok_b=a["L0_tok_b"].reshape(1, D), tok_cnt=_parts(count.reshape(FEAT, 1)),
        wqkv=_halves(a["L0_attn_Wqkv_w"]),
        bqk=a["L0_attn_Wqkv_b"][:2 * D].reshape(4, HW).T,
        bv=rep(a["L0_attn_Wqkv_b"][2 * D:]), sel_w=_halves(a["L0_attn_sel_w"]), sel_b=rep(a["L0_attn_sel_b"]),
        temp=rep(a["L0_attn_temperature"]), wo=_halves(a["L0_attn_out_w"]), bo=rep(a["L0_attn_out_b"]),
        rt_w=_halves(a["L0_ffn_router_w"]), rt_b=rep(a["L0_ffn_router_b"]),
        w1=a["L0_ffn_w1"].reshape(E0, 2, HW, F0).transpose(0, 2, 1, 3),
        b1=a["L0_ffn_b1"].reshape(E0, FB0, 128).transpose(0, 2, 1),
        w2=a["L0_ffn_w2"].reshape(E0, FB0, 128, D).transpose(0, 2, 1, 3),
        b2=a["L0_ffn_b2"], gam=rep(a["L0_ffn_gamma"]), bet=rep(a["L0_ffn_beta"]),
        wqkv1=_halves(wqkv1), wo1=a["L1_attn_w_o"].reshape(MB1, 128, D).transpose(1, 0, 2),
        rt1_w=_halves(a["L1_ffn_router_w"].T), rt1_b=rep(a["L1_ffn_router_b"]), corr=rep(a["L1_ffn_corr_bias"]),
    )
    for name, g, s, b, bs in (("gate", "gWg", "sWg", "gbg", "sbg"), ("up", "gWu", "sWu", "gbu", "sbu")):
        w = np.concatenate([a["L1_ffn_" + g].transpose(1, 0, 2).reshape(D, E1 * F1), a["L1_ffn_" + s]], 1)
        arrays["w_" + name] = _halves(w)
        arrays["b_" + name] = np.concatenate([a["L1_ffn_" + b].reshape(-1), a["L1_ffn_" + bs]]).reshape(EX, F1).T
    wd = np.concatenate([a["L1_ffn_gWd"].reshape(E1 * F1, D), a["L1_ffn_sWd"]], 0)
    arrays["w_down"] = wd.reshape(EX, F1, D).transpose(1, 0, 2)
    arrays["b_down"] = a["L1_ffn_gbd"]
    arrays["sb_down"] = a["L1_ffn_sbd"].reshape(1, D)
    for k, v in t.items():
        arrays[k + "_c"] = v
    nc = _bacc.Bacc("TRN2", target_bir_lowering=False, num_devices=1)
    arrays = {k: np.ascontiguousarray(v) for k, v in arrays.items()}
    args = {k: nc.dram_tensor("in_" + k, v.shape, mybir.dt.from_np(v.dtype), kind="ExternalInput").ap()
            for k, v in arrays.items()}
    args["out"] = nc.dram_tensor("out", (NG, R, D), mybir.dt.float32, kind="ExternalOutput").ap()
    vit_tower(nc, **args)
    r = _run(nc, [{"in_" + k: v for k, v in arrays.items()}], core_ids=[0])
    return r.results[0]["out"].reshape(NG * IPG, TOK, D)[:N_IMG]
```

```python
import numpy as np
import concourse.bass as bass
from concourse import mybir
from contextlib import ExitStack


N_IMG, C_IN, SIDE, PATCH = 64, 3, 96, 16
GRID = SIDE // PATCH
TOK = GRID * GRID
IPG = 3
R = IPG * TOK
NG = 2 * -(-N_IMG // (2 * IPG))
NP = NG // 2
D = 192
HW = D // 2
HALO = PATCH + 2
FEAT = C_IN * HALO * HALO
KP = 7 * HALO
KB = -(-FEAT // KP)
NS = 5
SHIFTS = ((0, 0), (0, -1), (0, 1), (-1, 0), (1, 0))
FULL = PATCH * PATCH * NS * C_IN
EPS = 1e-5
H0, D0 = 12, 16
HH = H0 // 2
KSEL = 6
QG = IPG * KSEL
E0, F0 = 8, 4 * D
FB0 = F0 // 128
K0 = 2
TS = 128
NT = (NG * R * K0 - E0) // TS + E0
NTH = -(-NG * R // TS)
H1, D1 = 12, 64
A1 = H1 * D1
MB1 = A1 // 128
E1, F1 = 16, 96
EX = E1 + 2
G1 = 4
GE = E1 // G1
K1 = 4
SCALE1 = 2.5
PH = 2 * R


def vit_tower(nc, x, tok_w, tok_g, tok_be, tok_b, tok_cnt,
              wqkv, bqk, bv, sel_w, sel_b, temp, wo, bo,
              rt_w, rt_b, w1, b1, w2, b2, gam, bet,
              wqkv1, wo1,
              rt1_w, rt1_b, corr, w_gate, b_gate, w_up, b_up, w_down, b_down, sb_down,
              ident_c, before_c, thr_c, below_c, tile_c, cmask_c, bmask_c, later_c, earlier_c, rtab_c, hmask_c, tri0_c, tri1_c, trig_c, out):
    fp32 = mybir.dt.float32
    ALU = mybir.AluOpType
    ACT = mybir.ActivationFunctionType
    AX = mybir.AxisListType.X

    with ExitStack() as ctx:
        def sb(name, shape, dtype=fp32):
            return ctx.enter_context(nc.sbuf_tensor(name, shape, dtype))

        def sem(name):
            return ctx.enter_context(nc.semaphore(name))

        def sem2(name):
            return [sem(f"{name}_{s}") for s in range(2)]

        ps = ctx.enter_context(nc.psum_tensor("ps", [128, 8, 512], fp32))
        bank = [ps[:, n, :] for n in range(8)]

        ident = sb("ident", [128, 128])
        ones = sb("ones", [128, 128])
        h = sb("h", [128, NG, D])
        mean = sb("mean", [128, NG])
        var = sb("var", [128, NG])
        dif = sb("dif", [128, NG])
        dif2 = sb("dif2", [128, NG])
        var2 = sb("var2", [128, NG])
        rstd = sb("rstd", [128, NG])
        sdev = sb("sdev", [128, NG])
        eps_t = sb("eps_t", [128, 1])
        warm = sb("warm", [1, 5])
        xn = [sb(f"xn{s}", [128, D]) for s in range(2)]
        xT = sb("xT", [128, 2, PH])
        st6 = sb("st6", [128, NG, 6])

        A_W = KB * NS * D
        arena1 = sb("arena1", [128, A_W + KB * (D + 1) + 4 * KB * R])
        tw = arena1[:, 0:A_W].rearrange("p (k s d) -> p k s d", k=KB, s=NS)
        tg = sb("tg", [128, KB, NS])
        tbe = sb("tbe", [128, KB, NS])
        weff = arena1[:, A_W:A_W + KB * (D + 1)].rearrange("p (k d) -> p k d", k=KB)
        cnt = sb("cnt", [128, KB, 1])
        tb_row = sb("tb_row", [1, D])
        bw_row = sb("bw_row", [1, D])
        csum = sb("csum", [128, D])
        bw = sb("bw", [128, D])
        patches = arena1[:, A_W + KB * (D + 1):].rearrange("p (n k r) -> p n k r", n=4, k=KB)
        xp = [patches[:, s, :, :] for s in range(2)]
        xsq = [patches[:, 2 + s, :, :] for s in range(2)]
        sums = sb("sums", [128, NG, 2])
        mu = sb("mu", [128, NG])
        nmu = sb("nmu", [128, NG])
        m2 = sb("m2", [128, NG])
        tmp = [sb(f"tmp{s}", [128, D]) for s in range(2)]

        cmask = sb("cmask", [128, R])
        bmask = sb("bmask", [128, R])
        later = sb("later", [128, R])
        earlier = sb("earlier", [128, R])
        rtab = sb("rtab", [128, R])
        hmask = sb("hmask", [128, R])
        hmaskq = sb("hmaskq", [128, R])
        wqkv_t = sb("wqkv_t", [128, 2, 3 * D])
        wo_t = sb("wo_t", [128, 2, D])
        bqk_t = sb("bqk_t", [128, 4])
        bv_t = sb("bv_t", [128, D])
        bo_t = sb("bo_t", [128, D])
        selw_t = sb("selw_t", [128, 2, 2])
        selb_t = sb("selb_t", [128, 2])
        temp_t = sb("temp_t", [128, 1])
        itemp = sb("itemp", [128, 1])
        dselb = sb("dselb", [128, 1])
        bz = sb("bz", [128, 1])
        dselw = sb("dselw", [128, 2, 1])
        wz = sb("wz", [128, 2, R])

        def slots(name, shape):
            return [sb(f"{name}{s}", shape) for s in range(2)]

        kT = sb("kT", [128, 2, PH])
        zr = slots("zr", [128, R])
        zc = slots("zc", [128, 1])
        junk = slots("junk", [128, 3, R])
        rka = slots("rka", [128, 1])
        rkb = slots("rkb", [128, 1])
        psel = slots("psel", [128, R])
        pselT = slots("pselT", [128, R])
        xs = slots("xs", [128, 2, QG])
        qb = slots("qb", [128, 2, R])
        v0 = slots("v0", [128, D])
        nmx = slots("nmx", [128, H1])
        den = slots("den", [128, H1])
        rden = slots("rden", [128, H1])
        p0 = slots("p0", [128, 2, R])
        pn = slots("pn", [128, 2, R])
        pt0 = slots("pt0", [128, 2, R])
        om = slots("om", [128, 2, R])
        ct0 = slots("ct0", [128, 2, QG])
        at0 = slots("at0", [128, D])
        ez = slots("ez", [128, 1])
        ez1 = slots("ez1", [128, 1])
        sig = slots("sig", [128, 1])
        y0 = slots("y0", [128, D])

        arena2 = sb("arena2", [128, 18560])
        taken = [0]

        def part(shape):
            n = int(np.prod(shape))
            v = arena2[:, taken[0]:taken[0] + n]
            taken[0] += n
            names = "abcd"[:len(shape)]
            return v.rearrange(f"p ({' '.join(names)}) -> p {' '.join(names)}",
                               **{c: m for c, m in zip(names, shape)}) if len(shape) > 1 else v

        acc = part([NG, D])
        w2_t = part([E0, FB0, D])
        u32, i32 = mybir.dt.uint32, mybir.dt.int32
        zero = part([D])
        chosen = part([NG, E0])
        place = part([NG, E0])
        pcmp = part([NG, E0])
        posf = [part([NG]) for _ in range(K0)]
        count = part([E0])
        tcmp = part([E0, NTH])
        tiles = part([E0])
        bcmp = part([E0, E0])
        first = part([E0])
        frow = part([E0])
        ecmp = part([NT, E0 - 1])
        etabf = part([NT])
        before = part([R])
        thr = part([NTH])
        below = part([E0, E0])
        tile_n = part([NT])
        pos = [sb(f"pos{k}", [128, NG], u32) for k in range(K0)]
        etab = sb("etab", [1, NT], i32)
        xtT = part([2, TS])
        cmp_at = taken[0]
        cmp0 = part([NG, E0 * 2 * E0])
        taken[0] = cmp_at
        xin = [part([D]) for _ in range(2)]
        hg = part([F0])
        hTt = part([FB0, TS])
        yt = [part([D]) for _ in range(2)]
        yg = [[part([D]) for _ in range(2)] for _ in range(K0)]
        w1_t = arena1[:, 0:E0 * 2 * F0].rearrange("p (e k f) -> p e k f", e=E0, k=2)
        sorted_x = nc.dram_tensor("sorted_x", (NT * TS, D), fp32).ap()
        sorted_y = nc.dram_tensor("sorted_y", (NT * TS, D), fp32).ap()
        assert NT % 2 == 1
        b2_t = sb("b2_t", [128, D])
        rtw_t = sb("rtw_t", [128, 2, E0])
        rtb_t = sb("rtb_t", [128, E0])
        gam_t = sb("gam_t", [128, D])
        bet_t = sb("bet_t", [128, D])
        tri0 = sb("tri0", [128, E0 * 2 * E0])
        lg = sb("lg", [128, NG, E0])
        rank0 = sb("rank0", [128, NG, E0])
        eq = [sb(f"eq{k}", [128, NG, E0]) for k in range(2)]
        eql = [sb(f"eql{k}", [128, NG, E0]) for k in range(2)]
        top = [sb(f"top{k}", [128, NG]) for k in range(2)]
        gap = sb("gap", [128, NG])
        egap = sb("egap", [128, NG])
        egap1 = sb("egap1", [128, NG])
        gw = [sb(f"gw{k}", [128, NG]) for k in range(2)]
        we = sb("we", [128, NG, E0])
        wes = slots("wes", [128, E0])
        weT = slots("weT", [128, R])
        y1 = slots("y1", [128, D])
        z1 = slots("z1", [128, D])
        z2 = slots("z2", [128, D])
        z3 = slots("z3", [128, D])
        y2 = z1

        taken[0] = 0
        qT = [part([MB1, PH]) for _ in range(2)]
        k1T = part([MB1, PH])
        v1 = [part([A1]) for _ in range(2)]
        sm = [part([H1, R]) for _ in range(2)]
        p1 = [part([H1, R]) for _ in range(2)]
        pt1 = sm
        cx = [part([A1]) for _ in range(2)]
        cT = [part([MB1, R]) for _ in range(2)]
        qscale = sb("qscale", [128, 2])
        w1qkv = arena1[:, 0:6 * A1].rearrange("p (k n) -> p k n", k=2)
        wo1_t = sb("wo1_t", [128, MB1, D])
        s_w4 = sem("s_w4")
        s_qs = sem("s_qs")
        s_qkp = [sem(f"s_qkp{n}") for n in range(MB1)]
        s_qk = [sem(f"s_qk{n}") for n in range(MB1)]
        s_sm = sem2("s_sm")
        s_pt1p = sem("s_pt1p")
        s_pt1 = sem("s_pt1")
        s_cTp = sem2("s_cTp")
        s_cT = sem2("s_cT")
        wg_t = arena1[:, 6 * A1:6 * A1 + 2 * EX * F1].rearrange("p (k n) -> p k n", k=2)
        wu_t = arena1[:, 6 * A1 + 2 * EX * F1:6 * A1 + 4 * EX * F1].rearrange("p (k n) -> p k n", k=2)
        taken[0] = 14736
        wd_t = part([EX, D])
        bd_t = sb("bd_t", [128, D])
        bg_t = sb("bg_t", [128, EX])
        bu_t = sb("bu_t", [128, EX])
        rt1w_t = sb("rt1w_t", [128, 2, E1])
        taken[0] = 0
        rt1b_t = sb("rt1b_t", [128, E1])
        corr_t = sb("corr_t", [128, E1])
        cmp1 = part([NG, 2 * E1 * E1])
        lg1 = part([NG, E1])
        sc1 = part([NG, E1])
        sfc = part([NG, E1])
        psum1 = part([NG * G1, 6])
        gtop = part([NG, G1])
        gcmp = part([NG, G1 * 2 * G1])
        grank = part([NG, G1])
        skept = part([NG, E1])
        tri1 = part([E1 * 2 * E1])
        trig = part([G1 * 2 * G1])
        taken[0] = 0
        hid = [part([PH]) for _ in range(3)]
        sg = [part([PH]) for _ in range(2)]
        acc5 = [part([D]) for _ in range(2)]
        o5 = [part([D]) for _ in range(2)]
        oh = [part([D]) for _ in range(2)]
        c1 = sb("c1", [128, NG, E1 + 1])
        wsum = sb("wsum", [128, NG])
        wsum1 = sb("wsum1", [128, NG])
        wrec = sb("wrec", [128, NG])
        cs = slots("cs", [128, E1 + 1])
        s_wgu = sem("s_wgu")
        s_w5 = sem("s_w5")
        s_c1 = sem("s_c1")
        s_r5 = sem("s_r5")
        s_sc = sem("s_sc")
        s_gp = sem("s_gp")
        s_sg = sem("s_sg")
        s_hid = sem("s_hid")
        s_dn = sem("s_dn")
        s_ac5 = sem("s_ac5")
        s_sh = sem("s_sh")
        s_o5 = sem("s_o5")
        s_oh = sem("s_oh")
        s_w3 = sem("s_w3")
        s_w1 = sem("s_w1")
        s_w2 = sem("s_w2")
        s_rows = sem("s_rows")
        s_z = sem("s_z")
        s_xz = sem("s_xz")
        s_chosen = sem("s_chosen")
        s_cntp = sem("s_cntp")
        s_pos = sem("s_pos")
        s_etab = sem("s_etab")
        s_scat = sem("s_scat")
        s_xin = sem2("s_xin")
        s_tTp = sem("s_tTp")
        s_tT = sem("s_tT")
        s_hp = sem("s_hp")
        s_hg = sem("s_hg")
        s_hTp = sem("s_hTp")
        s_hT = sem("s_hT")
        s_yp = sem("s_yp")
        s_yt = sem("s_yt")
        s_yst = sem2("s_yst")
        s_yg = sem2("s_yg")
        s_yadd = sem("s_yadd")
        s_lgp = sem("s_lgp")
        s_lg = sem("s_lg")
        s_rt = sem("s_rt")
        s_eg = sem("s_eg")
        s_wes = sem("s_wes")
        s_weTp = sem("s_weTp")
        s_weT = sem("s_weT")
        s_b2p = sem("s_b2p")
        s_y1 = sem("s_y1")
        s_y2 = sem("s_y2")
        s_z1 = sem("s_z1")
        s_z2 = sem("s_z2")
        s_z3 = sem("s_z3")
        s_w0 = sem("s_w0")
        s_sw = sem("s_sw")
        s_xn = sem2("s_xn")
        s_xTp = sem2("s_xTp")
        s_xT = sem2("s_xT")
        s_zp = sem("s_zp")
        s_zr = sem("s_zr")
        s_zc = sem("s_zc")
        s_rk = sem("s_rk")
        s_psel = sem("s_psel")
        s_ptp0 = sem("s_ptp0")
        s_pselT = sem("s_pselT")
        s_xsp = sem("s_xsp")
        s_xs = sem("s_xs")
        s_qp = sem("s_qp")
        s_qb = sem2("s_qb")
        s_kp = sem("s_kp")
        s_kT = sem("s_kT")
        s_vp = sem2("s_vp")
        s_v = sem2("s_v")
        s_sp = sem2("s_sp")
        s_mx = sem("s_mx")
        s_exp = sem2("s_exp")
        s_rd = sem("s_rd")
        s_pn = sem("s_pn")
        s_ptp = sem2("s_ptp")
        s_pt = sem2("s_pt")
        s_op = sem2("s_op")
        s_om = sem("s_om")
        s_ct = sem2("s_ct")
        s_ap = sem2("s_ap")
        s_at = sem("s_at")
        s_up = sem("s_up")
        s_ez = sem("s_ez")
        s_ez1 = sem("s_ez1")
        s_sig = sem("s_sig")
        s_y0 = sem("s_y0")

        s_const = sem("s_const")
        s_tokw = sem("s_tokw")
        s_ones = sem("s_ones")
        s_eps = sem("s_eps")
        s_weff = sem("s_weff")
        s_cnt = sem("s_cnt")
        s_bwrow_p = sem("s_bwrow_p")
        s_bwrow = sem("s_bwrow")
        s_bw_p = sem("s_bw_p")
        s_bw = sem("s_bw")
        s_x = sem2("s_x")
        s_xsq = sem2("s_xsq")
        s_emb = sem2("s_emb")
        s_raw = sem2("s_raw")
        s_mu = sem("s_mu")
        s_e1 = sem("s_e1")
        s_h = sem2("s_h")
        s_bn = sem2("s_bn")
        s_st = sem("s_st")
        s_sd = sem("s_sd")
        s_rstd = sem("s_rstd")
        s_out = sem("s_out")
        s_outs = sem2("s_outs")

        R5_END = 19
        POS_END = 13
        RT_GAP, RT_END = 11, 17

        block = ctx.enter_context(nc.Block())

        def grp(t, g, n=D):
            return t[0:R, :, :].rearrange("p g d -> p (g d)")[:, bass.ds(g * n, n)]

        def col(t, g):
            return t[0:R, bass.ds(g, 1)]

        def head_at(n):
            b, j = divmod(n, 3)
            return 2 * (b // 2 * 3 + j) + b % 2

        def row_stats(dve, time):
            st = 7 * (time - 1)
            a = st6[0:R, :, :]
            for s in range(2):
                dve.wait_ge(s_bn[s], NP * time)
            dve.tensor_tensor(mean[0:R, :], a[:, :, 1], a[:, :, 4], ALU.add).then_inc(s_st, 1)
            dve.tensor_tensor(dif[0:R, :], a[:, :, 1], a[:, :, 4], ALU.subtract).then_inc(s_st, 1)
            dve.tensor_tensor(var2[0:R, :], a[:, :, 2], a[:, :, 5], ALU.add).then_inc(s_st, 1)
            dve.wait_ge(s_st, st + 2)
            dve.scalar_tensor_tensor(dif2[0:R, :], dif[0:R, :], 0.25, dif[0:R, :], ALU.mult, ALU.mult).then_inc(s_st, 1)
            dve.tensor_scalar(mean[0:R, :], mean[0:R, :], 0.5, None, ALU.mult).then_inc(s_st, 1)
            dve.wait_ge(s_st, st + 4)
            dve.scalar_tensor_tensor(var[0:R, :], var2[0:R, :], 1.0 / D, dif2[0:R, :], ALU.mult, ALU.add).then_inc(s_st, 1)
            dve.wait_ge(s_sd, time + 1)
            dve.reciprocal(rstd[0:R, :], sdev[0:R, :]).then_inc(s_st, 1)
            dve.wait_ge(s_st, st + 7)

        def use_tables(act, func, n):
            act.activation(warm[0:1, n:n + 1], eps_t[0:1, :], func)

        def row_sdev(act, time):
            act.wait_ge(s_st, 7 * (time - 1) + 6)
            act.activation(sdev[0:R, :], var[0:R, :], ACT.Sqrt, bias=eps_t[0:R, :]).then_inc(s_sd, 1)

        @block.sync
        def _(sp):
            for t, d in ((ident[:, :], ident_c),):
                sp.dma_start(t, d).then_inc(s_const, 16)
            for t, d in ((arena1[0:KP, 0:A_W], tok_w), (tg[0:KP, :, :], tok_g), (tbe[0:KP, :, :], tok_be),
                         (tb_row[:, :], tok_b), (cnt[0:KP, :, :], tok_cnt)):
                sp.dma_start(t, d).then_inc(s_tokw, 16)
            for t, d in ((wqkv_t[0:HW, :, :], wqkv), (wo_t[0:HW, :, :], wo), (bqk_t[0:HW, :], bqk),
                         (bv_t[0:R, :], bv), (bo_t[0:R, :], bo), (selw_t[0:HW, :, :], sel_w),
                         (selb_t[0:R, :], sel_b), (temp_t[0:R, :], temp), (cmask[0:R, :], cmask_c),
                         (later[0:R, :], later_c), (earlier[0:R, :], earlier_c), (rtab[0:R, :], rtab_c),
                         (hmask[0:HW, :], hmask_c)):
                sp.dma_start(t, d).then_inc(s_w0, 16)
            with sp.Fori(0, NP) as i:
                for s in range(2):
                    sp.wait_ge(s_emb[s], i)
                    sp.wait_ge(s_xsq[s], i)
                    sp.dma_start(xp[s][0:KP, :, :].rearrange("p k r -> p (k r)"),
                                 x[bass.ds(2 * i + s, 1), :, :].rearrange("a p f -> p (a f)")).then_inc(s_x[s], 16)
            for t, d in ((rtw_t[0:HW, :, :], rt_w), (rtb_t[0:R, :], rt_b), (b2_t[0:E0, :], b2), (gam_t[0:R, :], gam),
                         (bet_t[0:R, :], bet), (tri0[0:R, :], tri0_c)):
                sp.dma_start(t, d).then_inc(s_w3, 16)
            for t, d in ((before[0:R, :], before_c), (thr[:, :], thr_c), (below[:, :, :], below_c),
                         (tile_n[0:1, :], tile_c)):
                sp.dma_start(t, d).then_inc(s_w3, 16)
            for s in range(2):
                sp.wait_ge(s_emb[s], NP)
            for e in range(E0):
                sp.dma_start(w1_t[0:HW, e, :, :], w1[e]).then_inc(s_w1, 16)
                sp.dma_start(w2_t[:, e, :, :], w2[e]).then_inc(s_w2, 16)
            sp.dma_start(w1_t[HW:HW + 1, :, 1, :], b1).then_inc(s_w1, 16)
            sp.wait_ge(s_z, 1)
            sp.dma_start(sorted_x.rearrange("(t p) d -> p t d", p=TS), zero[:, :].unsqueeze(1).broadcast_to([TS, NT, D])
                         ).then_inc(s_xz, 16)
            sp.wait_ge(s_scat, 16 * K0 * NG)

            def load_tile(t, s):
                sp.dma_start(xin[s][:, :], sorted_x[bass.ds(t * TS, TS), :]).then_inc(s_xin[s], 16)

            def store_tile(t, s):
                sp.wait_ge(s_yt, t + 1)
                sp.dma_start(sorted_y[bass.ds(t * TS, TS), :], yt[s][:, :]).then_inc(s_yst[s], 16)

            for t in range(2):
                load_tile(t, t)
            with sp.Fori(0, NT // 2 - 1) as i:
                for s in range(2):
                    sp.wait_ge(s_tTp, 2 * i + s + 1)
                    load_tile(2 * i + s + 2, s)
                    store_tile(2 * i + s, s)
            sp.wait_ge(s_tTp, NT - 2)
            load_tile(NT - 1, 0)
            for t in range(NT - 3, NT):
                store_tile(t, t % 2)
            sp.wait_ge(s_hp, NT)
            for t, d in ((w1qkv[0:HW, :, :], wqkv1), (wo1_t[:, :, :], wo1), (bmask[0:R, :], bmask_c)):
                sp.dma_start(t, d).then_inc(s_w4, 16)
            sp.dma_start(wg_t[0:HW, :, :], w_gate).then_inc(s_wgu, 16)
            sp.dma_start(wu_t[0:HW, :, :], w_up).then_inc(s_wgu, 16)
            for s in range(2):
                sp.wait_ge(s_h[s], 3 * NP)
            for t, d in ((wd_t[0:F1, :, :], w_down), (bd_t[0:E1, :], b_down), (bd_t[E1:E1 + 1, :], sb_down),
                         (bg_t[0:F1, :], b_gate), (bu_t[0:F1, :], b_up), (rt1w_t[0:HW, :, :], rt1_w),
                         (rt1b_t[0:R, :], rt1_b), (corr_t[0:R, :], corr)):
                sp.dma_start(t, d).then_inc(s_w5, 16)
            for s in range(2):
                sp.wait_ge(s_h[s], 4 * NP)
            sp.dma_start(tri1[0:R, :], tri1_c).then_inc(s_w5, 16)
            sp.dma_start(trig[0:R, :], trig_c).then_inc(s_w5, 16)
            with sp.Fori(0, NP) as i:
                for s in range(2):
                    sp.wait_ge(s_oh, 2 * i + s + 1)
                    sp.dma_start(out[bass.ds(2 * i + s, 1)].rearrange("a r d -> (a r) d"), oh[s][0:R, :]
                                 ).then_inc(s_outs[s], 16)
            for s in range(2):
                sp.wait_ge(s_outs[s], 16 * NP)
        @block.gpsimd
        def _(pool):
            pool.memset(ones[:, :], 1.0).then_inc(s_ones, 1)
            pool.memset(eps_t[:, :], EPS).then_inc(s_eps, 1)
            pool.memset(zero[:, :], 0.0).then_inc(s_z, 1)
            pool.wait_ge(s_z, 1)
            pool.memset(xtT[HW:HW + 1, 1, :], 1.0).then_inc(s_z, 1)
            pool.wait_ge(s_z, 2)
            pool.wait_ge(s_tokw, 5 * 16)
            pool.tensor_copy(weff[0:KP, :, D:D + 1], cnt[0:KP, :, :]).then_inc(s_cnt, 1)
            with pool.Fori(0, NP) as i:
                for s in range(2):
                    pool.wait_ge(s_ones, 1)
                    pool.wait_ge(s_xn[s], i + 1 + NP)
                    pool.tensor_copy(grp(acc, 2 * i + s), xn[s][0:R, :]).then_inc(s_rows, 1)
            pool.wait_ge(s_rows, 2 * NP)
            pool.wait_ge(s_xz, 16)
            pool.wait_ge(s_pos, POS_END)
            for g in range(NG):
                for k in range(K0):
                    pool.indirect_dma_start(sorted_x, bass.IndirectOffsetOnAxis(pos[k][0:R, g:g + 1], 0),
                                            acc[0:R, g, :], None).then_inc(s_scat, 16)
            pool.wait_ge(s_rt, RT_END)
            for s in range(2):
                pool.wait_ge(s_yst[s], 16 * (NT // 2 + 1 - s))
            for g in range(NG):
                s = g % 2
                if g >= 2:
                    pool.wait_ge(s_weTp, g - 1)
                pool.tensor_copy(wes[s][0:R, :], we[0:R, g, :]).then_inc(s_wes, 1)
                if g >= 2:
                    pool.wait_ge(s_y2, g - 1)
                for k in range(K0):
                    pool.indirect_dma_start(yg[k][s][0:R, :], None, sorted_y,
                                            bass.IndirectOffsetOnAxis(pos[k][0:R, g:g + 1], 0)).then_inc(s_yg[s], 16)
            pool.memset(c1[0:R, :, :], 1.0).then_inc(s_c1, 1)
            with pool.Fori(0, NP) as i:
                for s in range(2):
                    pool.wait_ge(s_ones, 1)
                    pool.wait_ge(s_r5, R5_END)
                    pool.wait_ge(s_ac5, E1 * 2 * i)
                    pool.wait_ge(s_weTp, 2 * i + 2 * NP)
                    pool.tensor_copy(cs[s][0:R, :], grp(c1, 2 * i + s, E1 + 1)).then_inc(s_wes, 1)

        @block.scalar
        def _(act):
            act.wait_ge(s_eps, 1)
            use_tables(act, ACT.Square, 0)
            with act.Fori(0, NP) as i:
                for s in range(2):
                    act.wait_ge(s_x[s], 16 * i + 16)
                    act.wait_ge(s_emb[s], i)
                    act.activation(xsq[s][0:KP, :, :], xp[s][0:KP, :, :], ACT.Square).then_inc(s_xsq[s], 1)
            act.wait_ge(s_eps, 1)
            act.wait_ge(s_mu, 3)
            act.activation(sdev[0:R, :], var[0:R, :], ACT.Sqrt, bias=eps_t[0:R, :]).then_inc(s_sd, 1)
            row_sdev(act, 1)

            use_tables(act, ACT.Exp, 1)
            act.wait_ge(s_w0, 13 * 16)
            with act.Fori(0, NP) as i:
                for s in range(2):
                    act.wait_ge(s_xTp[s], i + 1)
                    act.wait_ge(s_vp[s], i)
                    act.copy(xT[0:HW, :, s * R:(s + 1) * R],
                             bank[4 * s][0:HW, 0:PH].rearrange("p (k r) -> p k r", k=2)).then_inc(s_xT[s], 1)
                act.wait_ge(s_kp, i + 1)
                for s in range(2):
                    act.wait_ge(s_sp[s], i)
                for hh in range(2):
                    act.activation(kT[0:HW, hh, :], bank[0][0:HW, hh * PH:(hh + 1) * PH], ACT.Identity,
                                   bias=bqk_t[0:HW, 2 + hh:3 + hh]).then_inc(s_kT, 1)
                for s in range(2):
                    act.wait_ge(s_zc, 2 * i + s + 1)
                    act.wait_ge(s_ez1, 2 * i)
                    act.activation(ez[s][0:R, :], zc[s][0:R, :], ACT.Exp, scale=-1.0).then_inc(s_ez, 1)
                for s in range(2):
                    act.wait_ge(s_ptp0, 2 * i + s + 1)
                    act.wait_ge(s_up, 2 * i)
                    act.copy(pselT[s][0:QG, :], bank[4 * s + 3][0:QG, 0:R]).then_inc(s_pselT, 1)
                for s in range(2):
                    act.wait_ge(s_mx, 2 * i + s + 1)
                    act.wait_ge(s_pn, 2 * i)
                    for hh in range(2):
                        ex = act.activation(p0[s][0:R, hh, :], bank[4 * s + 2][0:R, D + hh * R:D + (hh + 1) * R], ACT.Exp,
                                            bias=nmx[s][0:R, hh:hh + 1], accum_out=den[s][0:R, hh:hh + 1])
                    ex.then_inc(s_exp[s], 1)
                for s in range(2):
                    act.wait_ge(s_ptp[s], i + 1)
                    act.wait_ge(s_op[s], i)
                    act.copy(pt0[s][0:R, :, :], bank[4 * s + 3][0:R, 0:PH].rearrange("p (k r) -> p k r", k=2)
                             ).then_inc(s_pt[s], 1)
            row_sdev(act, 2)

            with act.Fori(0, NP) as i:
                for s in range(2):
                    act.wait_ge(s_xTp[s], i + 1 + NP)
                    act.wait_ge(s_lgp, 2 * i)
                    act.copy(xT[0:HW, :, s * R:(s + 1) * R],
                             bank[4 * s][0:HW, 0:PH].rearrange("p (k r) -> p k r", k=2)).then_inc(s_xT[s], 1)
            act.wait_ge(s_rt, RT_GAP)
            act.activation(egap[0:R, :], gap[0:R, :], ACT.Exp).then_inc(s_eg, 1)
            use_tables(act, ACT.Gelu, 2)

            def gelu(t):
                act.wait_ge(s_hp, t + 1)
                act.activation(hg[:, :].rearrange("p (b f) -> p b f", b=2), ps[:, 1:3, 0:F0 // 2], ACT.Gelu).then_inc(s_hg, 1)

            gelu(0)
            with act.Fori(1, NT) as t:
                gelu(t)
            with act.Fori(0, NP) as i:
                for s in range(2):
                    act.wait_ge(s_weTp, 2 * i + s + 1)
                    act.wait_ge(s_b2p, 2 * i)
                    act.copy(weT[s][0:E0, :], bank[4 * s][0:E0, 0:R]).then_inc(s_weT, 1)
            row_sdev(act, 3)
            row_sdev(act, 4)

            act.wait_ge(s_w4, 3 * 16)
            act.wait_ge(s_qs, 4)
            use_tables(act, ACT.Exp, 3)

            def front1(i):
                for s in range(2):
                    act.wait_ge(s_xTp[1], i + 1 + 2 * NP)
                    act.copy(xT[0:HW, :, s * R:(s + 1) * R],
                             bank[4][0:HW, s * PH:(s + 1) * PH].rearrange("p (k r) -> p k r", k=2)).then_inc(s_xT[s], 1)
                for n in range(3):
                    act.wait_ge(s_qkp[n], i + 1)
                    for c in range(2):
                        q = act.activation(qT[c][:, 2 * n:2 * n + 2, :],
                                           bank[5 + n][:, 0:2 * PH].rearrange("p (m r) -> p m r", m=2),
                                           ACT.Copy, scale=qscale[:, c:c + 1])
                    q.then_inc(s_qk[n], 1)

            def attend1(i, more):
                for s in range(2):
                    act.wait_ge(s_vp[s], i + 1 + NP)
                    act.copy(v1[s][0:R, :].rearrange("p (b f) -> p b f", b=2), ps[0:R, 5:7, 0:A1 // 2]).then_inc(s_v[s], 1)
                for s in range(2):
                    if s == 1 and more:
                        front1(i + 1)
                    act.wait_ge(s_mx, 2 * i + s + 1 + 2 * NP)
                    for n in range(H1):
                        ex = act.activation(p1[s][0:R, head_at(n), :], sm[s][0:R, n, :], ACT.Exp, bias=nmx[s][0:R, n:n + 1],
                                            accum_out=den[s][0:R, head_at(n):head_at(n) + 1])
                    ex.then_inc(s_exp[s], 1)
                for s in range(2):
                    act.wait_ge(s_cTp[s], i + 1)
                    act.copy(cT[s].rearrange("p (b m) r -> p b (m r)", b=2), ps[:, 2:4, 0:3 * R]).then_inc(s_cT[s], 1)

            front1(0)
            with act.Fori(0, NP - 1) as i:
                attend1(i, True)
            attend1(NP - 1, False)
            row_sdev(act, 5)

            with act.Fori(0, NP) as i:
                for s in range(2):
                    act.wait_ge(s_xTp[1], i + 1 + 3 * NP)
                    act.wait_ge(s_lgp, 2 * i + 2 * NP)
                    act.copy(xT[0:HW, :, s * R:(s + 1) * R],
                             bank[4][0:HW, s * PH:(s + 1) * PH].rearrange("p (k r) -> p k r", k=2)).then_inc(s_xT[s], 1)
            for s in range(2):
                act.wait_ge(s_lg, 4 * NP)
            act.activation(sc1[0:R, :, :], lg1[0:R, :, :], ACT.Sigmoid).then_inc(s_sc, 1)
            use_tables(act, ACT.Silu, 4)
            act.wait_ge(s_w5, 10 * 16)
            with act.Fori(0, NP) as i:
                for s in range(2):
                    act.wait_ge(s_xTp[1], i + 1 + 4 * NP)
                    act.wait_ge(s_gp, EX * i)
                    act.copy(xT[0:HW, :, s * R:(s + 1) * R],
                             bank[7][0:HW, s * PH:(s + 1) * PH].rearrange("p (k r) -> p k r", k=2)).then_inc(s_xT[s], 1)
                for s in range(2):
                    act.wait_ge(s_weTp, 2 * i + 2 + 2 * NP)
                    act.wait_ge(s_sh, i)
                    act.copy(weT[s][0:E1 + 1, :], bank[7][0:E1 + 1, s * R:(s + 1) * R]).then_inc(s_weT, 1)
                for e in range(EX):
                    act.wait_ge(s_gp, EX * i + e + 1)
                    act.wait_ge(s_hid, EX * i + max(e - 1, 0))
                    act.activation(sg[e % 2][0:F1, :], bank[e % 2][0:F1, 0:PH], ACT.Silu, bias=bg_t[0:F1, e:e + 1]
                                   ).then_inc(s_sg, 1)

        @block.vector
        def _(dve):
            dve.wait_ge(s_tokw, 5 * 16)
            for k in range(KB):
                dve.tensor_scalar(weff[0:KP, k, 0:D], tw[0:KP, k, 0, :], tg[0:KP, k, 0:1], None,
                                  ALU.mult).then_inc(s_weff, 1)
            for j in range(1, NS):
                for k in range(KB):
                    dve.wait_ge(s_weff, KB * (j - 1) + k + 1)
                    dve.scalar_tensor_tensor(weff[0:KP, k, 0:D], tw[0:KP, k, j, :], tg[0:KP, k, j:j + 1],
                                             weff[0:KP, k, 0:D], ALU.mult, ALU.add).then_inc(s_weff, 1)
            dve.wait_ge(s_bwrow_p, 1)
            dve.tensor_copy(bw_row[:, :], bank[0][0:1, 0:D]).then_inc(s_bwrow, 1)
            dve.wait_ge(s_bw_p, 1)
            dve.tensor_copy(csum[0:R, :], bank[1][0:R, 0:D]).then_inc(s_bw, 1)
            dve.tensor_copy(bw[0:R, :], bank[1][0:R, D:2 * D]).then_inc(s_bw, 1)
            with dve.Fori(0, NP) as i:
                for s in range(2):
                    dve.wait_ge(s_emb[s], i + 1)
                    dve.tensor_copy(grp(h, 2 * i + s), bank[2 + s][0:R, 0:D])
                    dve.tensor_copy(grp(sums, 2 * i + s, 2), bank[2 + s][0:R, D:D + 2]).then_inc(s_raw[s], 1)
            for s in range(2):
                dve.wait_ge(s_raw[s], NP)
            dve.tensor_scalar(mu[0:R, :], sums[0:R, :, 0], 1.0 / FULL, None, ALU.mult).then_inc(s_mu, 1)
            dve.wait_ge(s_mu, 1)
            dve.scalar_tensor_tensor(m2[0:R, :], mu[0:R, :], -1.0, mu[0:R, :], ALU.mult, ALU.mult).then_inc(s_mu, 1)
            dve.tensor_scalar(nmu[0:R, :], mu[0:R, :], -1.0, None, ALU.mult)
            dve.wait_ge(s_mu, 2)
            dve.scalar_tensor_tensor(var[0:R, :], sums[0:R, :, 1], 1.0 / FULL, m2[0:R, :], ALU.mult,
                                     ALU.add).then_inc(s_mu, 1)
            dve.wait_ge(s_sd, 1)
            dve.reciprocal(rstd[0:R, :], sdev[0:R, :]).then_inc(s_rstd, 1)
            dve.wait_ge(s_rstd, 1)
            dve.wait_ge(s_bw, 2)
            with dve.Fori(0, NP) as i:
                for s in range(2):
                    dve.scalar_tensor_tensor(tmp[s][0:R, :], csum[0:R, :], col(nmu, 2 * i + s), grp(h, 2 * i + s),
                                             ALU.mult, ALU.add).then_inc(s_e1, 1)
                for s in range(2):
                    dve.wait_ge(s_e1, 2 * i + s + 1)
                    dve.scalar_tensor_tensor(grp(h, 2 * i + s), tmp[s][0:R, :], col(rstd, 2 * i + s), bw[0:R, :],
                                             ALU.mult, ALU.add).then_inc(s_h[s], 1)
                for s in range(2):
                    dve.wait_ge(s_bw, 2)
                    dve.wait_ge(s_h[s], i + 1)
                    dve.bn_stats(grp(st6, 2 * i + s, 6), grp(h, 2 * i + s)).then_inc(s_bn[s], 1)
            row_stats(dve, 1)

            dve.wait_ge(s_w0, 13 * 16)
            dve.reciprocal(itemp[0:R, :], temp_t[0:R, :]).then_inc(s_sw, 1)
            dve.tensor_tensor(dselb[0:R, :], selb_t[0:R, 1:2], selb_t[0:R, 0:1], ALU.subtract).then_inc(s_sw, 1)
            dve.tensor_tensor(dselw[0:HW, :, :], selw_t[0:HW, :, 1:2], selw_t[0:HW, :, 0:1], ALU.subtract).then_inc(s_sw, 1)
            dve.tensor_scalar(hmaskq[0:HW, :], hmask[0:HW, :], float(D0) ** -0.5, None, ALU.mult)
            dve.wait_ge(s_sw, 3)
            dve.tensor_scalar(bz[0:R, :], dselb[0:R, :], itemp[0:R, :], None, ALU.mult).then_inc(s_sw, 1)
            dve.tensor_scalar(wz[0:HW, :, :], dselw[0:HW, :, :].broadcast_to([HW, 2, R]), itemp[0:HW, :], None,
                              ALU.mult).then_inc(s_sw, 1)
            dve.wait_ge(s_sw, 5)
            with dve.Fori(0, NP) as i:
                for s in range(2):
                    dve.wait_ge(s_xsp, 2 * i)
                    dve.tensor_scalar(xn[s][0:R, :], grp(h, 2 * i + s), col(mean, 2 * i + s), col(rstd, 2 * i + s),
                                      ALU.subtract, ALU.mult).then_inc(s_xn[s], 1)
                for s in range(2):
                    dve.wait_ge(s_zp, 2 * i + s + 1)
                    dve.tensor_scalar(zr[s][0:R, :], bank[4 * s + 1][0:R, 0:R], bz[0:R, :], None,
                                      ALU.add).then_inc(s_zr, 1)
                for s in range(2):
                    dve.wait_ge(s_zr, 2 * i + s + 1)
                    dve.wait_ge(s_ez, 2 * i)
                    dve.scalar_tensor_tensor(junk[s][0:R, 0, :], zr[s][0:R, :], 1.0, ident[0:R, 0:R], ALU.mult, ALU.mult,
                                             accum_out=zc[s][0:R, :]).then_inc(s_zc, 1)
                for s in range(2):
                    dve.wait_ge(s_zc, 2 * i + s + 1)
                    dve.scalar_tensor_tensor(junk[s][0:R, 1, :], zr[s][0:R, :], zc[s][0:R, :], later[0:R, :], ALU.is_gt,
                                             ALU.mult, accum_out=rka[s][0:R, :]).then_inc(s_rk, 1)
                    dve.scalar_tensor_tensor(junk[s][0:R, 2, :], zr[s][0:R, :], zc[s][0:R, :], earlier[0:R, :], ALU.is_ge,
                                             ALU.mult, accum_out=rkb[s][0:R, :]).then_inc(s_rk, 1)
                for s in range(2):
                    dve.wait_ge(s_rk, 4 * i + 2 * s + 2)
                    dve.wait_ge(s_sp[s], i)
                    dve.tensor_scalar(psel[s][0:R, :], rtab[0:R, :], rka[s][0:R, :], rkb[s][0:R, :], ALU.subtract,
                                      ALU.is_equal).then_inc(s_psel, 1)
                for s in range(2):
                    dve.wait_ge(s_vp[s], i + 1)
                    dve.tensor_tensor(v0[s][0:R, :], bank[4 * s + 2][0:R, 0:D], bv_t[0:R, :], ALU.add).then_inc(s_v[s], 1)
                for s in range(2):
                    dve.wait_ge(s_xsp, 2 * i + s + 1)
                    dve.tensor_copy(xs[s][0:HW, :, :], bank[4 * s + 1][0:HW, R:R + 2 * QG].rearrange("p (k q) -> p k q", k=2)
                                    ).then_inc(s_xs, 1)
                for s in range(2):
                    dve.wait_ge(s_qp, 2 * i + s + 1)
                    for hh in range(2):
                        q = bank[4 * s + 1][0:HW, 256 + hh * QG:256 + (hh + 1) * QG]
                        dve.scalar_tensor_tensor(qb[s][0:HW, hh, :].rearrange("p (j q) -> p j q", j=HH),
                                                 q.unsqueeze(1).broadcast_to([HW, HH, QG]), bqk_t[0:HW, hh:hh + 1],
                                                 hmaskq[0:HW, :].rearrange("p (j q) -> p j q", j=HH),
                                                 ALU.add, ALU.mult).then_inc(s_qb[s], 1)
                for s in range(2):
                    dve.wait_ge(s_sp[s], i + 1)
                    dve.tensor_reduce(nmx[s][0:R, 0:2], bank[4 * s + 2][0:R, D:D + PH].rearrange("p (k r) -> p k r", k=2),
                                      AX, ALU.max, negate=True).then_inc(s_mx, 1)
                for s in range(2):
                    dve.wait_ge(s_ez, 2 * i + s + 1)
                    dve.tensor_scalar(ez1[s][0:R, :], ez[s][0:R, :], 1.0, None, ALU.add).then_inc(s_ez1, 1)
                for s in range(2):
                    dve.wait_ge(s_ez1, 2 * i + s + 1)
                    dve.reciprocal(sig[s][0:R, :], ez1[s][0:R, :]).then_inc(s_sig, 1)
                for s in range(2):
                    dve.wait_ge(s_exp[s], i + 1)
                    dve.reciprocal(rden[s][0:R, 0:2], den[s][0:R, 0:2]).then_inc(s_rd, 1)
                for s in range(2):
                    dve.wait_ge(s_rd, 2 * i + s + 1)
                    dve.wait_ge(s_ptp[s], i)
                    dve.tensor_tensor(pn[s][0:R, :, :], p0[s][0:R, :, :],
                                      rden[s][0:R, 0:2].unsqueeze(2).broadcast_to([R, 2, R]), ALU.mult).then_inc(s_pn, 1)
                for s in range(2):
                    dve.wait_ge(s_op[s], i + 1)
                    dve.tensor_tensor(om[s][0:HW, :, :], bank[4 * s + 3][0:HW, 0:PH].rearrange("p (k r) -> p k r", k=2),
                                      hmask[0:HW, :].unsqueeze(1).broadcast_to([HW, 2, R]), ALU.mult).then_inc(s_om, 1)
                for s in range(2):
                    dve.wait_ge(s_om, 2 * i + s + 1)
                    dve.tensor_reduce(ct0[s][0:HW, :, :], om[s][0:HW, :, :].rearrange("p k (j q) -> p k q j", j=HH), AX,
                                      ALU.add).then_inc(s_ct[s], 1)
                for s in range(2):
                    dve.wait_ge(s_ap[s], i + 1)
                    dve.tensor_tensor(at0[s][0:QG, :], bank[4 * s + 3][0:QG, 0:D], bo_t[0:QG, :], ALU.add).then_inc(s_at, 1)
                for s in range(2):
                    dve.wait_ge(s_sig, 2 * i + s + 1)
                    dve.wait_ge(s_up, 2 * i + s + 1)
                    dve.scalar_tensor_tensor(y0[s][0:R, :], bank[4 * s + 3][0:R, D:2 * D], sig[s][0:R, :], xn[s][0:R, :],
                                             ALU.mult, ALU.add).then_inc(s_y0, 1)
                for s in range(2):
                    dve.wait_ge(s_y0, 2 * i + s + 1)
                    dve.tensor_tensor(grp(h, 2 * i + s), grp(h, 2 * i + s), y0[s][0:R, :], ALU.add).then_inc(s_h[s], 1)
                for s in range(2):
                    dve.wait_ge(s_bw, 2)
                    dve.wait_ge(s_h[s], i + 1 + NP)
                    dve.bn_stats(grp(st6, 2 * i + s, 6), grp(h, 2 * i + s)).then_inc(s_bn[s], 1)
            row_stats(dve, 2)

            dve.wait_ge(s_w3, 10 * 16)
            with dve.Fori(0, NP) as i:
                for s in range(2):
                    dve.wait_ge(s_xTp[s], i + NP)
                    dve.wait_ge(s_rows, 2 * i)
                    dve.tensor_scalar(xn[s][0:R, :], grp(h, 2 * i + s), col(mean, 2 * i + s), col(rstd, 2 * i + s),
                                      ALU.subtract, ALU.mult).then_inc(s_xn[s], 1)
                for s in range(2):
                    dve.wait_ge(s_lgp, 2 * i + s + 1)
                    dve.tensor_tensor(grp(lg, 2 * i + s, E0), bank[4 * s + 1][0:R, 0:E0], rtb_t[0:R, :],
                                      ALU.add).then_inc(s_lg, 1)
            for s in range(2):
                dve.wait_ge(s_lg, 2 * NP)
            c4 = cmp0[0:R, :, :].rearrange("p g (e w j) -> p g e w j", e=E0, w=2)
            one = lg[0:R, :, :].unsqueeze(3).broadcast_to([R, NG, E0, E0])
            other = lg[0:R, :, :].unsqueeze(2).broadcast_to([R, NG, E0, E0])
            dve.tensor_tensor(c4[:, :, :, 0, :], other, one, ALU.is_gt).then_inc(s_rt, 1)
            dve.tensor_tensor(c4[:, :, :, 1, :], other, one, ALU.is_ge).then_inc(s_rt, 1)
            dve.wait_ge(s_rt, 2)
            dve.tensor_tensor(cmp0[0:R, :, :], cmp0[0:R, :, :],
                              tri0[0:R, :].unsqueeze(1).broadcast_to([R, NG, E0 * 2 * E0]), ALU.mult).then_inc(s_rt, 1)
            dve.wait_ge(s_rt, 3)
            dve.tensor_reduce(rank0[0:R, :, :], cmp0[0:R, :, :].rearrange("p g (e w) -> p g e w", e=E0), AX,
                              ALU.add).then_inc(s_rt, 1)
            dve.wait_ge(s_rt, 4)
            for k in range(2):
                dve.tensor_scalar(eq[k][0:R, :, :], rank0[0:R, :, :], float(k), None, ALU.is_equal).then_inc(s_rt, 1)
            dve.wait_ge(s_rt, 6)
            dve.tensor_tensor(chosen[0:R, :, :], eq[0][0:R, :, :], eq[1][0:R, :, :], ALU.add).then_inc(s_chosen, 1)
            for k in range(2):
                dve.tensor_tensor(eql[k][0:R, :, :], eq[k][0:R, :, :], lg[0:R, :, :], ALU.mult).then_inc(s_rt, 1)
            dve.wait_ge(s_rt, 8)
            for k in range(2):
                dve.tensor_reduce(top[k][0:R, :], eql[k][0:R, :, :], AX, ALU.add).then_inc(s_rt, 1)
            dve.wait_ge(s_rt, 10)
            dve.tensor_tensor(gap[0:R, :], top[1][0:R, :], top[0][0:R, :], ALU.subtract).then_inc(s_rt, 1)
            dve.wait_ge(s_eg, 1)
            dve.tensor_scalar(egap1[0:R, :], egap[0:R, :], 1.0, None, ALU.add).then_inc(s_rt, 1)
            dve.wait_ge(s_rt, 12)
            dve.reciprocal(gw[0][0:R, :], egap1[0:R, :]).then_inc(s_rt, 1)
            dve.wait_ge(s_rt, 13)
            dve.tensor_tensor(gw[1][0:R, :], egap[0:R, :], gw[0][0:R, :], ALU.mult).then_inc(s_rt, 1)
            dve.wait_ge(s_rt, 14)
            for k in range(2):
                dve.tensor_tensor(eql[k][0:R, :, :], eq[k][0:R, :, :],
                                  gw[k][0:R, :].unsqueeze(2).broadcast_to([R, NG, E0]), ALU.mult).then_inc(s_rt, 1)
            dve.wait_ge(s_rt, 16)
            dve.tensor_tensor(we[0:R, :, :], eql[0][0:R, :, :], eql[1][0:R, :, :], ALU.add).then_inc(s_rt, 1)
            dve.wait_ge(s_rt, RT_END)
            dve.wait_ge(s_cntp, 2)
            dve.tensor_reduce(count[:, :], bank[1][:, 0:NG * E0].rearrange("p (g e) -> p e g", g=NG), AX, ALU.add
                              ).then_inc(s_pos, 1)
            dve.wait_ge(s_pos, 1)
            dve.tensor_tensor(tcmp[:, :, :], count[:, :].unsqueeze(2).broadcast_to([TS, E0, NTH]),
                              thr[:, :].unsqueeze(1).broadcast_to([TS, E0, NTH]), ALU.is_gt).then_inc(s_pos, 1)
            dve.wait_ge(s_pos, 2)
            dve.tensor_reduce(tiles[:, :], tcmp[:, :, :], AX, ALU.add).then_inc(s_pos, 1)
            dve.wait_ge(s_pos, 3)
            dve.tensor_tensor(bcmp[:, :, :], tiles[:, :].unsqueeze(1).broadcast_to([TS, E0, E0]), below[:, :, :], ALU.mult
                              ).then_inc(s_pos, 1)
            dve.wait_ge(s_pos, 4)
            dve.tensor_reduce(first[:, :], bcmp[:, :, :], AX, ALU.add).then_inc(s_pos, 1)
            dve.wait_ge(s_pos, 5)
            dve.tensor_scalar(frow[:, :], first[:, :], float(TS), None, ALU.mult).then_inc(s_pos, 1)
            dve.wait_ge(s_pos, 6)
            dve.tensor_tensor(place[0:R, :, :], bank[0][0:R, 0:NG * E0].rearrange("p (g e) -> p g e", g=NG),
                              frow[0:R, :].unsqueeze(1).broadcast_to([R, NG, E0]), ALU.add).then_inc(s_pos, 1)
            for k in range(K0):
                dve.wait_ge(s_pos, 7 + 3 * k)
                dve.tensor_tensor(pcmp[0:R, :, :], place[0:R, :, :], eq[k][0:R, :, :], ALU.mult).then_inc(s_pos, 1)
                dve.wait_ge(s_pos, 8 + 3 * k)
                dve.tensor_reduce(posf[k][0:R, :], pcmp[0:R, :, :], AX, ALU.add).then_inc(s_pos, 1)
                dve.wait_ge(s_pos, 9 + 3 * k)
                dve.tensor_copy(pos[k][0:R, :], posf[k][0:R, :]).then_inc(s_pos, 1)
            dve.tensor_tensor(ecmp[0:1, :, :], first[0:1, 1:E0].unsqueeze(1).broadcast_to([1, NT, E0 - 1]),
                              tile_n[0:1, :].unsqueeze(2).broadcast_to([1, NT, E0 - 1]), ALU.is_le).then_inc(s_etab, 1)
            dve.wait_ge(s_etab, 1)
            dve.tensor_reduce(etabf[0:1, :], ecmp[0:1, :, :], AX, ALU.add).then_inc(s_etab, 1)
            dve.wait_ge(s_etab, 2)
            dve.tensor_copy(etab[0:1, :], etabf[0:1, :]).then_inc(s_etab, 1)

            def tile_x(t):
                dve.wait_ge(s_tTp, t + 1)
                dve.tensor_copy(xtT[0:HW, :, :], bank[0][0:HW, 0:2 * TS].rearrange("p (k r) -> p k r", k=2)).then_inc(s_tT, 1)

            def tile_h(t):
                dve.wait_ge(s_hTp, t + 1)
                dve.tensor_copy(hTt.rearrange("p (b m) r -> p b (m r)", b=2), ps[:, 3:5, 0:3 * TS]).then_inc(s_hT, 1)

            def tile_y(t, s, stores):
                dve.wait_ge(s_yp, t + 1)
                if stores is not None:
                    dve.wait_ge(s_yst[s], 16 * stores)
                dve.tensor_copy(yt[s][:, :], bank[5][:, 0:D]).then_inc(s_yt, 1)

            tile_x(0)
            tile_x(1)
            for t in range(2):
                tile_h(t)
                tile_y(t, t, None)
                tile_x(t + 2)
            with dve.Fori(1, NT // 2 - 1) as i:
                for s in range(2):
                    tile_h(2 * i + s)
                    tile_y(2 * i + s, s, i)
                    tile_x(2 * i + s + 2)
            tile_h(NT - 3)
            tile_y(NT - 3, 0, (NT - 3) // 2)
            tile_x(NT - 1)
            for t in (NT - 2, NT - 1):
                tile_h(t)
                tile_y(t, t % 2, t // 2)

            dve.wait_ge(s_rows, 2 * NP)
            with dve.Fori(0, NP) as i:
                for s in range(2):
                    dve.wait_ge(s_b2p, 2 * i + s + 1)
                    dve.tensor_tensor(y1[s][0:R, :], bank[4 * s + 1][0:R, 0:D], grp(acc, 2 * i + s), ALU.add).then_inc(s_y1, 1)
                for s in range(2):
                    dve.wait_ge(s_y1, 2 * i + s + 1)
                    dve.wait_ge(s_yg[s], 16 * K0 * i + 16 * K0)
                    dve.scalar_tensor_tensor(y2[s][0:R, :], yg[0][s][0:R, :], col(gw[0], 2 * i + s), y1[s][0:R, :],
                                             ALU.mult, ALU.add).then_inc(s_yadd, 1)
                for s in range(2):
                    dve.wait_ge(s_yadd, 2 * i + s + 1)
                    dve.scalar_tensor_tensor(grp(acc, 2 * i + s), yg[1][s][0:R, :], col(gw[1], 2 * i + s), y2[s][0:R, :],
                                             ALU.mult, ALU.add).then_inc(s_y2, 1)
                for s in range(2):
                    dve.wait_ge(s_bw, 2)
                    dve.wait_ge(s_y2, 2 * i + s + 1)
                    dve.bn_stats(grp(st6, 2 * i + s, 6), grp(acc, 2 * i + s)).then_inc(s_bn[s], 1)
            row_stats(dve, 3)
            with dve.Fori(0, NP) as i:
                for s in range(2):
                    dve.wait_ge(s_z2, 2 * i)
                    dve.tensor_scalar(z1[s][0:R, :], grp(acc, 2 * i + s), col(mean, 2 * i + s), col(rstd, 2 * i + s),
                                      ALU.subtract, ALU.mult).then_inc(s_z1, 1)
                for s in range(2):
                    dve.wait_ge(s_z1, 2 * i + s + 1)
                    dve.tensor_tensor(z2[s][0:R, :], z1[s][0:R, :], gam_t[0:R, :], ALU.mult).then_inc(s_z2, 1)
                for s in range(2):
                    dve.wait_ge(s_z2, 2 * i + s + 1)
                    dve.tensor_tensor(z3[s][0:R, :], z2[s][0:R, :], bet_t[0:R, :], ALU.add).then_inc(s_z3, 1)
                for s in range(2):
                    dve.wait_ge(s_z3, 2 * i + s + 1)
                    dve.tensor_tensor(grp(h, 2 * i + s), grp(h, 2 * i + s), z3[s][0:R, :], ALU.add).then_inc(s_h[s], 1)
                for s in range(2):
                    dve.wait_ge(s_bw, 2)
                    dve.wait_ge(s_h[s], i + 1 + 2 * NP)
                    dve.bn_stats(grp(st6, 2 * i + s, 6), grp(h, 2 * i + s)).then_inc(s_bn[s], 1)
            row_stats(dve, 4)

            for c in range(2):
                for half in range(2):
                    dve.memset(qscale[half * D1:(half + 1) * D1, c:c + 1], float(D1) ** -0.5 if c == half else 0.0
                                ).then_inc(s_qs, 1)
            dve.wait_ge(s_w4, 3 * 16)

            def rows1(i):
                for s in range(2):
                    dve.wait_ge(s_xTp[s], i + 2 * NP)
                    dve.tensor_scalar(xn[s][0:R, :], grp(h, 2 * i + s), col(mean, 2 * i + s), col(rstd, 2 * i + s),
                                      ALU.subtract, ALU.mult).then_inc(s_xn[s], 1)

            def keys1(i):
                for n in range(3, 6):
                    dve.wait_ge(s_qkp[n], i + 1)
                    dve.tensor_copy(k1T[:, 2 * n - 6:2 * n - 4, :],
                                    bank[2 + n][:, 0:2 * PH].rearrange("p (m r) -> p m r", m=2)).then_inc(s_qk[n], 1)

            def attend1(i, more):
                if more:
                    rows1(i + 1)
                for s in range(2):
                    dve.wait_ge(s_sp[s], i + 1 + NP)
                    dve.tensor_tensor(sm[s][0:R, :, :].rearrange("p (b j) r -> p b j r", b=4),
                                      ps[0:R, 0:4, 0:3 * R].rearrange("p b (j r) -> p b j r", j=3),
                                      bmask[0:R, :].unsqueeze(1).unsqueeze(1).broadcast_to([R, 4, 3, R]),
                                      ALU.add).then_inc(s_sm[s], 1)
                    dve.wait_ge(s_sm[s], i + 1)
                    dve.tensor_reduce(nmx[s][0:R, :], sm[s][0:R, :, :], AX, ALU.max, negate=True).then_inc(s_mx, 1)
                if more:
                    keys1(i + 1)
                for s in range(2):
                    dve.wait_ge(s_exp[s], i + 1 + NP)
                    dve.reciprocal(rden[s][0:R, :], den[s][0:R, :]).then_inc(s_rd, 1)
                    for b in range(3):
                        dve.wait_ge(s_pt1p, 6 * i + 3 * s + b + 1)
                        dve.tensor_copy(pt1[s][0:R, 4 * b:4 * b + 4, :],
                                        bank[5 + b][0:R, 0:4 * R].rearrange("p (n r) -> p n r", n=4)).then_inc(s_pt1, 1)
                    dve.wait_ge(s_rd, 2 * i + s + 1 + 2 * NP)
                    dve.wait_ge(s_op[s], i + 1 + NP)
                    dve.tensor_tensor(cx[s][0:R, :].rearrange("p (b j d) -> p b j d", b=2, j=H1 // 2),
                                      ps[0:R, 0:2, 0:A1 // 2].rearrange("p b (j d) -> p b j d", j=H1 // 2),
                                      rden[s][0:R, :].rearrange("p (b j) -> p b j", b=2).unsqueeze(3)
                                      .broadcast_to([R, 2, H1 // 2, D1]), ALU.mult).then_inc(s_ct[s], 1)
                for s in range(2):
                    dve.wait_ge(s_bw, 2)
                    dve.wait_ge(s_ap[s], i + 1 + NP)
                    dve.tensor_tensor(grp(h, 2 * i + s), bank[4][0:R, s * D:(s + 1) * D], grp(h, 2 * i + s),
                                      ALU.add).then_inc(s_h[s], 1)
                for s in range(2):
                    dve.wait_ge(s_bw, 2)
                    dve.wait_ge(s_h[s], i + 1 + 3 * NP)
                    dve.bn_stats(grp(st6, 2 * i + s, 6), grp(h, 2 * i + s)).then_inc(s_bn[s], 1)

            rows1(0)
            keys1(0)
            with dve.Fori(0, NP - 1) as i:
                attend1(i, True)
            attend1(NP - 1, False)
            row_stats(dve, 5)

            dve.wait_ge(s_w5, 10 * 16)
            with dve.Fori(0, NP) as i:
                for s in range(2):
                    dve.wait_ge(s_xTp[s], i + 3 * NP)
                    dve.tensor_scalar(xn[s][0:R, :], grp(h, 2 * i + s), col(mean, 2 * i + s), col(rstd, 2 * i + s),
                                      ALU.subtract, ALU.mult).then_inc(s_xn[s], 1)
                for s in range(2):
                    dve.wait_ge(s_lgp, 2 * i + s + 1 + 2 * NP)
                    dve.tensor_tensor(grp(lg1, 2 * i + s, E1), bank[5 + s][0:R, 0:E1], rt1b_t[0:R, :],
                                      ALU.add).then_inc(s_lg, 1)
            dve.wait_ge(s_sc, 1)
            dve.tensor_tensor(sfc[0:R, :, :], sc1[0:R, :, :], corr_t[0:R, :].unsqueeze(1).broadcast_to([R, NG, E1]),
                              ALU.add).then_inc(s_r5, 1)
            dve.wait_ge(s_r5, 1)
            s4 = sfc[0:R, :, :].rearrange("p g (c e) -> p (g c) e", e=GE)
            for d, o in ((1, 0), (2, 3), (3, 5)):
                dve.tensor_tensor(psum1[0:R, :, o:o + GE - d], s4[:, :, 0:GE - d], s4[:, :, d:GE], ALU.add).then_inc(s_r5, 1)
            dve.wait_ge(s_r5, 4)
            dve.tensor_reduce(gtop[0:R, :, :], psum1[0:R, :, :].rearrange("p (g c) e -> p g c e", g=NG), AX,
                              ALU.max).then_inc(s_r5, 1)

            def ranks(val, cmp, tri, rank, n, at):
                c = cmp[0:R, :, :].rearrange("p g (e w j) -> p g e w j", e=n, w=2)
                mine = val[0:R, :, :].unsqueeze(3).broadcast_to([R, NG, n, n])
                other = val[0:R, :, :].unsqueeze(2).broadcast_to([R, NG, n, n])
                dve.wait_ge(s_r5, at)
                dve.tensor_tensor(c[:, :, :, 0, :], other, mine, ALU.is_gt).then_inc(s_r5, 1)
                dve.tensor_tensor(c[:, :, :, 1, :], other, mine, ALU.is_ge).then_inc(s_r5, 1)
                dve.wait_ge(s_r5, at + 2)
                dve.tensor_tensor(cmp[0:R, :, :], cmp[0:R, :, :], tri[0:R, :].unsqueeze(1).broadcast_to([R, NG, 2 * n * n]),
                                  ALU.mult).then_inc(s_r5, 1)
                dve.wait_ge(s_r5, at + 3)
                dve.tensor_reduce(rank[0:R, :, :], cmp[0:R, :, :].rearrange("p g (e w) -> p g e w", e=n), AX,
                                  ALU.add).then_inc(s_r5, 1)
                dve.wait_ge(s_r5, at + 4)

            ranks(gtop, gcmp, trig, grank, G1, 5)
            dve.scalar_tensor_tensor(skept[0:R, :, :].rearrange("p g (c e) -> p (g c) e", e=GE),
                                     grank[0:R, :, :].rearrange("p g c -> p (g c)").unsqueeze(2).broadcast_to([R, NG * G1, GE]),
                                     2.0, s4, ALU.is_lt, ALU.mult).then_inc(s_r5, 1)
            ranks(skept, cmp1, tri1, lg1, E1, 10)
            dve.wait_ge(s_c1, 1)
            dve.scalar_tensor_tensor(sfc[0:R, :, :], lg1[0:R, :, :], float(K1), sc1[0:R, :, :], ALU.is_lt,
                                     ALU.mult).then_inc(s_r5, 1)
            dve.wait_ge(s_r5, 15)
            dve.tensor_reduce(wsum[0:R, :], sfc[0:R, :, :], AX, ALU.add).then_inc(s_r5, 1)
            dve.wait_ge(s_r5, 16)
            dve.tensor_scalar(wsum1[0:R, :], wsum[0:R, :], 1e-20, None, ALU.add).then_inc(s_r5, 1)
            dve.wait_ge(s_r5, 17)
            dve.reciprocal(wrec[0:R, :], wsum1[0:R, :]).then_inc(s_r5, 1)
            dve.wait_ge(s_r5, 18)
            dve.scalar_tensor_tensor(c1[0:R, :, 0:E1], sfc[0:R, :, :], SCALE1,
                                     wrec[0:R, :].unsqueeze(2).broadcast_to([R, NG, E1]), ALU.mult, ALU.mult).then_inc(s_r5, 1)
            dve.wait_ge(s_r5, R5_END)

            def weigh(i, e):
                dve.wait_ge(s_dn, E1 * i + e + 1)
                for s in range(2):
                    y = bank[4 + e % 2][0:R, s * D:(s + 1) * D]
                    if e == 0:
                        dve.wait_ge(s_wes, 2 * i + s + 1 + 2 * NP)
                        dve.wait_ge(s_o5, 2 * i)
                        dve.tensor_scalar(acc5[s][0:R, :], y, cs[s][0:R, 0:1], None, ALU.mult).then_inc(s_ac5, 1)
                    else:
                        dve.wait_ge(s_ac5, 2 * E1 * i + 2 * e - 1 + s)
                        dve.scalar_tensor_tensor(acc5[s][0:R, :], y, cs[s][0:R, e:e + 1], acc5[s][0:R, :], ALU.mult,
                                                 ALU.add).then_inc(s_ac5, 1)

            with dve.Fori(0, NP) as i:
                for s in range(2):
                    dve.wait_ge(s_xTp[s], i + 4 * NP)
                    dve.tensor_scalar(xn[s][0:R, :], grp(h, 2 * i + s), col(mean, 2 * i + s), col(rstd, 2 * i + s),
                                      ALU.subtract, ALU.mult).then_inc(s_xn[s], 1)
                for e in range(EX):
                    dve.wait_ge(s_sg, EX * i + e + 1)
                    dve.wait_ge(s_dn, E1 * i + min(max(e - 2, 0), E1))
                    if e < 3:
                        dve.wait_ge(s_sh, i)
                    dve.scalar_tensor_tensor(hid[e % 3][0:F1, :], bank[2 + e % 2][0:F1, 0:PH], bu_t[0:F1, e:e + 1],
                                             sg[e % 2][0:F1, :], ALU.add, ALU.mult).then_inc(s_hid, 1)
                    if 1 <= e <= E1:
                        weigh(i, e - 1)
                for s in range(2):
                    dve.wait_ge(s_ac5, 2 * E1 * i + 2 * E1 - 1 + s)
                    dve.wait_ge(s_sh, i + 1)
                    dve.tensor_tensor(o5[s][0:R, :], bank[6][0:R, s * D:(s + 1) * D], acc5[s][0:R, :], ALU.add).then_inc(s_o5, 1)
                for s in range(2):
                    dve.wait_ge(s_o5, 2 * i + s + 1)
                    dve.wait_ge(s_outs[s], 16 * i)
                    dve.tensor_tensor(oh[s][0:R, :], o5[s][0:R, :], grp(h, 2 * i + s), ALU.add).then_inc(s_oh, 1)

        @block.tensor
        def _(pe):
            pe.wait_ge(s_tokw, 5 * 16)
            pe.wait_ge(s_ones, 1)
            pe.matmul(bank[0][0:1, 0:D], ones[0:1, 0:1], tb_row[:, :], start=True, stop=False)
            for k in range(KB):
                for j in range(NS):
                    row = pe.matmul(bank[0][0:1, 0:D], tbe[0:KP, k, j:j + 1], tw[0:KP, k, j, :],
                                    start=False, stop=(k == KB - 1 and j == NS - 1))
            row.then_inc(s_bwrow_p, 1)
            pe.wait_ge(s_weff, KB * NS)
            pe.wait_ge(s_cnt, 1)
            for k in range(KB):
                pe.matmul(bank[1][0:R, 0:D], ones[0:KP, 0:R], weff[0:KP, k, 0:D], start=(k == 0), stop=(k == KB - 1))
            pe.wait_ge(s_bwrow, 1)
            pe.matmul(bank[1][0:R, D:2 * D], ones[0:1, 0:R], bw_row[:, :], start=True, stop=True).then_inc(s_bw_p, 1)
            with pe.Fori(0, NP) as i:
                for s in range(2):
                    pe.wait_ge(s_x[s], 16 * i + 16)
                    pe.wait_ge(s_raw[s], i)
                    for k in range(KB):
                        pe.matmul(bank[2 + s][0:R, 0:D + 1], xp[s][0:KP, k, :], weff[0:KP, k, :],
                                  start=(k == 0), stop=(k == KB - 1))
                    pe.wait_ge(s_xsq[s], i + 1)
                    for k in range(KB):
                        mm = pe.matmul(bank[2 + s][0:R, D + 1:D + 2], xsq[s][0:KP, k, :], weff[0:KP, k, D:D + 1],
                                       start=(k == 0), stop=(k == KB - 1))
                    mm.then_inc(s_emb[s], 1)
            for s in range(2):
                pe.wait_ge(s_raw[s], NP)

            pe.wait_ge(s_const, 16)
            pe.wait_ge(s_w0, 13 * 16)
            pe.wait_ge(s_sw, 5)
            with pe.Fori(0, NP) as i:
                for s in range(2):
                    pe.wait_ge(s_kT, 2 * i)
                    pe.wait_ge(s_xn[s], i + 1)
                    for k in range(2):
                        tr = pe.transpose(bank[4 * s][0:HW, k * R:(k + 1) * R], xn[s][0:R, k * HW:(k + 1) * HW],
                                          ident[0:R, 0:R])
                    tr.then_inc(s_xTp[s], 1)
                for s in range(2):
                    pe.wait_ge(s_xT[s], i + 1)
                    for k in range(2):
                        mm = pe.matmul(bank[4 * s + 1][0:R, 0:R], wz[0:HW, k, :], xT[0:HW, k, s * R:(s + 1) * R],
                                       start=(k == 0), stop=(k == 1))
                    mm.then_inc(s_zp, 1)
                for hh in range(2):
                    for k in range(2):
                        mm = pe.matmul(bank[0][0:HW, hh * PH:(hh + 1) * PH],
                                       wqkv_t[0:HW, k, D + hh * HW:D + (hh + 1) * HW], xT[0:HW, k, :],
                                       start=(k == 0), stop=(k == 1))
                mm.then_inc(s_kp, 1)
                for s in range(2):
                    pe.wait_ge(s_exp[s], i)
                    for k in range(2):
                        mm = pe.matmul(bank[4 * s + 2][0:R, 0:D], xT[0:HW, k, s * R:(s + 1) * R],
                                       wqkv_t[0:HW, k, 2 * D:3 * D], start=(k == 0), stop=(k == 1))
                    mm.then_inc(s_vp[s], 1)
                for s in range(2):
                    pe.wait_ge(s_psel, 2 * i + s + 1)
                    pe.wait_ge(s_y0, 2 * i)
                    pe.transpose(bank[4 * s + 3][0:QG, 0:R], psel[s][0:R, 0:QG], ident[0:R, 0:R]).then_inc(s_ptp0, 1)
                    for k in range(2):
                        mm = pe.matmul(bank[4 * s + 1][0:HW, R + k * QG:R + (k + 1) * QG], xn[s][0:R, k * HW:(k + 1) * HW],
                                       psel[s][0:R, 0:QG], start=True, stop=True)
                    mm.then_inc(s_xsp, 1)
                for s in range(2):
                    pe.wait_ge(s_xs, 2 * i + s + 1)
                    for hh in range(2):
                        for k in range(2):
                            mm = pe.matmul(bank[4 * s + 1][0:HW, 256 + hh * QG:256 + (hh + 1) * QG],
                                           wqkv_t[0:HW, k, hh * HW:(hh + 1) * HW], xs[s][0:HW, k, :],
                                           start=(k == 0), stop=(k == 1))
                    mm.then_inc(s_qp, 1)
                for s in range(2):
                    pe.wait_ge(s_kT, 2 * i + 2)
                    pe.wait_ge(s_v[s], i + 1)
                    pe.wait_ge(s_qb[s], 2 * i + 2)
                    for hh in range(2):
                        o = bank[4 * s + 2][0:R, D + hh * R:D + (hh + 1) * R]
                        pe.matmul(o, psel[s][0:R, :], cmask[0:R, :], start=True, stop=False)
                        mm = pe.matmul(o, qb[s][0:HW, hh, :], kT[0:HW, hh, s * R:(s + 1) * R], start=False, stop=True)
                    mm.then_inc(s_sp[s], 1)
                for s in range(2):
                    pe.wait_ge(s_pselT, 2 * i + s + 1)
                    pe.wait_ge(s_pn, 2 * i + s + 1)
                    for hh in range(2):
                        tr = pe.transpose(bank[4 * s + 3][0:R, hh * R:(hh + 1) * R], pn[s][0:R, hh, :], ident[0:R, 0:R])
                    tr.then_inc(s_ptp[s], 1)
                for s in range(2):
                    pe.wait_ge(s_pt[s], i + 1)
                    for hh in range(2):
                        mm = pe.matmul(bank[4 * s + 3][0:HW, hh * R:(hh + 1) * R], v0[s][0:R, hh * HW:(hh + 1) * HW],
                                       pt0[s][0:R, hh, :], start=True, stop=True)
                    mm.then_inc(s_op[s], 1)
                for s in range(2):
                    pe.wait_ge(s_ct[s], i + 1)
                    for hh in range(2):
                        mm = pe.matmul(bank[4 * s + 3][0:QG, 0:D], ct0[s][0:HW, hh, :], wo_t[0:HW, hh, :],
                                       start=(hh == 0), stop=(hh == 1))
                    mm.then_inc(s_ap[s], 1)
                for s in range(2):
                    pe.wait_ge(s_at, 2 * i + s + 1)
                    pe.matmul(bank[4 * s + 3][0:R, D:2 * D], pselT[s][0:QG, :], at0[s][0:QG, :], start=True,
                              stop=True).then_inc(s_up, 1)
            for s in range(2):
                pe.wait_ge(s_y0, 2 * NP)

            pe.wait_ge(s_w3, 10 * 16)
            with pe.Fori(0, NP) as i:
                for s in range(2):
                    pe.wait_ge(s_xT[s], i + NP)
                    pe.wait_ge(s_xn[s], i + 1 + NP)
                    for k in range(2):
                        tr = pe.transpose(bank[4 * s][0:HW, k * R:(k + 1) * R], xn[s][0:R, k * HW:(k + 1) * HW],
                                          ident[0:R, 0:R])
                    tr.then_inc(s_xTp[s], 1)
                for s in range(2):
                    pe.wait_ge(s_lg, 2 * i)
                    pe.wait_ge(s_xT[s], i + 1 + NP)
                    for k in range(2):
                        mm = pe.matmul(bank[4 * s + 1][0:R, 0:E0], xT[0:HW, k, s * R:(s + 1) * R], rtw_t[0:HW, k, :],
                                       start=(k == 0), stop=(k == 1))
                    mm.then_inc(s_lgp, 1)
            for s in range(2):
                pe.wait_ge(s_xT[s], 2 * NP)
                pe.wait_ge(s_lg, 2 * NP)
            pe.wait_ge(s_chosen, 1)
            ch = chosen[0:R, :, :].rearrange("p g e -> p (g e)")
            pe.matmul(bank[0][0:R, 0:NG * E0], before[0:R, :], ch, start=True, stop=False)
            for d in range(1, NG):
                mm = pe.matmul(bank[0][0:R, d * E0:NG * E0], ones[0:R, 0:R], ch[:, 0:(NG - d) * E0], start=False,
                               stop=(d == NG - 1))
            mm.then_inc(s_cntp, 1)
            pe.matmul(bank[1][:, 0:NG * E0], ones[0:R, :], ch, start=True, stop=True).then_inc(s_cntp, 1)

            for k, w in enumerate((s_w1, s_w2)):
                pe.wait_ge(w, 16 * (E0 + 1 - k))
            pe.wait_ge(s_z, 2)
            pe.wait_ge(s_pos, POS_END)
            pe.wait_ge(s_etab, 3)

            def expert_of(t):
                return pe.value_load(etab[0:1, bass.ds(t, 1)], min_val=0, max_val=E0 - 1)

            def rows_in(s, loads):
                for k in range(2):
                    tr = pe.transpose(bank[0][0:HW, k * TS:(k + 1) * TS], xin[s][:, k * HW:(k + 1) * HW], ident[:, :])
                tr.then_inc(s_tTp, 1)

            def hidden(t):
                pe.wait_ge(s_tT, t + 1)
                e = expert_of(t)
                for b in range(2):
                    for k in range(2):
                        mm = pe.matmul(bank[1 + b][:, 0:F0 // 2], xtT[0:HW + k, k, :],
                                       w1_t[0:HW + k, :, :, :].rearrange("p e k f -> p (e k f)")
                                       [:, bass.ds(e * (2 * F0) + (k * F0 + b * (F0 // 2)), F0 // 2)],
                                       start=(k == 0), stop=(k == 1))
                mm.then_inc(s_hp, 1)

            def turn_hidden(t):
                pe.wait_ge(s_hg, t + 1)
                for m in range(FB0):
                    tr = pe.transpose(bank[3 + m // 3][:, (m % 3) * TS:(m % 3 + 1) * TS], hg[:, m * 128:(m + 1) * 128], ident[:, :])
                tr.then_inc(s_hTp, 1)

            def output(t):
                e = expert_of(t)
                pe.wait_ge(s_hT, t + 1)
                if not isinstance(t, int) or t > 0:
                    pe.wait_ge(s_yt, t)
                for m in range(FB0):
                    mm = pe.matmul(bank[5][:, 0:D], hTt[:, m, :],
                                   w2_t[:, :, :, :].rearrange("p e m d -> p (e m d)")[:, bass.ds(e * (FB0 * D) + m * D, D)],
                                   start=(m == 0), stop=(m == FB0 - 1))
                mm.then_inc(s_yp, 1)

            def step(t, s, loads, more):
                turn_hidden(t - 1)
                hidden(t)
                output(t - 1)
                if more:
                    pe.wait_ge(s_xin[1 - s], 16 * loads)
                    rows_in(1 - s, loads)

            pe.wait_ge(s_xin[0], 16)
            rows_in(0, 1)
            hidden(0)
            pe.wait_ge(s_xin[1], 16)
            rows_in(1, 1)
            with pe.Fori(0, NT // 2 - 1) as i:
                step(2 * i + 1, 1, i + 2, True)
                step(2 * i + 2, 0, i + 2, True)
            step(NT - 2, 1, NT // 2 + 1, True)
            step(NT - 1, 0, 0, False)
            turn_hidden(NT - 1)
            output(NT - 1)
            pe.wait_ge(s_yt, NT)
            with pe.Fori(0, NP) as i:
                for s in range(2):
                    pe.wait_ge(s_weT, 2 * i)
                    pe.wait_ge(s_wes, 2 * i + s + 1)
                    pe.transpose(bank[4 * s][0:E0, 0:R], wes[s][0:R, :], ident[0:R, 0:R]).then_inc(s_weTp, 1)
                for s in range(2):
                    pe.wait_ge(s_y1, 2 * i)
                    pe.wait_ge(s_weT, 2 * i + s + 1)
                    pe.matmul(bank[4 * s + 1][0:R, 0:D], weT[s][0:E0, :], b2_t[0:E0, :], start=True,
                              stop=True).then_inc(s_b2p, 1)

            pe.wait_ge(s_w4, 3 * 16)
            pe.wait_ge(s_y1, 2 * NP)

            def front1(i):
                for s in range(2):
                    pe.wait_ge(s_h[s], i - 1 + 3 * NP)
                    pe.wait_ge(s_xn[s], i + 1 + 2 * NP)
                    for k in range(2):
                        tr = pe.transpose(bank[4][0:HW, s * PH + k * R:s * PH + (k + 1) * R], xn[s][0:R, k * HW:(k + 1) * HW],
                                          ident[0:R, 0:R])
                    tr.then_inc(s_xTp[s], 1)
                for s in range(2):
                    pe.wait_ge(s_xT[s], i + 1 + 2 * NP)
                for n in range(6):
                    if n >= 3:
                        pe.wait_ge(s_qk[n - 3], i + 1)
                    for m in (2 * n, 2 * n + 1):
                        for k in range(2):
                            mm = pe.matmul(bank[5 + n % 3][:, (m % 2) * PH:(m % 2 + 1) * PH],
                                           w1qkv[0:HW, k, m * 128:(m + 1) * 128], xT[0:HW, k, :],
                                           start=(k == 0), stop=(k == 1))
                    mm.then_inc(s_qkp[n], 1)

            def attend1(i, more):
                for s in range(2):
                    if s == 0:
                        for n in range(3, 6):
                            pe.wait_ge(s_qk[n], i + 1)
                        pe.wait_ge(s_pt1, 6 * i)
                    else:
                        pe.wait_ge(s_v[0], i + 1 + NP)
                    for b in range(2):
                        for k in range(2):
                            mm = pe.matmul(bank[5 + b][0:R, 0:A1 // 2], xT[0:HW, k, s * R:(s + 1) * R],
                                           w1qkv[0:HW, k, 2 * A1 + b * A1 // 2:2 * A1 + (b + 1) * A1 // 2],
                                           start=(k == 0), stop=(k == 1))
                    mm.then_inc(s_vp[s], 1)
                    if s == 0:
                        pe.wait_ge(s_ct[1], i + NP)
                        pe.wait_ge(s_cT[1], i)
                    else:
                        pe.wait_ge(s_sm[0], i + 1)
                    for n in range(H1):
                        hd = head_at(n)
                        mm = pe.matmul(bank[n // 3][0:R, (n % 3) * R:(n % 3 + 1) * R], qT[hd % 2][:, hd // 2, s * R:(s + 1) * R],
                                       k1T[:, hd // 2, s * R:(s + 1) * R], start=True, stop=True)
                    mm.then_inc(s_sp[s], 1)
                pe.wait_ge(s_v[1], i + 1 + NP)
                if more:
                    front1(i + 1)
                    for n in range(3, 6):
                        pe.wait_ge(s_qk[n], i + 2)
                for s in range(2):
                    pe.wait_ge(s_exp[s], i + 1 + NP)
                    for b in range(3):
                        if s == 1:
                            pe.wait_ge(s_pt1, 6 * i + b + 1)
                        for n in range(4):
                            tr = pe.transpose(bank[5 + b][0:R, n * R:(n + 1) * R], p1[s][0:R, 4 * b + n, :], ident[0:R, 0:R])
                        tr.then_inc(s_pt1p, 1)
                    if s == 0:
                        pe.wait_ge(s_sm[1], i + 1)
                    else:
                        pe.wait_ge(s_ct[0], i + 1 + NP)
                    for n in range(H1):
                        if n % 4 == 0:
                            pe.wait_ge(s_pt1, 6 * i + 3 * s + n // 4 + 1)
                        mm = pe.matmul(bank[n // 6][0:R, (n % 6) * D1:(n % 6 + 1) * D1], pt1[s][0:R, n, :],
                                       v1[s][0:R, n * D1:(n + 1) * D1], start=True, stop=True)
                    mm.then_inc(s_op[s], 1)
                for s in range(2):
                    pe.wait_ge(s_ct[s], i + 1 + NP)
                    if s == 1:
                        pe.wait_ge(s_cT[0], i + 1)
                    for m in range(MB1):
                        tr = pe.transpose(bank[2 + m // 3][:, (m % 3) * R:(m % 3 + 1) * R], cx[s][0:R, m * 128:(m + 1) * 128],
                                          ident[0:R, 0:R])
                    tr.then_inc(s_cTp[s], 1)
                for s in range(2):
                    pe.wait_ge(s_cT[s], i + 1)
                    if s == 1:
                        pe.wait_ge(s_h[0], i + 1 + 3 * NP)
                    for m in range(MB1):
                        mm = pe.matmul(bank[4][0:R, s * D:(s + 1) * D], cT[s][:, m, :], wo1_t[:, m, :],
                                       start=(m == 0), stop=(m == MB1 - 1))
                    mm.then_inc(s_ap[s], 1)

            front1(0)
            with pe.Fori(0, NP - 1) as i:
                attend1(i, True)
            attend1(NP - 1, False)
            for s in range(2):
                pe.wait_ge(s_h[s], 4 * NP)

            pe.wait_ge(s_w5, 10 * 16)
            pe.wait_ge(s_wgu, 2 * 16)
            with pe.Fori(0, NP) as i:
                for s in range(2):
                    pe.wait_ge(s_xT[1], i + 3 * NP)
                    pe.wait_ge(s_xn[s], i + 1 + 3 * NP)
                    for k in range(2):
                        tr = pe.transpose(bank[4][0:HW, s * PH + k * R:s * PH + (k + 1) * R], xn[s][0:R, k * HW:(k + 1) * HW],
                                          ident[0:R, 0:R])
                    tr.then_inc(s_xTp[s], 1)
                for s in range(2):
                    pe.wait_ge(s_lg, 2 * i + 2 * NP)
                    pe.wait_ge(s_xT[s], i + 1 + 3 * NP)
                    for k in range(2):
                        mm = pe.matmul(bank[5 + s][0:R, 0:E1], xT[0:HW, k, s * R:(s + 1) * R], rt1w_t[0:HW, k, :],
                                       start=(k == 0), stop=(k == 1))
                    mm.then_inc(s_lgp, 1)
            pe.wait_ge(s_xT[1], 4 * NP)
            pe.wait_ge(s_lg, 4 * NP)

            def down(i, e):
                pe.wait_ge(s_hid, EX * i + e + 1)
                pe.wait_ge(s_ac5, 2 * E1 * i + 2 * max(e - 1, 0))
                for s in range(2):
                    mm = pe.matmul(bank[4 + e % 2][0:R, s * D:(s + 1) * D], hid[e % 3][0:F1, s * R:(s + 1) * R],
                                   wd_t[0:F1, e, :], start=True, stop=True)
                mm.then_inc(s_dn, 1)

            with pe.Fori(0, NP) as i:
                for s in range(2):
                    pe.wait_ge(s_weT, 2 * i + 2 * NP)
                    pe.wait_ge(s_xn[s], i + 1 + 4 * NP)
                    for k in range(2):
                        tr = pe.transpose(bank[7][0:HW, s * PH + k * R:s * PH + (k + 1) * R], xn[s][0:R, k * HW:(k + 1) * HW],
                                          ident[0:R, 0:R])
                    tr.then_inc(s_xTp[s], 1)
                for s in range(2):
                    pe.wait_ge(s_xT[1], i + 1 + 4 * NP)
                    pe.wait_ge(s_wes, 2 * i + s + 1 + 2 * NP)
                    pe.transpose(bank[7][0:E1 + 1, s * R:(s + 1) * R], cs[s][0:R, :], ident[0:R, 0:R]).then_inc(s_weTp, 1)
                for e in range(EX):
                    pe.wait_ge(s_hid, EX * i + max(e - 1, 0))
                    for w, b in ((wg_t, 0), (wu_t, 2)):
                        for k in range(2):
                            mm = pe.matmul(bank[b + e % 2][0:F1, 0:PH], w[0:HW, k, e * F1:(e + 1) * F1], xT[0:HW, k, :],
                                           start=(k == 0), stop=(k == 1))
                    mm.then_inc(s_gp, 1)
                    if 1 <= e <= E1:
                        down(i, e - 1)
                pe.wait_ge(s_hid, EX * i + EX)
                pe.wait_ge(s_weT, 2 * i + 2 + 2 * NP)
                pe.wait_ge(s_o5, 2 * i)
                for s in range(2):
                    o = bank[6][0:R, s * D:(s + 1) * D]
                    pe.matmul(o, weT[s][0:E1 + 1, :], bd_t[0:E1 + 1, :], start=True, stop=False)
                    for e in (E1, E1 + 1):
                        mm = pe.matmul(o, hid[e % 3][0:F1, s * R:(s + 1) * R], wd_t[0:F1, e, :], start=False,
                                       stop=(e == E1 + 1))
                mm.then_inc(s_sh, 1)


def _parts(a):
    a = np.pad(a, [(0, KB * KP - FEAT)] + [(0, 0)] * (a.ndim - 1))
    return np.ascontiguousarray(a.reshape(KB, KP, *a.shape[1:]).swapaxes(0, 1))


def _patches(x):
    xh = np.zeros((NG * IPG, C_IN, SIDE + 2, SIDE + 2), np.float32)
    xh[:N_IMG, :, 1:-1, 1:-1] = x
    f = np.empty((C_IN, HALO, HALO, NG * IPG, GRID, GRID), np.float32)
    for a in range(HALO):
        for b in range(HALO):
            f[:, a, b] = xh[:, :, a:a + SIDE:PATCH, b:b + SIDE:PATCH].swapaxes(0, 1)
    f = _parts(f.reshape(FEAT, NG, R))
    return np.ascontiguousarray(f.transpose(2, 0, 1, 3)).reshape(NG, KP, KB * R)


def _shifted(w):
    w = np.asarray(w).reshape(PATCH, PATCH, NS, C_IN, -1)
    o = np.zeros((C_IN, HALO, HALO, NS, w.shape[-1]), np.float32)
    for j, (dy, dx) in enumerate(SHIFTS):
        o[:, 1 + dy:1 + dy + PATCH, 1 + dx:1 + dx + PATCH, j] = w[:, :, j].transpose(2, 0, 1, 3)
    return _parts(o.reshape(FEAT, NS, -1))


def _halves(w):
    w = np.asarray(w)
    return np.ascontiguousarray(w.reshape(2, HW, -1).swapaxes(0, 1))


def _tables():
    tok = np.arange(R)
    same = tok[:, None] // TOK == tok[None, :] // TOK
    later = (same & (tok[None, :] > tok[:, None])).astype(np.float32)
    earlier = (same & (tok[None, :] < tok[:, None])).astype(np.float32)
    bmask = np.where(same, 0.0, -1e30).astype(np.float32)
    cmask = np.where(same, np.where(later > 0, -10000.0, 0.0), -1e30).astype(np.float32)
    slot = np.tile(np.arange(QG), HH)
    rtab = np.where(tok[:, None] // TOK == slot[None, :] // KSEL, slot[None, :] % KSEL, -1).astype(np.float32)
    head = np.repeat(np.arange(HH), QG)
    hmask = (np.arange(HW)[:, None] // D0 == head[None, :]).astype(np.float32)

    before = (tok[:, None] < tok[None, :]).astype(np.float32)
    thr = np.broadcast_to(TS * np.arange(NTH, dtype=np.float32), (TS, NTH))
    below = np.broadcast_to((np.arange(E0)[None, :] < np.arange(E0)[:, None]).astype(np.float32), (TS, E0, E0))
    tile = np.arange(NT, dtype=np.float32).reshape(1, NT)

    def tri(n):
        j, e = np.arange(n)[None, :], np.arange(n)[:, None]
        t = np.stack([(j > e), (j < e)], 1).astype(np.float32).reshape(1, n * 2 * n)
        return np.ascontiguousarray(np.broadcast_to(t, (R, n * 2 * n)))
    return dict(ident=np.eye(128, dtype=np.float32), before=before, thr=thr, below=below, tile=tile,
                cmask=cmask, bmask=bmask, later=later, earlier=earlier,
                rtab=rtab, hmask=hmask, tri0=tri(E0), tri1=tri(E1), trig=tri(G1))


def kernel(**inputs):
    import concourse.bacc as _bacc
    from concourse.bass_utils import run_bass_kernel_spmd as _run

    a = {k: np.asarray(v) for k, v in inputs.items()}
    count = np.zeros((C_IN, HALO, HALO), np.float32)
    for dy, dx in SHIFTS:
        count[:, 1 + dy:1 + dy + PATCH, 1 + dx:1 + dx + PATCH] += 1
    t = _tables()
    rep = lambda v: np.ascontiguousarray(np.broadcast_to(np.asarray(v).reshape(1, -1), (R, np.asarray(v).size)))
    wqkv1 = a["L1_attn_w_qkv"].transpose(2, 1, 0, 3).reshape(D, 3 * A1)
    arrays = dict(
        x=_patches(a["x"]), tok_w=_shifted(a["L0_tok_W"]).reshape(KP, KB * NS * D),
        tok_g=_shifted(a["L0_tok_ln_gamma"])[..., 0], tok_be=_shifted(a["L0_tok_ln_beta"])[..., 0],
        tok_b=a["L0_tok_b"].reshape(1, D), tok_cnt=_parts(count.reshape(FEAT, 1)),
        wqkv=_halves(a["L0_attn_Wqkv_w"]),
        bqk=a["L0_attn_Wqkv_b"][:2 * D].reshape(4, HW).T,
        bv=rep(a["L0_attn_Wqkv_b"][2 * D:]), sel_w=_halves(a["L0_attn_sel_w"]), sel_b=rep(a["L0_attn_sel_b"]),
        temp=rep(a["L0_attn_temperature"]), wo=_halves(a["L0_attn_out_w"]), bo=rep(a["L0_attn_out_b"]),
        rt_w=_halves(a["L0_ffn_router_w"]), rt_b=rep(a["L0_ffn_router_b"]),
        w1=a["L0_ffn_w1"].reshape(E0, 2, HW, F0).transpose(0, 2, 1, 3),
        b1=a["L0_ffn_b1"].reshape(1, E0, F0),
        w2=a["L0_ffn_w2"].reshape(E0, FB0, 128, D).transpose(0, 2, 1, 3),
        b2=a["L0_ffn_b2"], gam=rep(a["L0_ffn_gamma"]), bet=rep(a["L0_ffn_beta"]),
        wqkv1=_halves(wqkv1), wo1=a["L1_attn_w_o"].reshape(MB1, 128, D).transpose(1, 0, 2),
        rt1_w=_halves(a["L1_ffn_router_w"].T), rt1_b=rep(a["L1_ffn_router_b"]), corr=rep(a["L1_ffn_corr_bias"]),
    )
    for name, g, s, b, bs in (("gate", "gWg", "sWg", "gbg", "sbg"), ("up", "gWu", "sWu", "gbu", "sbu")):
        w = np.concatenate([a["L1_ffn_" + g].transpose(1, 0, 2).reshape(D, E1 * F1), a["L1_ffn_" + s]], 1)
        arrays["w_" + name] = _halves(w)
        arrays["b_" + name] = np.concatenate([a["L1_ffn_" + b].reshape(-1), a["L1_ffn_" + bs]]).reshape(EX, F1).T
    wd = np.concatenate([a["L1_ffn_gWd"].reshape(E1 * F1, D), a["L1_ffn_sWd"]], 0)
    arrays["w_down"] = wd.reshape(EX, F1, D).transpose(1, 0, 2)
    arrays["b_down"] = a["L1_ffn_gbd"]
    arrays["sb_down"] = a["L1_ffn_sbd"].reshape(1, D)
    for k, v in t.items():
        arrays[k + "_c"] = v
    nc = _bacc.Bacc("TRN2", target_bir_lowering=False, num_devices=1)
    arrays = {k: np.ascontiguousarray(v) for k, v in arrays.items()}
    args = {k: nc.dram_tensor("in_" + k, v.shape, mybir.dt.from_np(v.dtype), kind="ExternalInput").ap()
            for k, v in arrays.items()}
    args["out"] = nc.dram_tensor("out", (NG, R, D), mybir.dt.float32, kind="ExternalOutput").ap()
    vit_tower(nc, **args)
    r = _run(nc, [{"in_" + k: v for k, v in arrays.items()}], core_ids=[0])
    return r.results[0]["out"].reshape(NG * IPG, TOK, D)[:N_IMG]
```

```python
import numpy as np
import concourse.bass as bass
from concourse import mybir
from contextlib import ExitStack


N_IMG, C_IN, SIDE, PATCH = 64, 3, 96, 16
GRID = SIDE // PATCH
TOK = GRID * GRID
IPG = 3
R = IPG * TOK
NG = 2 * -(-N_IMG // (2 * IPG))
NP = NG // 2
D = 192
HW = D // 2
HALO = PATCH + 2
FEAT = C_IN * HALO * HALO
KP = 7 * HALO
KB = -(-FEAT // KP)
NS = 5
SHIFTS = ((0, 0), (0, -1), (0, 1), (-1, 0), (1, 0))
XB = 4
FULL = PATCH * PATCH * NS * C_IN
EPS = 1e-5
H0, D0 = 12, 16
HH = H0 // 2
KSEL = 6
QG = IPG * KSEL
E0, F0 = 8, 4 * D
FB0 = F0 // 128
K0 = 2
TS = 128
NT = (NG * R * K0 - E0) // TS + E0
NTH = -(-NG * R // TS)
H1, D1 = 12, 64
A1 = H1 * D1
MB1 = A1 // 128
E1, F1 = 16, 96
EX = E1 + 2
HID1 = EX * F1
FB1 = -(-HID1 // 128)
W1 = 128 * FB1
G1 = 4
GE = E1 // G1
K1 = 4
SCALE1 = 2.5
PH = 2 * R


def vit_tower(nc, x, tok_w, tok_g, tok_be, tok_b, tok_cnt,
              wqkv, bqk, bv, sel_w, sel_b, temp, wo, bo,
              rt_w, rt_b, w1, b1, w2, b2, gam, bet,
              wqkv1, wo1,
              rt1_w, rt1_b, corr, w_gate, b_gate, w_up, b_up, w_down, b_down, sb_down,
              ident_c, before_c, thr_c, below_c, tile_c, cmask_c, bmask_c, later_c, earlier_c, rtab_c, hmask_c, order0_c, order_c, trig_c, expert_c, out):
    fp32 = mybir.dt.float32
    ALU = mybir.AluOpType
    ACT = mybir.ActivationFunctionType
    AX = mybir.AxisListType.X

    with ExitStack() as ctx:
        def sb(name, shape, dtype=fp32):
            return ctx.enter_context(nc.sbuf_tensor(name, shape, dtype))

        def sem(name):
            return ctx.enter_context(nc.semaphore(name))

        def sem2(name):
            return [sem(f"{name}_{s}") for s in range(2)]

        ps = ctx.enter_context(nc.psum_tensor("ps", [128, 8, 512], fp32))
        bank = [ps[:, n, :] for n in range(8)]

        ident = sb("ident", [128, 128])
        ones = sb("ones", [128, 128])
        h = sb("h", [128, NG, D])
        pm, pdif, pdif2, pvar2, pvar, pdev, prs = ([sb(f"{n}{q}", [128, 2]) for q in range(2)] for n in (
            "pm", "pdif", "pdif2", "pvar2", "pvar", "pdev", "prs"))
        mean = sb("mean", [128, NG])
        var = sb("var", [128, NG])
        dif = sb("dif", [128, NG])
        dif2 = sb("dif2", [128, NG])
        var2 = sb("var2", [128, NG])
        rstd = sb("rstd", [128, NG])
        sdev = sb("sdev", [128, NG])
        eps_t = sb("eps_t", [128, 1])
        warm = sb("warm", [1, 5])
        xn = [sb(f"xn{s}", [128, D]) for s in range(2)]
        xT = sb("xT", [128, 2, PH])
        st6 = sb("st6", [128, NG, 6])

        A_W = KB * NS * D
        arena1 = sb("arena1", [128, A_W + KB * (D + 1) + 4 * KB * R])
        tw = arena1[:, 0:A_W].rearrange("p (k s d) -> p k s d", k=KB, s=NS)
        tg = sb("tg", [128, KB, NS])
        tbe = sb("tbe", [128, KB, NS])
        weff = arena1[:, A_W:A_W + KB * (D + 1)].rearrange("p (k d) -> p k d", k=KB)
        cnt = sb("cnt", [128, KB, 1])
        tb_row = sb("tb_row", [1, D])
        bw_row = sb("bw_row", [1, D])
        csum = sb("csum", [128, D])
        bw = sb("bw", [128, D])
        patches = arena1[:, A_W + KB * (D + 1):].rearrange("p (n k r) -> p n k r", n=4, k=KB)
        xp = [patches[:, n, :, :] for n in range(XB)]
        nmu, m2, evar, edev, erstd = ([sb(f"{n}{s}", [128, 1]) for s in range(2)] for n in ("nmu", "m2", "evar", "edev", "erstd"))
        tmp = [sb(f"tmp{s}", [128, D]) for s in range(2)]

        cmask = sb("cmask", [128, R])
        bmask = sb("bmask", [128, R])
        later = sb("later", [128, R])
        earlier = sb("earlier", [128, R])
        rtab = sb("rtab", [128, R])
        hmask = sb("hmask", [128, R])
        hmaskq = sb("hmaskq", [128, R])
        wqkv_t = sb("wqkv_t", [128, 2, 3 * D])
        wo_t = sb("wo_t", [128, 2, D])
        bqk_t = sb("bqk_t", [128, 4])
        bv_t = sb("bv_t", [128, D])
        bo_t = sb("bo_t", [128, D])
        selw_t = sb("selw_t", [128, 2, 2])
        selb_t = sb("selb_t", [128, 2])
        temp_t = sb("temp_t", [128, 1])
        itemp = sb("itemp", [128, 1])
        dselb = sb("dselb", [128, 1])
        bz = sb("bz", [128, 1])
        dselw = sb("dselw", [128, 2, 1])
        wz = sb("wz", [128, 2, R])

        def slots(name, shape):
            return [sb(f"{name}{s}", shape) for s in range(2)]

        kT = sb("kT", [128, 2, PH])
        zr = slots("zr", [128, R])
        zc = slots("zc", [128, 1])
        junk = slots("junk", [128, 3, R])
        rka = slots("rka", [128, 1])
        rkb = slots("rkb", [128, 1])
        psel = slots("psel", [128, R])
        pselT = slots("pselT", [128, R])
        xs = slots("xs", [128, 2, QG])
        qb = slots("qb", [128, 2, R])
        v0 = slots("v0", [128, D])
        nmx = slots("nmx", [128, H1])
        den = slots("den", [128, H1])
        rden = slots("rden", [128, H1])
        p0 = slots("p0", [128, 2, R])
        pn = slots("pn", [128, 2, R])
        pt0 = slots("pt0", [128, 2, R])
        om = slots("om", [128, 2, R])
        ct0 = slots("ct0", [128, 2, QG])
        at0 = slots("at0", [128, D])
        ez = slots("ez", [128, 1])
        ez1 = slots("ez1", [128, 1])
        sig = slots("sig", [128, 1])

        arena2 = sb("arena2", [128, 18560])
        taken = [0]

        def part(shape):
            n = int(np.prod(shape))
            v = arena2[:, taken[0]:taken[0] + n]
            taken[0] += n
            names = "abcd"[:len(shape)]
            return v.rearrange(f"p ({' '.join(names)}) -> p {' '.join(names)}",
                               **{c: m for c, m in zip(names, shape)}) if len(shape) > 1 else v

        acc = part([NG, D])
        xsq = [arena2[:, taken[0] + n * KB * R:taken[0] + (n + 1) * KB * R].rearrange("p (k r) -> p k r", k=KB)
               for n in range(XB)]
        w2_t = part([E0, FB0, D])
        u32, i32 = mybir.dt.uint32, mybir.dt.int32
        xtT = part([2, TS])
        routing_at = taken[0]
        zero = part([D])
        chosen = part([NG, E0])
        place = part([NG, E0])
        pcmp = part([NG, E0])
        posf = [part([NG]) for _ in range(K0)]
        count = part([E0])
        tcmp = part([E0, NTH])
        tiles = part([E0])
        bcmp = part([E0, E0])
        first = part([E0])
        frow = part([E0])
        ecmp = part([NT, E0 - 1])
        etabf = part([NT])
        before = part([R])
        thr = part([NTH])
        below = part([E0, E0])
        tile_n = part([NT])
        pos = [sb(f"pos{k}", [128, NG], u32) for k in range(K0)]
        etab = sb("etab", [1, NT], i32)
        left0 = part([NG, E0])
        best0 = part([NG])
        taken[0] = routing_at
        xin = [part([D]) for _ in range(2)]
        hg = part([F0])
        hTt = part([FB0, TS])
        yt = [part([D]) for _ in range(2)]
        yg = [[part([D]) for _ in range(2)] for _ in range(K0)]
        w1_t = arena1[:, 0:E0 * 2 * F0].rearrange("p (e k f) -> p e k f", e=E0, k=2)
        sorted_x = nc.dram_tensor("sorted_x", (NT * TS, D), fp32).ap()
        sorted_y = nc.dram_tensor("sorted_y", (NT * TS, D), fp32).ap()
        assert NT % 2 == 1
        b2_t = sb("b2_t", [128, D])
        rtw_t = sb("rtw_t", [128, 2, E0])
        rtb_t = sb("rtb_t", [128, E0])
        gam_t = sb("gam_t", [128, D])
        bet_t = sb("bet_t", [128, D])
        order0 = sb("order0", [128, E0])
        lg = sb("lg", [128, NG, E0])
        eq = [sb(f"eq{k}", [128, NG, E0]) for k in range(2)]
        eql = [sb(f"eql{k}", [128, NG, E0]) for k in range(2)]
        top = [sb(f"top{k}", [128, NG]) for k in range(2)]
        gap = sb("gap", [128, NG])
        egap = sb("egap", [128, NG])
        egap1 = sb("egap1", [128, NG])
        gw = [sb(f"gw{k}", [128, NG]) for k in range(2)]
        we = sb("we", [128, NG, E0])
        wes = slots("wes", [128, E0])
        weT = slots("weT", [128, R])
        z1 = slots("z1", [128, D])
        y2 = slots("y2", [128, D])
        z3 = slots("z3", [128, D])

        taken[0] = 0
        qT = [part([MB1, PH]) for _ in range(2)]
        k1T = part([MB1, PH])
        v1 = [part([A1]) for _ in range(2)]
        sm = [part([H1, R]) for _ in range(2)]
        p1 = [part([H1, R]) for _ in range(2)]
        pt1 = sm
        cx = [part([A1]) for _ in range(2)]
        cT = [part([MB1, R]) for _ in range(2)]
        qscale = sb("qscale", [128, 2])
        w1qkv = arena1[:, 0:6 * A1].rearrange("p (k n) -> p k n", k=2)
        wo1_t = sb("wo1_t", [128, MB1, D])
        s_w4 = sem("s_w4")
        s_qs = sem("s_qs")
        s_qkp = sem("s_qkp")
        s_qc = sem("s_qc")
        s_kc = sem("s_kc")
        s_sm = sem2("s_sm")
        s_pt1p = sem("s_pt1p")
        s_pt1 = sem("s_pt1")
        s_cTp = sem2("s_cTp")
        s_cT = sem2("s_cT")
        wg_t = arena1[:, 6 * A1:6 * A1 + 2 * W1].rearrange("p (k n) -> p k n", k=2)
        wu_t = arena1[:, 6 * A1 + 2 * W1:6 * A1 + 4 * W1].rearrange("p (k n) -> p k n", k=2)
        taken[0] = 14736
        wd_t = part([FB1, D])
        bd_t = sb("bd_t", [128, D])
        bg_t = sb("bg_t", [128, FB1])
        bu_t = sb("bu_t", [128, FB1])
        rt1w_t = sb("rt1w_t", [128, 2, E1])
        taken[0] = 0
        rt1b_t = sb("rt1b_t", [128, E1])
        corr_t = sb("corr_t", [128, E1])
        xTall = part([2, NG * R])
        pick = [part([NG, E1]) for _ in range(2)]
        best = [part([NG]) for _ in range(2)]
        lg1 = part([NG, E1])
        sc1 = part([NG, E1])
        sfc = part([NG, E1])
        psum1 = part([NG * G1, 6])
        gtop = part([NG, G1])
        gcmp = part([NG, G1 * 2 * G1])
        grank = part([NG, G1])
        skept = part([NG, E1])
        order = part([E1])
        trig = part([G1 * 2 * G1])
        expert_of_hid = part([W1])
        c1T = part([PH])
        hid = [part([PH]) for _ in range(2)]
        hidw = [part([PH]) for _ in range(2)]
        sg = [part([PH]) for _ in range(2)]
        oh = [part([D]) for _ in range(2)]
        c1 = sb("c1", [128, NG, E1 + 1])
        wsum = sb("wsum", [128, NG])
        wsum1 = sb("wsum1", [128, NG])
        wrec = sb("wrec", [128, NG])
        cs = slots("cs", [128, E1 + 1])
        s_wgu = sem("s_wgu")
        s_w5 = sem("s_w5")
        s_c1 = sem("s_c1")
        s_r5 = sem("s_r5")
        s_sc = sem("s_sc")
        s_gp = sem("s_gp")
        s_sg = sem("s_sg")
        s_hid = sem("s_hid")
        s_cb = sem("s_cb")
        s_hw = sem("s_hw")
        s_sh = sem("s_sh")
        s_oh = sem("s_oh")
        s_w3 = sem("s_w3")
        s_w1 = sem("s_w1")
        s_w2 = sem("s_w2")
        s_xTa = sem("s_xTa")
        s_rows = sem("s_rows")
        s_z = sem("s_z")
        s_xz = sem("s_xz")
        s_chosen = sem("s_chosen")
        s_cntp = sem("s_cntp")
        s_pos = sem("s_pos")
        s_etab = sem("s_etab")
        s_scat = sem("s_scat")
        s_xin = sem2("s_xin")
        s_tTp = sem("s_tTp")
        s_tT = sem("s_tT")
        s_hp = sem("s_hp")
        s_hg = sem("s_hg")
        s_hTp = sem("s_hTp")
        s_hT = sem("s_hT")
        s_yp = sem("s_yp")
        s_yt = sem("s_yt")
        s_yst = sem2("s_yst")
        s_yg = sem2("s_yg")
        s_yadd = sem("s_yadd")
        s_lgp = sem("s_lgp")
        s_lg = sem("s_lg")
        s_rt = sem("s_rt")
        s_eg = sem("s_eg")
        s_wes = sem("s_wes")
        s_weTp = sem("s_weTp")
        s_weT = sem("s_weT")
        s_b2p = sem("s_b2p")
        s_y2 = sem("s_y2")
        s_z1 = sem("s_z1")
        s_z3 = sem("s_z3")
        s_w0 = sem("s_w0")
        s_sw = sem("s_sw")
        s_xn = sem2("s_xn")
        s_xTp = sem2("s_xTp")
        s_xT = sem2("s_xT")
        s_zp = sem("s_zp")
        s_zr = sem("s_zr")
        s_zc = sem("s_zc")
        s_rk = sem("s_rk")
        s_psel = sem("s_psel")
        s_ptp0 = sem("s_ptp0")
        s_pselT = sem("s_pselT")
        s_xsp = sem("s_xsp")
        s_xs = sem("s_xs")
        s_qp = sem("s_qp")
        s_qb = sem2("s_qb")
        s_kp = sem("s_kp")
        s_kT = sem("s_kT")
        s_vp = sem2("s_vp")
        s_v = sem2("s_v")
        s_sp = sem2("s_sp")
        s_mx = sem("s_mx")
        s_exp = sem2("s_exp")
        s_rd = sem("s_rd")
        s_pn = sem("s_pn")
        s_ptp = sem2("s_ptp")
        s_pt = sem2("s_pt")
        s_op = sem2("s_op")
        s_om = sem("s_om")
        s_ct = sem2("s_ct")
        s_ap = sem2("s_ap")
        s_at = sem("s_at")
        s_up = sem("s_up")
        s_ez = sem("s_ez")
        s_ez1 = sem("s_ez1")
        s_sig = sem("s_sig")
        s_hx = sem("s_hx")

        s_const = sem("s_const")
        s_tokw = sem("s_tokw")
        s_ones = sem("s_ones")
        s_eps = sem("s_eps")
        s_weff = sem("s_weff")
        s_cnt = sem("s_cnt")
        s_bwrow_p = sem("s_bwrow_p")
        s_bwrow = sem("s_bwrow")
        s_bw_p = sem("s_bw_p")
        s_bw = sem("s_bw")
        s_x, s_emb, s_raw = ([sem(f"{n}_{b}") for b in range(XB)] for n in ("s_x", "s_emb", "s_raw"))
        s_xsq = sem("s_xsq")
        s_er = sem("s_er")
        s_err = sem("s_err")
        s_e1 = sem("s_e1")
        s_h = sem2("s_h")
        s_bn = sem2("s_bn")
        s_mo = sem2("s_mo")
        s_dv = sem2("s_dv")
        s_rs = sem2("s_rs")
        s_kept = sem("s_kept")
        s_st = sem("s_st")
        s_sd = sem("s_sd")
        s_outs = sem2("s_outs")

        R5_END = 15 + 6 * K1
        PICKED = -3e38
        POS_END = 13
        RT_GAP, RT_END = 12, 18

        block = ctx.enter_context(nc.Block())

        turned = (ps[:, 2:4, :], ps[:, 0:2, :])
        attended = (bank[4], bank[5])
        def has_earlier(i):
            return not isinstance(i, int) or i > 0

        def grp(t, g, n=D):
            return t[0:R, :, :].rearrange("p g d -> p (g d)")[:, bass.ds(g * n, n)]

        def col(t, g):
            return t[0:R, bass.ds(g, 1)]

        def head_at(n):
            b, j = divmod(n, 3)
            return 2 * (b // 2 * 3 + j) + b % 2

        def row_stats(dve, time):
            st = 7 * (time - 1)
            a = st6[0:R, :, :]
            for s in range(2):
                dve.wait_ge(s_bn[s], NP * (1, 4)[time - 1] + NP)
            dve.tensor_tensor(mean[0:R, :], a[:, :, 1], a[:, :, 4], ALU.add).then_inc(s_st, 1)
            dve.tensor_tensor(dif[0:R, :], a[:, :, 1], a[:, :, 4], ALU.subtract).then_inc(s_st, 1)
            dve.tensor_tensor(var2[0:R, :], a[:, :, 2], a[:, :, 5], ALU.add).then_inc(s_st, 1)
            dve.wait_ge(s_st, st + 2)
            dve.scalar_tensor_tensor(dif2[0:R, :], dif[0:R, :], 0.25, dif[0:R, :], ALU.mult, ALU.mult).then_inc(s_st, 1)
            dve.tensor_scalar(mean[0:R, :], mean[0:R, :], 0.5, None, ALU.mult).then_inc(s_st, 1)
            dve.wait_ge(s_st, st + 4)
            dve.scalar_tensor_tensor(var[0:R, :], var2[0:R, :], 1.0 / D, dif2[0:R, :], ALU.mult, ALU.add).then_inc(s_st, 1)
            dve.wait_ge(s_sd, time)
            dve.reciprocal(rstd[0:R, :], sdev[0:R, :]).then_inc(s_st, 1)
            dve.wait_ge(s_st, st + 7)

        def spread(dve, i, k, src, ready):
            q, n = k // 2, i + NP * (k == 1)
            bn = i if k == 0 else 2 * i + (2 * NP + k - 1)
            a = st6[0:R, 2 * q:2 * q + 2, :]
            for s in range(2):
                dve.wait_ge(s_bw, 2)
                ready(s)
                dve.bn_stats(st6[0:R, 2 * q + s, :], grp(src, 2 * i + s)).then_inc(s_bn[s], 1)
            for s in range(2):
                dve.wait_ge(s_bn[s], bn + 1)
            dve.tensor_tensor(pm[q][0:R, :], a[:, :, 1], a[:, :, 4], ALU.add).then_inc(s_mo[q], 1)
            dve.tensor_tensor(pdif[q][0:R, :], a[:, :, 1], a[:, :, 4], ALU.subtract).then_inc(s_mo[q], 1)
            dve.tensor_tensor(pvar2[q][0:R, :], a[:, :, 2], a[:, :, 5], ALU.add).then_inc(s_mo[q], 1)
            dve.wait_ge(s_mo[q], 6 * n + 2)
            dve.scalar_tensor_tensor(pdif2[q][0:R, :], pdif[q][0:R, :], 0.25, pdif[q][0:R, :], ALU.mult, ALU.mult
                                     ).then_inc(s_mo[q], 1)
            dve.wait_ge(s_mo[q], 6 * n + 4)
            dve.scalar_tensor_tensor(pvar[q][0:R, :], pvar2[q][0:R, :], 1.0 / D, pdif2[q][0:R, :], ALU.mult, ALU.add
                                     ).then_inc(s_mo[q], 1)
            dve.tensor_scalar(mean[0:R, bass.ds(2 * i, 2)], pm[q][0:R, :], 0.5, None, ALU.mult).then_inc(s_mo[q], 1)

        def deviations(act, i, k):
            q, n = k // 2, i + NP * (k == 1)
            act.wait_ge(s_mo[q], 6 * n + 5)
            act.activation(pdev[q][0:R, :], pvar[q][0:R, :], ACT.Sqrt, bias=eps_t[0:R, :]).then_inc(s_dv[q], 1)

        def inverse(dve, i, k):
            q, n = k // 2, i + NP * (k == 1)
            dve.wait_ge(s_dv[q], n + 1)
            dve.reciprocal(prs[q][0:R, :], pdev[q][0:R, :]).then_inc(s_rs[q], 1)

        def keep_inverse(dve, i, k):
            q, n = k // 2, i + NP * (k == 1)
            dve.wait_ge(s_rs[q], n + 1)
            dve.tensor_scalar(rstd[0:R, bass.ds(2 * i, 2)], prs[q][0:R, :], 1.0, None, ALU.mult).then_inc(s_kept, 1)

        def rows_of(dve, i, free):
            for s in range(2):
                free(s)
                dve.tensor_scalar(xn[s][0:R, :], grp(h, 2 * i + s), col(mean, 2 * i + s), col(rstd, 2 * i + s),
                                  ALU.subtract, ALU.mult).then_inc(s_xn[s], 1)

        def load_patches(sp, j, b):
            sp.dma_start(xp[b][0:KP, :, :].rearrange("p k r -> p (k r)"),
                         x[bass.ds(XB * j + b, 1), :, :].rearrange("a p f -> p (a f)")).then_inc(s_x[b], 16)

        def emb_count(b):
            return (NG - b + XB - 1) // XB

        def use_tables(act, func, n):
            act.activation(warm[0:1, n:n + 1], eps_t[0:1, :], func)

        def row_sdev(act, time):
            act.wait_ge(s_st, 7 * (time - 1) + 6)
            act.activation(sdev[0:R, :], var[0:R, :], ACT.Sqrt, bias=eps_t[0:R, :]).then_inc(s_sd, 1)

        @block.sync
        def _(sp):
            for t, d in ((ident[:, :], ident_c),):
                sp.dma_start(t, d).then_inc(s_const, 16)
            for t, d in ((arena1[0:KP, 0:A_W], tok_w), (tg[0:KP, :, :], tok_g), (tbe[0:KP, :, :], tok_be),
                         (tb_row[:, :], tok_b), (cnt[0:KP, :, :], tok_cnt)):
                sp.dma_start(t, d).then_inc(s_tokw, 16)
            for t, d in ((wqkv_t[0:HW, :, :], wqkv), (wo_t[0:HW, :, :], wo), (bqk_t[0:HW, :], bqk),
                         (bv_t[0:R, :], bv), (bo_t[0:R, :], bo), (selw_t[0:HW, :, :], sel_w),
                         (selb_t[0:R, :], sel_b), (temp_t[0:R, :], temp), (cmask[0:R, :], cmask_c),
                         (later[0:R, :], later_c), (earlier[0:R, :], earlier_c), (rtab[0:R, :], rtab_c),
                         (hmask[0:HW, :], hmask_c)):
                sp.dma_start(t, d).then_inc(s_w0, 16)
            for b in range(XB):
                load_patches(sp, 0, b)
            with sp.Fori(1, NG // XB) as j:
                for b in range(XB):
                    sp.wait_ge(s_emb[b], j)
                    load_patches(sp, j, b)
            for b in range(NG % XB):
                sp.wait_ge(s_emb[b], NG // XB)
                load_patches(sp, NG // XB, b)
            for t, d in ((rtw_t[0:HW, :, :], rt_w), (rtb_t[0:R, :], rt_b), (b2_t[0:E0, :], b2), (gam_t[0:R, :], gam),
                         (bet_t[0:R, :], bet), (order0[0:R, :], order0_c)):
                sp.dma_start(t, d).then_inc(s_w3, 16)
            for t, d in ((before[0:R, :], before_c), (thr[:, :], thr_c), (below[:, :, :], below_c),
                         (tile_n[0:1, :], tile_c)):
                sp.dma_start(t, d).then_inc(s_w3, 16)
            for b in range(XB):
                sp.wait_ge(s_emb[b], emb_count(b))
            for e in range(E0):
                sp.dma_start(w1_t[0:HW, e, :, :], w1[e]).then_inc(s_w1, 16)
                sp.dma_start(w2_t[:, e, :, :], w2[e]).then_inc(s_w2, 16)
            sp.dma_start(w1_t[HW:HW + 1, :, 1, :], b1).then_inc(s_w1, 16)
            sp.wait_ge(s_z, 1)
            sp.dma_start(sorted_x.rearrange("(t p) d -> p t d", p=TS), zero[:, :].unsqueeze(1).broadcast_to([TS, NT, D])
                         ).then_inc(s_xz, 16)
            sp.wait_ge(s_scat, 16 * K0 * NG)

            def load_tile(t, s):
                sp.dma_start(xin[s][:, :], sorted_x[bass.ds(t * TS, TS), :]).then_inc(s_xin[s], 16)

            def store_tile(t, s):
                sp.wait_ge(s_yt, t + 1)
                sp.dma_start(sorted_y[bass.ds(t * TS, TS), :], yt[s][:, :]).then_inc(s_yst[s], 16)

            for t in range(2):
                load_tile(t, t)
            with sp.Fori(0, NT // 2 - 1) as i:
                for s in range(2):
                    sp.wait_ge(s_tTp, 2 * i + s + 1)
                    load_tile(2 * i + s + 2, s)
                    store_tile(2 * i + s, s)
            sp.wait_ge(s_tTp, NT - 2)
            load_tile(NT - 1, 0)
            for t in range(NT - 3, NT):
                store_tile(t, t % 2)
            sp.wait_ge(s_hp, NT)
            for t, d in ((w1qkv[0:HW, :, :], wqkv1), (wo1_t[:, :, :], wo1), (bmask[0:R, :], bmask_c)):
                sp.dma_start(t, d).then_inc(s_w4, 16)
            sp.dma_start(wg_t[0:HW, :, :], w_gate).then_inc(s_wgu, 16)
            sp.dma_start(wu_t[0:HW, :, :], w_up).then_inc(s_wgu, 16)
            for s in range(2):
                sp.wait_ge(s_h[s], 3 * NP)
            for t, d in ((wd_t[:, :, :], w_down), (bd_t[0:E1, :], b_down), (bd_t[E1:E1 + 1, :], sb_down),
                         (bg_t[:, :], b_gate), (bu_t[:, :], b_up), (rt1w_t[0:HW, :, :], rt1_w),
                         (rt1b_t[0:R, :], rt1_b), (corr_t[0:R, :], corr)):
                sp.dma_start(t, d).then_inc(s_w5, 16)
            for s in range(2):
                sp.wait_ge(s_h[s], 4 * NP)
            sp.dma_start(order[0:R, :], order_c).then_inc(s_w5, 16)
            sp.dma_start(expert_of_hid[0:E1 + 1, :], expert_c).then_inc(s_w5, 16)
            sp.dma_start(trig[0:R, :], trig_c).then_inc(s_w5, 16)
            with sp.Fori(0, NP) as i:
                for s in range(2):
                    sp.wait_ge(s_oh, 2 * i + s + 1)
                    sp.dma_start(out[bass.ds(2 * i + s, 1)].rearrange("a r d -> (a r) d"), oh[s][0:R, :]
                                 ).then_inc(s_outs[s], 16)
            for s in range(2):
                sp.wait_ge(s_outs[s], 16 * NP)

        @block.gpsimd
        def _(pool):
            pool.memset(ones[:, :], 1.0).then_inc(s_ones, 1)
            pool.memset(eps_t[:, :], EPS).then_inc(s_eps, 1)
            pool.memset(zero[:, :], 0.0).then_inc(s_z, 1)
            pool.wait_ge(s_z, 1)
            pool.memset(xtT[HW:HW + 1, 1, :], 1.0).then_inc(s_z, 1)
            pool.wait_ge(s_z, 2)
            pool.wait_ge(s_tokw, 5 * 16)
            pool.tensor_copy(weff[0:KP, :, D:D + 1], cnt[0:KP, :, :]).then_inc(s_cnt, 1)
            pool.wait_ge(s_rows, 2 * NP)
            pool.wait_ge(s_xz, 16)
            pool.wait_ge(s_pos, POS_END)
            for g in range(NG):
                for k in range(K0):
                    pool.indirect_dma_start(sorted_x, bass.IndirectOffsetOnAxis(pos[k][0:R, g:g + 1], 0),
                                            acc[0:R, g, :], None).then_inc(s_scat, 16)
            pool.wait_ge(s_rt, RT_END)
            for s in range(2):
                pool.wait_ge(s_yst[s], 16 * (NT // 2 + 1 - s))
            for g in range(NG):
                s = g % 2
                if g >= 2:
                    pool.wait_ge(s_weTp, g - 1)
                pool.tensor_copy(wes[s][0:R, :], we[0:R, g, :]).then_inc(s_wes, 1)
                if g >= 2:
                    pool.wait_ge(s_y2, g - 1)
                for k in range(K0):
                    pool.indirect_dma_start(yg[k][s][0:R, :], None, sorted_y,
                                            bass.IndirectOffsetOnAxis(pos[k][0:R, g:g + 1], 0)).then_inc(s_yg[s], 16)
            pool.memset(c1[0:R, :, :], 1.0).then_inc(s_c1, 1)
            with pool.Fori(0, NP) as i:
                for s in range(2):
                    pool.wait_ge(s_ones, 1)
                    pool.wait_ge(s_xT[s], i + 1 + 3 * NP)
                    pool.tensor_copy(xTall[0:HW, :, bass.ds((2 * i + s) * R, R)], xT[0:HW, :, s * R:(s + 1) * R]
                                     ).then_inc(s_xTa, 1)
            with pool.Fori(0, NP) as i:
                for s in range(2):
                    pool.wait_ge(s_ones, 1)
                    pool.wait_ge(s_r5, R5_END)
                    pool.wait_ge(s_weTp, 2 * i + 2 * NP)
                    pool.tensor_copy(cs[s][0:R, :], grp(c1, 2 * i + s, E1 + 1)).then_inc(s_wes, 1)

        @block.scalar
        def _(act):
            act.wait_ge(s_eps, 1)
            use_tables(act, ACT.Sqrt, 0)

            def squares(j, b):
                act.wait_ge(s_x[b], 16 * j + 16)
                if has_earlier(j):
                    act.wait_ge(s_emb[b], j)
                act.activation(xsq[b][0:KP, :, :], xp[b][0:KP, :, :], ACT.Square).then_inc(s_xsq, 1)

            def roots(j, half):
                for s in range(2):
                    act.wait_ge(s_eps, 1)
                    act.wait_ge(s_e1, 6 * (XB // 2 * j + half) + s + 5)
                    act.activation(edev[s][0:R, :], evar[s][0:R, :], ACT.Sqrt, bias=eps_t[0:R, :]).then_inc(s_er, 1)
                deviations(act, XB // 2 * j + half, 0)

            for b in range(XB):
                squares(0, b)
            roots(0, 0)
            with act.Fori(1, NG // XB) as j:
                for b in (0, 1):
                    squares(j, b)
                roots(j - 1, 1)
                for b in (2, 3):
                    squares(j, b)
                roots(j, 0)
            for b in range(NG % XB):
                squares(NG // XB, b)
            roots(NG // XB - 1, 1)
            roots(NG // XB, 0)

            use_tables(act, ACT.Exp, 1)
            act.wait_ge(s_w0, 13 * 16)

            def rows0(i):
                for s in range(2):
                    act.wait_ge(s_xTp[s], i + 1)
                    if has_earlier(i):
                        act.wait_ge(s_vp[s], i)
                    act.copy(xT[0:HW, :, s * R:(s + 1) * R],
                             bank[4 * s][0:HW, 0:PH].rearrange("p (k r) -> p k r", k=2)).then_inc(s_xT[s], 1)

            def keys0(i):
                act.wait_ge(s_kp, i + 1)
                for s in range(2):
                    if has_earlier(i):
                        act.wait_ge(s_sp[s], i)
                for hh in range(2):
                    act.activation(kT[0:HW, hh, :], bank[0][0:HW, hh * PH:(hh + 1) * PH], ACT.Identity,
                                   bias=bqk_t[0:HW, 2 + hh:3 + hh]).then_inc(s_kT, 1)

            def attend0(i, more):
                for s in range(2):
                    act.wait_ge(s_zc, 2 * i + s + 1)
                    if has_earlier(i):
                        act.wait_ge(s_ez1, 2 * i)
                    act.activation(ez[s][0:R, :], zc[s][0:R, :], ACT.Exp, scale=-1.0).then_inc(s_ez, 1)
                for s in range(2):
                    act.wait_ge(s_ptp0, 2 * i + s + 1)
                    if has_earlier(i):
                        act.wait_ge(s_up, 2 * i)
                    act.copy(pselT[s][0:QG, :], bank[4 * s + 3][0:QG, 0:R]).then_inc(s_pselT, 1)
                for s in range(2):
                    act.wait_ge(s_mx, 2 * i + s + 1)
                    if has_earlier(i):
                        act.wait_ge(s_pn, 2 * i)
                    for hh in range(2):
                        ex = act.activation(p0[s][0:R, hh, :], bank[4 * s + 2][0:R, D + hh * R:D + (hh + 1) * R], ACT.Exp,
                                            bias=nmx[s][0:R, hh:hh + 1], accum_out=den[s][0:R, hh:hh + 1])
                    ex.then_inc(s_exp[s], 1)
                if more:
                    rows0(i + 1)
                    keys0(i + 1)
                for s in range(2):
                    act.wait_ge(s_ptp[s], i + 1)
                    if has_earlier(i):
                        act.wait_ge(s_op[s], i)
                    act.copy(pt0[s][0:R, :, :], bank[4 * s + 3][0:R, 0:PH].rearrange("p (k r) -> p k r", k=2)
                             ).then_inc(s_pt[s], 1)

            rows0(0)
            keys0(0)
            attend0(0, True)
            with act.Fori(1, NP - 1) as i:
                attend0(i, True)
            attend0(NP - 1, False)
            row_sdev(act, 1)


            def router_rows0(i):
                for s in range(2):
                    act.wait_ge(s_xTp[s], i + 1 + NP)
                    if has_earlier(i):
                        act.wait_ge(s_lgp, 2 * i)
                    act.copy(xT[0:HW, :, s * R:(s + 1) * R],
                             bank[4 * s][0:HW, 0:PH].rearrange("p (k r) -> p k r", k=2)).then_inc(s_xT[s], 1)

            router_rows0(0)
            with act.Fori(1, NP) as i:
                router_rows0(i)
            act.wait_ge(s_rt, RT_GAP)
            act.activation(egap[0:R, :], gap[0:R, :], ACT.Exp).then_inc(s_eg, 1)
            use_tables(act, ACT.Gelu, 2)

            def gelu(t):
                act.wait_ge(s_hp, t + 1)
                act.activation(hg[:, :].rearrange("p (b f) -> p b f", b=2), ps[:, 1:3, 0:F0 // 2], ACT.Gelu).then_inc(s_hg, 1)

            gelu(0)
            with act.Fori(1, NT) as t:
                gelu(t)
            use_tables(act, ACT.Sqrt, 1)

            def weights0(i):
                for s in range(2):
                    act.wait_ge(s_weTp, 2 * i + s + 1)
                    if has_earlier(i):
                        act.wait_ge(s_b2p, 2 * i)
                    act.copy(weT[s][0:E0, :], bank[4 * s][0:E0, 0:R]).then_inc(s_weT, 1)

            weights0(0)
            with act.Fori(0, NP - 1) as i:
                weights0(i + 1)
                deviations(act, i, 1)
                deviations(act, i, 2)
            deviations(act, NP - 1, 1)
            deviations(act, NP - 1, 2)

            act.wait_ge(s_w4, 3 * 16)
            act.wait_ge(s_qs, 4)
            use_tables(act, ACT.Exp, 3)

            def rows1(i):
                for s in range(2):
                    act.wait_ge(s_xTp[1], i + 1 + 2 * NP)
                    act.copy(xT[0:HW, :, s * R:(s + 1) * R],
                             bank[4][0:HW, s * PH:(s + 1) * PH].rearrange("p (k r) -> p k r", k=2)).then_inc(s_xT[s], 1)

            def queries1(i):
                for n in range(3):
                    act.wait_ge(s_qkp, 6 * i + n + 1)
                    for c in range(2):
                        q = act.activation(qT[c][:, 2 * n:2 * n + 2, :],
                                           bank[5 + n][:, 0:2 * PH].rearrange("p (m r) -> p m r", m=2),
                                           ACT.Copy, scale=qscale[:, c:c + 1])
                    q.then_inc(s_qc, 1)

            def values1(i, s):
                act.wait_ge(s_vp[s], i + 1 + NP)
                act.copy(v1[s][0:R, :].rearrange("p (b f) -> p b f", b=2), ps[0:R, 5:7, 0:A1 // 2]).then_inc(s_v[s], 1)

            def attend1(i, more):
                values1(i, 1)
                if more:
                    rows1(i + 1)
                for s in range(2):
                    if s == 1 and more:
                        queries1(i + 1)
                    act.wait_ge(s_mx, 2 * i + s + 1 + 2 * NP)
                    for n in range(H1):
                        ex = act.activation(p1[s][0:R, head_at(n), :], sm[s][0:R, n, :], ACT.Exp, bias=nmx[s][0:R, n:n + 1],
                                            accum_out=den[s][0:R, head_at(n):head_at(n) + 1])
                    ex.then_inc(s_exp[s], 1)
                if more:
                    values1(i + 1, 0)
                for s in range(2):
                    act.wait_ge(s_cTp[s], i + 1)
                    act.copy(cT[s].rearrange("p (b m) r -> p b (m r)", b=2), turned[s][:, :, 0:3 * R]).then_inc(s_cT[s], 1)

            rows1(0)
            queries1(0)
            values1(0, 0)
            with act.Fori(0, NP - 1) as i:
                attend1(i, True)
            attend1(NP - 1, False)
            row_sdev(act, 2)


            def router_rows1(i):
                for s in range(2):
                    act.wait_ge(s_xTp[1], i + 1 + 3 * NP)
                    act.wait_ge(s_lgp, 2 * i + 2 * NP)
                    if has_earlier(i):
                        act.wait_ge(s_xTa, 2 * i)
                    act.copy(xT[0:HW, :, s * R:(s + 1) * R],
                             bank[4][0:HW, s * PH:(s + 1) * PH].rearrange("p (k r) -> p k r", k=2)).then_inc(s_xT[s], 1)

            router_rows1(0)
            with act.Fori(1, NP) as i:
                router_rows1(i)
            for s in range(2):
                act.wait_ge(s_lg, 4 * NP)
            act.activation(sc1[0:R, :, :], lg1[0:R, :, :], ACT.Sigmoid).then_inc(s_sc, 1)
            use_tables(act, ACT.Silu, 4)
            act.wait_ge(s_w5, 11 * 16)

            def experts1(i):
                for m in range(FB1):
                    act.wait_ge(s_gp, FB1 * i + m + 1)
                    if m >= 2 or has_earlier(i):
                        act.wait_ge(s_hid, FB1 * i + m - 1)
                    act.activation(sg[m % 2][:, :], bank[m % 2][:, 0:PH], ACT.Silu,
                                   bias=bg_t[:, m:m + 1]).then_inc(s_sg, 1)
                    if m == 0:
                        act.wait_ge(s_weTp, 2 * i + 2 + 2 * NP)
                        act.copy(c1T[0:E1 + 1, :], bank[4][0:E1 + 1, 0:PH]).then_inc(s_weT, 1)

            experts1(0)
            with act.Fori(1, NP) as i:
                experts1(i)

        @block.vector
        def _(dve):
            dve.wait_ge(s_tokw, 5 * 16)
            for k in range(KB):
                dve.tensor_scalar(weff[0:KP, k, 0:D], tw[0:KP, k, 0, :], tg[0:KP, k, 0:1], None,
                                  ALU.mult).then_inc(s_weff, 1)
            for j in range(1, NS):
                for k in range(KB):
                    dve.wait_ge(s_weff, KB * (j - 1) + k + 1)
                    dve.scalar_tensor_tensor(weff[0:KP, k, 0:D], tw[0:KP, k, j, :], tg[0:KP, k, j:j + 1],
                                             weff[0:KP, k, 0:D], ALU.mult, ALU.add).then_inc(s_weff, 1)
            dve.wait_ge(s_bwrow_p, 1)
            dve.tensor_copy(bw_row[:, :], bank[0][0:1, 0:D]).then_inc(s_bwrow, 1)
            dve.wait_ge(s_bw_p, 1)
            dve.tensor_copy(csum[0:R, :], bank[1][0:R, 0:D]).then_inc(s_bw, 1)
            dve.tensor_copy(bw[0:R, :], bank[1][0:R, D:2 * D]).then_inc(s_bw, 1)
            dve.wait_ge(s_bw, 2)

            def embed(j, half):
                at = 6 * (XB // 2 * j + half)
                for s in range(2):
                    b = 2 * half + s
                    dve.wait_ge(s_emb[b], j + 1)
                    dve.tensor_scalar(nmu[s][0:R, :], bank[2 + b][0:R, D:D + 1], -1.0 / FULL, None, ALU.mult).then_inc(s_e1, 1)
                for s in range(2):
                    dve.wait_ge(s_e1, at + s + 1)
                    dve.tensor_tensor(m2[s][0:R, :], nmu[s][0:R, :], nmu[s][0:R, :], ALU.mult).then_inc(s_e1, 1)
                for s in range(2):
                    dve.wait_ge(s_e1, at + s + 3)
                    dve.scalar_tensor_tensor(evar[s][0:R, :], bank[2 + 2 * half + s][0:R, D + 1:D + 2], 1.0 / FULL,
                                             m2[s][0:R, :], ALU.mult, ALU.subtract).then_inc(s_e1, 1)
                for s in range(2):
                    b = 2 * half + s
                    dve.scalar_tensor_tensor(tmp[s][0:R, :], csum[0:R, :], nmu[s][0:R, :], bank[2 + b][0:R, 0:D],
                                             ALU.mult, ALU.add).then_inc(s_raw[b], 1)
                for s in range(2):
                    dve.wait_ge(s_er, 2 * (XB // 2 * j + half) + s + 1)
                    dve.reciprocal(erstd[s][0:R, :], edev[s][0:R, :]).then_inc(s_err, 1)
                for s in range(2):
                    b = 2 * half + s
                    dve.wait_ge(s_err, 2 * (XB // 2 * j + half) + s + 1)
                    dve.wait_ge(s_raw[b], j + 1)
                    dve.scalar_tensor_tensor(grp(h, XB * j + b), tmp[s][0:R, :], erstd[s][0:R, :], bw[0:R, :],
                                             ALU.mult, ALU.add).then_inc(s_h[s], 1)
                spread(dve, XB // 2 * j + half, 0, h, lambda s: dve.wait_ge(s_h[s], XB // 2 * j + half + 1))
                inverse(dve, XB // 2 * j + half, 0)
                keep_inverse(dve, XB // 2 * j + half, 0)

            with dve.Fori(0, NG // XB) as j:
                for half in range(XB // 2):
                    embed(j, half)
            for half in range(NG % XB // 2):
                embed(NG // XB, half)

            dve.wait_ge(s_mo[0], 6 * NP)
            dve.wait_ge(s_kept, NP)
            dve.wait_ge(s_w0, 13 * 16)
            dve.reciprocal(itemp[0:R, :], temp_t[0:R, :]).then_inc(s_sw, 1)
            dve.tensor_tensor(dselb[0:R, :], selb_t[0:R, 1:2], selb_t[0:R, 0:1], ALU.subtract).then_inc(s_sw, 1)
            dve.tensor_tensor(dselw[0:HW, :, :], selw_t[0:HW, :, 1:2], selw_t[0:HW, :, 0:1], ALU.subtract).then_inc(s_sw, 1)
            dve.tensor_scalar(hmaskq[0:HW, :], hmask[0:HW, :], float(D0) ** -0.5, None, ALU.mult)
            dve.wait_ge(s_sw, 3)
            dve.tensor_scalar(bz[0:R, :], dselb[0:R, :], itemp[0:R, :], None, ALU.mult).then_inc(s_sw, 1)
            dve.tensor_scalar(wz[0:HW, :, :], dselw[0:HW, :, :].broadcast_to([HW, 2, R]), itemp[0:HW, :], None,
                              ALU.mult).then_inc(s_sw, 1)
            dve.wait_ge(s_sw, 5)

            def add_rows0(i):
                for s in range(2):
                    dve.wait_ge(s_xn[s], i + 1)
                    dve.tensor_tensor(grp(h, 2 * i + s), grp(h, 2 * i + s), xn[s][0:R, :], ALU.add).then_inc(s_hx, 1)

            def select0(i):
                for s in range(2):
                    dve.wait_ge(s_zp, 2 * i + s + 1)
                    dve.tensor_scalar(zr[s][0:R, :], bank[4 * s + 1][0:R, 0:R], bz[0:R, :], None,
                                      ALU.add).then_inc(s_zr, 1)
                for s in range(2):
                    dve.wait_ge(s_zr, 2 * i + s + 1)
                    if has_earlier(i):
                        dve.wait_ge(s_ez, 2 * i)
                    dve.scalar_tensor_tensor(junk[s][0:R, 0, :], zr[s][0:R, :], 1.0, ident[0:R, 0:R], ALU.mult, ALU.mult,
                                             accum_out=zc[s][0:R, :]).then_inc(s_zc, 1)
                for s in range(2):
                    dve.wait_ge(s_zc, 2 * i + s + 1)
                    dve.scalar_tensor_tensor(junk[s][0:R, 1, :], zr[s][0:R, :], zc[s][0:R, :], later[0:R, :], ALU.is_gt,
                                             ALU.mult, accum_out=rka[s][0:R, :]).then_inc(s_rk, 1)
                    dve.scalar_tensor_tensor(junk[s][0:R, 2, :], zr[s][0:R, :], zc[s][0:R, :], earlier[0:R, :], ALU.is_ge,
                                             ALU.mult, accum_out=rkb[s][0:R, :]).then_inc(s_rk, 1)
                for s in range(2):
                    dve.wait_ge(s_rk, 4 * i + 2 * s + 2)
                    if has_earlier(i):
                        dve.wait_ge(s_sp[s], i)
                    dve.tensor_scalar(psel[s][0:R, :], rtab[0:R, :], rka[s][0:R, :], rkb[s][0:R, :], ALU.subtract,
                                      ALU.is_equal).then_inc(s_psel, 1)

            def attend0(i, more):
                for s in range(2):
                    dve.wait_ge(s_vp[s], i + 1)
                    dve.tensor_tensor(v0[s][0:R, :], bank[4 * s + 2][0:R, 0:D], bv_t[0:R, :], ALU.add).then_inc(s_v[s], 1)
                for s in range(2):
                    dve.wait_ge(s_xsp, 2 * i + s + 1)
                    dve.tensor_copy(xs[s][0:HW, :, :], bank[4 * s + 1][0:HW, R:R + 2 * QG].rearrange("p (k q) -> p k q", k=2)
                                    ).then_inc(s_xs, 1)
                for s in range(2):
                    dve.wait_ge(s_qp, 2 * i + s + 1)
                    for hh in range(2):
                        q = bank[4 * s + 1][0:HW, 256 + hh * QG:256 + (hh + 1) * QG]
                        dve.scalar_tensor_tensor(qb[s][0:HW, hh, :].rearrange("p (j q) -> p j q", j=HH),
                                                 q.unsqueeze(1).broadcast_to([HW, HH, QG]), bqk_t[0:HW, hh:hh + 1],
                                                 hmaskq[0:HW, :].rearrange("p (j q) -> p j q", j=HH),
                                                 ALU.add, ALU.mult).then_inc(s_qb[s], 1)
                if more:
                    rows_of(dve, i + 1, lambda s: dve.wait_ge(s_xsp, 2 * i + 2))
                for s in range(2):
                    dve.wait_ge(s_sp[s], i + 1)
                    dve.tensor_reduce(nmx[s][0:R, 0:2], bank[4 * s + 2][0:R, D:D + PH].rearrange("p (k r) -> p k r", k=2),
                                      AX, ALU.max, negate=True).then_inc(s_mx, 1)
                if more:
                    add_rows0(i + 1)
                for s in range(2):
                    dve.wait_ge(s_ez, 2 * i + s + 1)
                    dve.tensor_scalar(ez1[s][0:R, :], ez[s][0:R, :], 1.0, None, ALU.add).then_inc(s_ez1, 1)
                for s in range(2):
                    dve.wait_ge(s_ez1, 2 * i + s + 1)
                    dve.reciprocal(sig[s][0:R, :], ez1[s][0:R, :]).then_inc(s_sig, 1)
                for s in range(2):
                    dve.wait_ge(s_exp[s], i + 1)
                    dve.reciprocal(rden[s][0:R, 0:2], den[s][0:R, 0:2]).then_inc(s_rd, 1)
                for s in range(2):
                    dve.wait_ge(s_rd, 2 * i + s + 1)
                    dve.tensor_tensor(pn[s][0:R, :, :], p0[s][0:R, :, :],
                                      rden[s][0:R, 0:2].unsqueeze(2).broadcast_to([R, 2, R]), ALU.mult).then_inc(s_pn, 1)
                if more:
                    select0(i + 1)
                for s in range(2):
                    dve.wait_ge(s_op[s], i + 1)
                    dve.tensor_tensor(om[s][0:HW, :, :], bank[4 * s + 3][0:HW, 0:PH].rearrange("p (k r) -> p k r", k=2),
                                      hmask[0:HW, :].unsqueeze(1).broadcast_to([HW, 2, R]), ALU.mult).then_inc(s_om, 1)
                for s in range(2):
                    dve.wait_ge(s_om, 2 * i + s + 1)
                    dve.tensor_reduce(ct0[s][0:HW, :, :], om[s][0:HW, :, :].rearrange("p k (j q) -> p k q j", j=HH), AX,
                                      ALU.add).then_inc(s_ct[s], 1)
                for s in range(2):
                    dve.wait_ge(s_ap[s], i + 1)
                    dve.tensor_tensor(at0[s][0:QG, :], bank[4 * s + 3][0:QG, 0:D], bo_t[0:QG, :], ALU.add).then_inc(s_at, 1)
                for s in range(2):
                    dve.wait_ge(s_sig, 2 * i + s + 1)
                    dve.wait_ge(s_up, 2 * i + s + 1)
                    dve.wait_ge(s_hx, 2 * i + s + 1)
                    dve.scalar_tensor_tensor(grp(h, 2 * i + s), bank[4 * s + 3][0:R, D:2 * D], sig[s][0:R, :],
                                             grp(h, 2 * i + s), ALU.mult, ALU.add).then_inc(s_h[s], 1)
                for s in range(2):
                    dve.wait_ge(s_bw, 2)
                    dve.wait_ge(s_h[s], i + 1 + NP)
                    dve.bn_stats(grp(st6, 2 * i + s, 6), grp(h, 2 * i + s)).then_inc(s_bn[s], 1)

            rows_of(dve, 0, lambda s: None)
            add_rows0(0)
            select0(0)
            with dve.Fori(0, NP - 1) as i:
                attend0(i, True)
            attend0(NP - 1, False)
            row_stats(dve, 1)

            dve.wait_ge(s_w3, 10 * 16)

            def rows0(i):
                def free(s):
                    dve.wait_ge(s_xTp[s], i + NP)
                rows_of(dve, i, free)
                for s in range(2):
                    dve.tensor_scalar(grp(acc, 2 * i + s), grp(h, 2 * i + s), col(mean, 2 * i + s), col(rstd, 2 * i + s),
                                      ALU.subtract, ALU.mult).then_inc(s_rows, 1)

            def logits0(i):
                for s in range(2):
                    dve.wait_ge(s_lgp, 2 * i + s + 1)
                    dve.tensor_tensor(grp(lg, 2 * i + s, E0), bank[4 * s + 1][0:R, 0:E0], rtb_t[0:R, :],
                                      ALU.add).then_inc(s_lg, 1)

            rows0(0)
            rows0(1)
            with dve.Fori(0, NP - 2) as i:
                rows0(i + 2)
                logits0(i)
            logits0(NP - 2)
            logits0(NP - 1)
            for s in range(2):
                dve.wait_ge(s_lg, 2 * NP)
            left = lg
            for k in range(K0):
                at = 6 * k
                if k:
                    dve.wait_ge(s_rt, at - 1)
                    left = left0
                    dve.scalar_tensor_tensor(left0[0:R, :, :], eq[0][0:R, :, :], PICKED, lg[0:R, :, :], ALU.mult,
                                             ALU.add).then_inc(s_rt, 1)
                    dve.wait_ge(s_rt, at)
                dve.tensor_reduce(top[k][0:R, :], left[0:R, :, :], AX, ALU.max).then_inc(s_rt, 1)
                dve.wait_ge(s_rt, at + 1)
                dve.tensor_tensor(eql[0][0:R, :, :], left[0:R, :, :], top[k][0:R, :].unsqueeze(2).broadcast_to([R, NG, E0]),
                                  ALU.is_equal).then_inc(s_rt, 1)
                dve.wait_ge(s_rt, at + 2)
                dve.tensor_tensor(eql[1][0:R, :, :], eql[0][0:R, :, :], order0[0:R, :].unsqueeze(1).broadcast_to([R, NG, E0]),
                                  ALU.mult).then_inc(s_rt, 1)
                dve.wait_ge(s_rt, at + 3)
                dve.tensor_reduce(best0[0:R, :], eql[1][0:R, :, :], AX, ALU.max).then_inc(s_rt, 1)
                dve.wait_ge(s_rt, at + 4)
                dve.tensor_tensor(eq[k][0:R, :, :], eql[1][0:R, :, :], best0[0:R, :].unsqueeze(2).broadcast_to([R, NG, E0]),
                                  ALU.is_equal).then_inc(s_rt, 1)
            dve.wait_ge(s_rt, 11)
            dve.tensor_tensor(chosen[0:R, :, :], eq[0][0:R, :, :], eq[1][0:R, :, :], ALU.add).then_inc(s_chosen, 1)
            dve.tensor_tensor(gap[0:R, :], top[1][0:R, :], top[0][0:R, :], ALU.subtract).then_inc(s_rt, 1)
            dve.wait_ge(s_eg, 1)
            dve.tensor_scalar(egap1[0:R, :], egap[0:R, :], 1.0, None, ALU.add).then_inc(s_rt, 1)
            dve.wait_ge(s_rt, 13)
            dve.reciprocal(gw[0][0:R, :], egap1[0:R, :]).then_inc(s_rt, 1)
            dve.wait_ge(s_rt, 14)
            dve.tensor_tensor(gw[1][0:R, :], egap[0:R, :], gw[0][0:R, :], ALU.mult).then_inc(s_rt, 1)
            dve.wait_ge(s_rt, 15)
            for k in range(2):
                dve.tensor_tensor(eql[k][0:R, :, :], eq[k][0:R, :, :],
                                  gw[k][0:R, :].unsqueeze(2).broadcast_to([R, NG, E0]), ALU.mult).then_inc(s_rt, 1)
            dve.wait_ge(s_rt, 17)
            dve.tensor_tensor(we[0:R, :, :], eql[0][0:R, :, :], eql[1][0:R, :, :], ALU.add).then_inc(s_rt, 1)
            dve.wait_ge(s_rt, RT_END)
            dve.wait_ge(s_cntp, 2)
            dve.tensor_reduce(count[:, :], bank[1][:, 0:NG * E0].rearrange("p (g e) -> p e g", g=NG), AX, ALU.add
                              ).then_inc(s_pos, 1)
            dve.wait_ge(s_pos, 1)
            dve.tensor_tensor(tcmp[:, :, :], count[:, :].unsqueeze(2).broadcast_to([TS, E0, NTH]),
                              thr[:, :].unsqueeze(1).broadcast_to([TS, E0, NTH]), ALU.is_gt).then_inc(s_pos, 1)
            dve.wait_ge(s_pos, 2)
            dve.tensor_reduce(tiles[:, :], tcmp[:, :, :], AX, ALU.add).then_inc(s_pos, 1)
            dve.wait_ge(s_pos, 3)
            dve.tensor_tensor(bcmp[:, :, :], tiles[:, :].unsqueeze(1).broadcast_to([TS, E0, E0]), below[:, :, :], ALU.mult
                              ).then_inc(s_pos, 1)
            dve.wait_ge(s_pos, 4)
            dve.tensor_reduce(first[:, :], bcmp[:, :, :], AX, ALU.add).then_inc(s_pos, 1)
            dve.wait_ge(s_pos, 5)
            dve.tensor_scalar(frow[:, :], first[:, :], float(TS), None, ALU.mult).then_inc(s_pos, 1)
            dve.wait_ge(s_pos, 6)
            dve.tensor_tensor(place[0:R, :, :], bank[0][0:R, 0:NG * E0].rearrange("p (g e) -> p g e", g=NG),
                              frow[0:R, :].unsqueeze(1).broadcast_to([R, NG, E0]), ALU.add).then_inc(s_pos, 1)
            for k in range(K0):
                dve.wait_ge(s_pos, 7 + 3 * k)
                dve.tensor_tensor(pcmp[0:R, :, :], place[0:R, :, :], eq[k][0:R, :, :], ALU.mult).then_inc(s_pos, 1)
                dve.wait_ge(s_pos, 8 + 3 * k)
                dve.tensor_reduce(posf[k][0:R, :], pcmp[0:R, :, :], AX, ALU.add).then_inc(s_pos, 1)
                dve.wait_ge(s_pos, 9 + 3 * k)
                dve.tensor_copy(pos[k][0:R, :], posf[k][0:R, :]).then_inc(s_pos, 1)
            dve.tensor_tensor(ecmp[0:1, :, :], first[0:1, 1:E0].unsqueeze(1).broadcast_to([1, NT, E0 - 1]),
                              tile_n[0:1, :].unsqueeze(2).broadcast_to([1, NT, E0 - 1]), ALU.is_le).then_inc(s_etab, 1)
            dve.wait_ge(s_etab, 1)
            dve.tensor_reduce(etabf[0:1, :], ecmp[0:1, :, :], AX, ALU.add).then_inc(s_etab, 1)
            dve.wait_ge(s_etab, 2)
            dve.tensor_copy(etab[0:1, :], etabf[0:1, :]).then_inc(s_etab, 1)

            def tile_x(t):
                dve.wait_ge(s_tTp, t + 1)
                dve.tensor_copy(xtT[0:HW, :, :], bank[0][0:HW, 0:2 * TS].rearrange("p (k r) -> p k r", k=2)).then_inc(s_tT, 1)

            def tile_h(t):
                dve.wait_ge(s_hTp, t + 1)
                dve.tensor_copy(hTt.rearrange("p (b m) r -> p b (m r)", b=2), ps[:, 3:5, 0:3 * TS]).then_inc(s_hT, 1)

            def tile_y(t, s, stores):
                dve.wait_ge(s_yp, t + 1)
                if stores is not None:
                    dve.wait_ge(s_yst[s], 16 * stores)
                dve.tensor_copy(yt[s][:, :], bank[5][:, 0:D]).then_inc(s_yt, 1)

            tile_x(0)
            tile_x(1)
            for t in range(2):
                tile_h(t)
                tile_y(t, t, None)
                tile_x(t + 2)
            with dve.Fori(1, NT // 2 - 1) as i:
                for s in range(2):
                    tile_h(2 * i + s)
                    tile_y(2 * i + s, s, i)
                    tile_x(2 * i + s + 2)
            tile_h(NT - 3)
            tile_y(NT - 3, 0, (NT - 3) // 2)
            tile_x(NT - 1)
            for t in (NT - 2, NT - 1):
                tile_h(t)
                tile_y(t, t % 2, t // 2)

            dve.wait_ge(s_rows, 2 * NP)

            def combine(i):
                for s in range(2):
                    dve.wait_ge(s_b2p, 2 * i + s + 1)
                    dve.wait_ge(s_yg[s], 16 * K0 * i + 16 * K0)
                    dve.scalar_tensor_tensor(y2[s][0:R, :], yg[0][s][0:R, :], col(gw[0], 2 * i + s), bank[4 * s + 1][0:R, 0:D],
                                             ALU.mult, ALU.add).then_inc(s_yadd, 1)
                for s in range(2):
                    dve.wait_ge(s_yadd, 2 * i + s + 1)
                    dve.scalar_tensor_tensor(grp(acc, 2 * i + s), yg[1][s][0:R, :], col(gw[1], 2 * i + s), y2[s][0:R, :],
                                             ALU.mult, ALU.add).then_inc(s_y2, 1)
                spread(dve, i, 1, acc, lambda s: dve.wait_ge(s_y2, 2 * i + s + 1))
                dve.wait_ge(s_mo[0], 6 * i + (6 * NP + 6))
                for s in range(2):
                    dve.scalar_tensor_tensor(z1[s][0:R, :], grp(acc, 2 * i + s), col(mean, 2 * i + s), gam_t[0:R, :],
                                             ALU.subtract, ALU.mult).then_inc(s_z1, 1)
                if has_earlier(i):
                    inverse(dve, i - 1, 2)
                inverse(dve, i, 1)
                for s in range(2):
                    dve.wait_ge(s_z1, 2 * i + s + 1)
                    dve.wait_ge(s_rs[0], i + 1 + NP)
                    dve.scalar_tensor_tensor(z3[s][0:R, :], z1[s][0:R, :], prs[0][0:R, s:s + 1], bet_t[0:R, :], ALU.mult,
                                             ALU.add).then_inc(s_z3, 1)
                for s in range(2):
                    dve.wait_ge(s_z3, 2 * i + s + 1)
                    dve.tensor_tensor(grp(h, 2 * i + s), grp(h, 2 * i + s), z3[s][0:R, :], ALU.add).then_inc(s_h[s], 1)
                if has_earlier(i):
                    dve.wait_ge(s_h[0], i + 1 + 2 * NP)
                    keep_inverse(dve, i - 1, 2)
                spread(dve, i, 2, h, lambda s: dve.wait_ge(s_h[s], i + 1 + 2 * NP))

            combine(0)
            with dve.Fori(1, NP) as i:
                combine(i)
            inverse(dve, NP - 1, 2)
            keep_inverse(dve, NP - 1, 2)
            dve.wait_ge(s_mo[1], 6 * NP)
            dve.wait_ge(s_kept, 2 * NP)

            for c in range(2):
                for half in range(2):
                    dve.memset(qscale[half * D1:(half + 1) * D1, c:c + 1], float(D1) ** -0.5 if c == half else 0.0
                                ).then_inc(s_qs, 1)
            dve.wait_ge(s_w4, 3 * 16)

            def rows1(i):
                rows_of(dve, i, lambda s: dve.wait_ge(s_xTp[s], i + 2 * NP))

            def keys1(i):
                for n in range(3, 6):
                    dve.wait_ge(s_qkp, 6 * i + n + 1)
                    dve.tensor_copy(k1T[:, 2 * n - 6:2 * n - 4, :],
                                    bank[2 + n][:, 0:2 * PH].rearrange("p (m r) -> p m r", m=2)).then_inc(s_kc, 1)

            def attend1(i, more):
                if more:
                    rows1(i + 1)
                for s in range(2):
                    dve.wait_ge(s_sp[s], i + 1 + NP)
                    dve.tensor_tensor(sm[s][0:R, :, :].rearrange("p (b j) r -> p b j r", b=4),
                                      ps[0:R, 0:4, 0:3 * R].rearrange("p b (j r) -> p b j r", j=3),
                                      bmask[0:R, :].unsqueeze(1).unsqueeze(1).broadcast_to([R, 4, 3, R]),
                                      ALU.add).then_inc(s_sm[s], 1)
                    dve.wait_ge(s_sm[s], i + 1)
                    dve.tensor_reduce(nmx[s][0:R, :], sm[s][0:R, :, :], AX, ALU.max, negate=True).then_inc(s_mx, 1)
                if more:
                    keys1(i + 1)
                for s in range(2):
                    dve.wait_ge(s_exp[s], i + 1 + NP)
                    dve.reciprocal(rden[s][0:R, :], den[s][0:R, :]).then_inc(s_rd, 1)
                    for b in range(3):
                        dve.wait_ge(s_pt1p, 6 * i + 3 * s + b + 1)
                        dve.tensor_copy(pt1[s][0:R, 4 * b:4 * b + 4, :],
                                        bank[5 + b][0:R, 0:4 * R].rearrange("p (n r) -> p n r", n=4)).then_inc(s_pt1, 1)
                    dve.wait_ge(s_rd, 2 * i + s + 1 + 2 * NP)
                    dve.wait_ge(s_op[s], i + 1 + NP)
                    dve.tensor_tensor(cx[s][0:R, :].rearrange("p (b j d) -> p b j d", b=2, j=H1 // 2),
                                      ps[0:R, 0:2, 0:A1 // 2].rearrange("p b (j d) -> p b j d", j=H1 // 2),
                                      rden[s][0:R, :].rearrange("p (b j) -> p b j", b=2).unsqueeze(3)
                                      .broadcast_to([R, 2, H1 // 2, D1]), ALU.mult).then_inc(s_ct[s], 1)
                for s in range(2):
                    dve.wait_ge(s_bw, 2)
                    dve.wait_ge(s_ap[s], i + 1 + NP)
                    dve.tensor_tensor(grp(h, 2 * i + s), attended[s][0:R, 0:D], grp(h, 2 * i + s),
                                      ALU.add).then_inc(s_h[s], 1)
                for s in range(2):
                    dve.wait_ge(s_bw, 2)
                    dve.wait_ge(s_h[s], i + 1 + 3 * NP)
                    dve.bn_stats(grp(st6, 2 * i + s, 6), grp(h, 2 * i + s)).then_inc(s_bn[s], 1)

            rows1(0)
            keys1(0)
            with dve.Fori(0, NP - 1) as i:
                attend1(i, True)
            attend1(NP - 1, False)
            row_stats(dve, 2)

            dve.wait_ge(s_w5, 11 * 16)

            def rows5(i):
                rows_of(dve, i, lambda s: dve.wait_ge(s_xTp[s], i + 3 * NP))

            def logits1(i):
                for s in range(2):
                    dve.wait_ge(s_lgp, 2 * i + s + 1 + 2 * NP)
                    dve.tensor_tensor(grp(lg1, 2 * i + s, E1), bank[5 + s][0:R, 0:E1], rt1b_t[0:R, :],
                                      ALU.add).then_inc(s_lg, 1)

            rows5(0)
            rows5(1)
            with dve.Fori(0, NP - 2) as i:
                rows5(i + 2)
                logits1(i)
            logits1(NP - 2)
            logits1(NP - 1)
            dve.wait_ge(s_sc, 1)
            dve.tensor_tensor(sfc[0:R, :, :], sc1[0:R, :, :], corr_t[0:R, :].unsqueeze(1).broadcast_to([R, NG, E1]),
                              ALU.add).then_inc(s_r5, 1)
            dve.wait_ge(s_r5, 1)
            s4 = sfc[0:R, :, :].rearrange("p g (c e) -> p (g c) e", e=GE)
            for d, o in ((1, 0), (2, 3), (3, 5)):
                dve.tensor_tensor(psum1[0:R, :, o:o + GE - d], s4[:, :, 0:GE - d], s4[:, :, d:GE], ALU.add).then_inc(s_r5, 1)
            dve.wait_ge(s_r5, 4)
            dve.tensor_reduce(gtop[0:R, :, :], psum1[0:R, :, :].rearrange("p (g c) e -> p g c e", g=NG), AX,
                              ALU.max).then_inc(s_r5, 1)

            def ranks(val, cmp, tri, rank, n, at):
                c = cmp[0:R, :, :].rearrange("p g (e w j) -> p g e w j", e=n, w=2)
                mine = val[0:R, :, :].unsqueeze(3).broadcast_to([R, NG, n, n])
                other = val[0:R, :, :].unsqueeze(2).broadcast_to([R, NG, n, n])
                dve.wait_ge(s_r5, at)
                dve.tensor_tensor(c[:, :, :, 0, :], other, mine, ALU.is_gt).then_inc(s_r5, 1)
                dve.tensor_tensor(c[:, :, :, 1, :], other, mine, ALU.is_ge).then_inc(s_r5, 1)
                dve.wait_ge(s_r5, at + 2)
                dve.tensor_tensor(cmp[0:R, :, :], cmp[0:R, :, :], tri[0:R, :].unsqueeze(1).broadcast_to([R, NG, 2 * n * n]),
                                  ALU.mult).then_inc(s_r5, 1)
                dve.wait_ge(s_r5, at + 3)
                dve.tensor_reduce(rank[0:R, :, :], cmp[0:R, :, :].rearrange("p g (e w) -> p g e w", e=n), AX,
                                  ALU.add).then_inc(s_r5, 1)
                dve.wait_ge(s_r5, at + 4)

            ranks(gtop, gcmp, trig, grank, G1, 5)
            dve.scalar_tensor_tensor(skept[0:R, :, :].rearrange("p g (c e) -> p (g c) e", e=GE),
                                     grank[0:R, :, :].rearrange("p g c -> p (g c)").unsqueeze(2).broadcast_to([R, NG * G1, GE]),
                                     2.0, s4, ALU.is_lt, ALU.mult).then_inc(s_r5, 1)
            for k in range(K1):
                at = 10 + 6 * k
                dve.wait_ge(s_r5, at)
                dve.tensor_reduce(best[0][0:R, :], skept[0:R, :, :], AX, ALU.max).then_inc(s_r5, 1)
                dve.wait_ge(s_r5, at + 1)
                dve.tensor_tensor(pick[0][0:R, :, :], skept[0:R, :, :], best[0][0:R, :].unsqueeze(2).broadcast_to([R, NG, E1]),
                                  ALU.is_equal).then_inc(s_r5, 1)
                dve.wait_ge(s_r5, at + 2)
                dve.tensor_tensor(pick[1][0:R, :, :], pick[0][0:R, :, :], order[0:R, :].unsqueeze(1).broadcast_to([R, NG, E1]),
                                  ALU.mult).then_inc(s_r5, 1)
                dve.wait_ge(s_r5, at + 3)
                dve.tensor_reduce(best[1][0:R, :], pick[1][0:R, :, :], AX, ALU.max).then_inc(s_r5, 1)
                dve.wait_ge(s_r5, at + 4)
                dve.tensor_tensor(pick[0][0:R, :, :], pick[1][0:R, :, :], best[1][0:R, :].unsqueeze(2).broadcast_to([R, NG, E1]),
                                  ALU.is_equal).then_inc(s_r5, 1)
                dve.wait_ge(s_r5, at + 5)
                dve.scalar_tensor_tensor(skept[0:R, :, :], pick[0][0:R, :, :], PICKED, skept[0:R, :, :], ALU.mult,
                                         ALU.add).then_inc(s_r5, 1)
            dve.wait_ge(s_r5, R5_END - 5)
            dve.wait_ge(s_c1, 1)
            dve.scalar_tensor_tensor(sfc[0:R, :, :], skept[0:R, :, :], PICKED / 2, sc1[0:R, :, :], ALU.is_lt,
                                     ALU.mult).then_inc(s_r5, 1)
            dve.wait_ge(s_r5, R5_END - 4)
            dve.tensor_reduce(wsum[0:R, :], sfc[0:R, :, :], AX, ALU.add).then_inc(s_r5, 1)
            dve.wait_ge(s_r5, R5_END - 3)
            dve.tensor_scalar(wsum1[0:R, :], wsum[0:R, :], 1e-20, None, ALU.add).then_inc(s_r5, 1)
            dve.wait_ge(s_r5, R5_END - 2)
            dve.reciprocal(wrec[0:R, :], wsum1[0:R, :]).then_inc(s_r5, 1)
            dve.wait_ge(s_r5, R5_END - 1)
            dve.scalar_tensor_tensor(c1[0:R, :, 0:E1], sfc[0:R, :, :], SCALE1,
                                     wrec[0:R, :].unsqueeze(2).broadcast_to([R, NG, E1]), ALU.mult, ALU.mult).then_inc(s_r5, 1)
            dve.wait_ge(s_r5, R5_END)

            def weigh(i, m):
                dve.wait_ge(s_cb, FB1 * i + m + 1)
                dve.wait_ge(s_hid, FB1 * i + m + 1)
                dve.tensor_tensor(hidw[m % 2][:, :], bank[4 + m % 2][:, 0:PH],
                                  hid[m % 2][:, :], ALU.mult).then_inc(s_hw, 1)

            def finish(i):
                dve.wait_ge(s_sh, i + 1)
                for s in range(2):
                    if has_earlier(i):
                        dve.wait_ge(s_outs[s], 16 * i)
                    dve.tensor_tensor(oh[s][0:R, :], bank[6 + s][0:R, 0:D], grp(h, 2 * i + s), ALU.add).then_inc(s_oh, 1)

            def experts1(i, earlier):
                for m in range(FB1):
                    if m > 0:
                        weigh(i, m - 1)
                    elif earlier:
                        weigh(i - 1, FB1 - 1)
                    dve.wait_ge(s_sg, FB1 * i + m + 1)
                    dve.scalar_tensor_tensor(hid[m % 2][:, :], bank[2 + m % 2][:, 0:PH],
                                             bu_t[:, m:m + 1], sg[m % 2][:, :],
                                             ALU.add, ALU.mult).then_inc(s_hid, 1)
                    if m == 1 and earlier:
                        finish(i - 1)

            experts1(0, False)
            experts1(1, True)
            with dve.Fori(2, NP) as i:
                experts1(i, True)
            weigh(NP - 1, FB1 - 1)
            finish(NP - 1)

        @block.tensor
        def _(pe):
            pe.wait_ge(s_tokw, 5 * 16)
            pe.wait_ge(s_ones, 1)
            pe.matmul(bank[0][0:1, 0:D], ones[0:1, 0:1], tb_row[:, :], start=True, stop=False)
            for k in range(KB):
                for j in range(NS):
                    row = pe.matmul(bank[0][0:1, 0:D], tbe[0:KP, k, j:j + 1], tw[0:KP, k, j, :],
                                    start=False, stop=(k == KB - 1 and j == NS - 1))
            row.then_inc(s_bwrow_p, 1)
            pe.wait_ge(s_weff, KB * NS)
            pe.wait_ge(s_cnt, 1)
            for k in range(KB):
                pe.matmul(bank[1][0:R, 0:D], ones[0:KP, 0:R], weff[0:KP, k, 0:D], start=(k == 0), stop=(k == KB - 1))
            pe.wait_ge(s_bwrow, 1)
            pe.matmul(bank[1][0:R, D:2 * D], ones[0:1, 0:R], bw_row[:, :], start=True, stop=True).then_inc(s_bw_p, 1)

            def embed(j, b):
                pe.wait_ge(s_x[b], 16 * j + 16)
                if has_earlier(j):
                    pe.wait_ge(s_raw[b], j)
                for k in range(KB):
                    pe.matmul(bank[2 + b][0:R, 0:D + 1], xp[b][0:KP, k, :], weff[0:KP, k, :],
                              start=(k == 0), stop=(k == KB - 1))
                pe.wait_ge(s_xsq, XB * j + b + 1)
                for k in range(KB):
                    mm = pe.matmul(bank[2 + b][0:R, D + 1:D + 2], xsq[b][0:KP, k, :], weff[0:KP, k, D:D + 1],
                                   start=(k == 0), stop=(k == KB - 1))
                mm.then_inc(s_emb[b], 1)

            for b in range(XB):
                embed(0, b)
            with pe.Fori(1, NG // XB) as j:
                for b in range(XB):
                    embed(j, b)
            for b in range(NG % XB):
                embed(NG // XB, b)
            for b in range(XB):
                pe.wait_ge(s_raw[b], emb_count(b))

            pe.wait_ge(s_const, 16)
            pe.wait_ge(s_w0, 13 * 16)
            pe.wait_ge(s_sw, 5)

            def rows0(i):
                for s in range(2):
                    if has_earlier(i):
                        pe.wait_ge(s_kT, 2 * i)
                    pe.wait_ge(s_xn[s], i + 1)
                    for k in range(2):
                        tr = pe.transpose(bank[4 * s][0:HW, k * R:(k + 1) * R], xn[s][0:R, k * HW:(k + 1) * HW],
                                          ident[0:R, 0:R])
                    tr.then_inc(s_xTp[s], 1)
                for s in range(2):
                    pe.wait_ge(s_xT[s], i + 1)
                    for k in range(2):
                        mm = pe.matmul(bank[4 * s + 1][0:R, 0:R], wz[0:HW, k, :], xT[0:HW, k, s * R:(s + 1) * R],
                                       start=(k == 0), stop=(k == 1))
                    mm.then_inc(s_zp, 1)
                for hh in range(2):
                    for k in range(2):
                        mm = pe.matmul(bank[0][0:HW, hh * PH:(hh + 1) * PH],
                                       wqkv_t[0:HW, k, D + hh * HW:D + (hh + 1) * HW], xT[0:HW, k, :],
                                       start=(k == 0), stop=(k == 1))
                mm.then_inc(s_kp, 1)

            def attend0(i, more):
                for s in range(2):
                    if has_earlier(i):
                        pe.wait_ge(s_exp[s], i)
                    for k in range(2):
                        mm = pe.matmul(bank[4 * s + 2][0:R, 0:D], xT[0:HW, k, s * R:(s + 1) * R],
                                       wqkv_t[0:HW, k, 2 * D:3 * D], start=(k == 0), stop=(k == 1))
                    mm.then_inc(s_vp[s], 1)
                for s in range(2):
                    pe.wait_ge(s_psel, 2 * i + s + 1)
                    pe.wait_ge(s_h[s], i + NP)
                    pe.transpose(bank[4 * s + 3][0:QG, 0:R], psel[s][0:R, 0:QG], ident[0:R, 0:R]).then_inc(s_ptp0, 1)
                    for k in range(2):
                        mm = pe.matmul(bank[4 * s + 1][0:HW, R + k * QG:R + (k + 1) * QG], xn[s][0:R, k * HW:(k + 1) * HW],
                                       psel[s][0:R, 0:QG], start=True, stop=True)
                    mm.then_inc(s_xsp, 1)
                for s in range(2):
                    pe.wait_ge(s_xs, 2 * i + s + 1)
                    for hh in range(2):
                        for k in range(2):
                            mm = pe.matmul(bank[4 * s + 1][0:HW, 256 + hh * QG:256 + (hh + 1) * QG],
                                           wqkv_t[0:HW, k, hh * HW:(hh + 1) * HW], xs[s][0:HW, k, :],
                                           start=(k == 0), stop=(k == 1))
                    mm.then_inc(s_qp, 1)
                for s in range(2):
                    pe.wait_ge(s_kT, 2 * i + 2)
                    pe.wait_ge(s_v[s], i + 1)
                    pe.wait_ge(s_qb[s], 2 * i + 2)
                    for hh in range(2):
                        o = bank[4 * s + 2][0:R, D + hh * R:D + (hh + 1) * R]
                        pe.matmul(o, psel[s][0:R, :], cmask[0:R, :], start=True, stop=False)
                        mm = pe.matmul(o, qb[s][0:HW, hh, :], kT[0:HW, hh, s * R:(s + 1) * R], start=False, stop=True)
                    mm.then_inc(s_sp[s], 1)
                if more:
                    rows0(i + 1)
                for s in range(2):
                    pe.wait_ge(s_pselT, 2 * i + s + 1)
                    pe.wait_ge(s_pn, 2 * i + s + 1)
                    for hh in range(2):
                        tr = pe.transpose(bank[4 * s + 3][0:R, hh * R:(hh + 1) * R], pn[s][0:R, hh, :], ident[0:R, 0:R])
                    tr.then_inc(s_ptp[s], 1)
                for s in range(2):
                    pe.wait_ge(s_pt[s], i + 1)
                    for hh in range(2):
                        mm = pe.matmul(bank[4 * s + 3][0:HW, hh * R:(hh + 1) * R], v0[s][0:R, hh * HW:(hh + 1) * HW],
                                       pt0[s][0:R, hh, :], start=True, stop=True)
                    mm.then_inc(s_op[s], 1)
                for s in range(2):
                    pe.wait_ge(s_ct[s], i + 1)
                    for hh in range(2):
                        mm = pe.matmul(bank[4 * s + 3][0:QG, 0:D], ct0[s][0:HW, hh, :], wo_t[0:HW, hh, :],
                                       start=(hh == 0), stop=(hh == 1))
                    mm.then_inc(s_ap[s], 1)
                for s in range(2):
                    pe.wait_ge(s_at, 2 * i + s + 1)
                    pe.matmul(bank[4 * s + 3][0:R, D:2 * D], pselT[s][0:QG, :], at0[s][0:QG, :], start=True,
                              stop=True).then_inc(s_up, 1)

            rows0(0)
            attend0(0, True)
            with pe.Fori(1, NP - 1) as i:
                attend0(i, True)
            attend0(NP - 1, False)
            for s in range(2):
                pe.wait_ge(s_h[s], 2 * NP)

            pe.wait_ge(s_w3, 10 * 16)

            def turn0(i):
                for s in range(2):
                    pe.wait_ge(s_xT[s], i + NP)
                    pe.wait_ge(s_xn[s], i + 1 + NP)
                    for k in range(2):
                        tr = pe.transpose(bank[4 * s][0:HW, k * R:(k + 1) * R], xn[s][0:R, k * HW:(k + 1) * HW],
                                          ident[0:R, 0:R])
                    tr.then_inc(s_xTp[s], 1)

            def logits0(i):
                for s in range(2):
                    if has_earlier(i):
                        pe.wait_ge(s_lg, 2 * i)
                    pe.wait_ge(s_xT[s], i + 1 + NP)
                    for k in range(2):
                        mm = pe.matmul(bank[4 * s + 1][0:R, 0:E0], xT[0:HW, k, s * R:(s + 1) * R], rtw_t[0:HW, k, :],
                                       start=(k == 0), stop=(k == 1))
                    mm.then_inc(s_lgp, 1)

            turn0(0)
            turn0(1)
            logits0(0)
            with pe.Fori(1, NP - 1) as i:
                turn0(i + 1)
                logits0(i)
            logits0(NP - 1)
            for s in range(2):
                pe.wait_ge(s_xT[s], 2 * NP)
                pe.wait_ge(s_lg, 2 * NP)
            pe.wait_ge(s_chosen, 1)
            ch = chosen[0:R, :, :].rearrange("p g e -> p (g e)")
            pe.matmul(bank[0][0:R, 0:NG * E0], before[0:R, :], ch, start=True, stop=False)
            for d in range(1, NG):
                mm = pe.matmul(bank[0][0:R, d * E0:NG * E0], ones[0:R, 0:R], ch[:, 0:(NG - d) * E0], start=False,
                               stop=(d == NG - 1))
            mm.then_inc(s_cntp, 1)
            pe.matmul(bank[1][:, 0:NG * E0], ones[0:R, :], ch, start=True, stop=True).then_inc(s_cntp, 1)

            for k, w in enumerate((s_w1, s_w2)):
                pe.wait_ge(w, 16 * (E0 + 1 - k))
            pe.wait_ge(s_z, 2)
            pe.wait_ge(s_pos, POS_END)
            pe.wait_ge(s_etab, 3)

            def expert_of(t):
                return pe.value_load(etab[0:1, bass.ds(t, 1)], min_val=0, max_val=E0 - 1)

            def rows_in(s, loads):
                for k in range(2):
                    tr = pe.transpose(bank[0][0:HW, k * TS:(k + 1) * TS], xin[s][:, k * HW:(k + 1) * HW], ident[:, :])
                tr.then_inc(s_tTp, 1)

            def hidden(t):
                pe.wait_ge(s_tT, t + 1)
                e = expert_of(t)
                for b in range(2):
                    for k in range(2):
                        mm = pe.matmul(bank[1 + b][:, 0:F0 // 2], xtT[0:HW + k, k, :],
                                       w1_t[0:HW + k, :, :, :].rearrange("p e k f -> p (e k f)")
                                       [:, bass.ds(e * (2 * F0) + (k * F0 + b * (F0 // 2)), F0 // 2)],
                                       start=(k == 0), stop=(k == 1))
                mm.then_inc(s_hp, 1)

            def turn_hidden(t):
                pe.wait_ge(s_hg, t + 1)
                for m in range(FB0):
                    tr = pe.transpose(bank[3 + m // 3][:, (m % 3) * TS:(m % 3 + 1) * TS], hg[:, m * 128:(m + 1) * 128], ident[:, :])
                tr.then_inc(s_hTp, 1)

            def output(t):
                e = expert_of(t)
                pe.wait_ge(s_hT, t + 1)
                if has_earlier(t):
                    pe.wait_ge(s_yt, t)
                for m in range(FB0):
                    mm = pe.matmul(bank[5][:, 0:D], hTt[:, m, :],
                                   w2_t[:, :, :, :].rearrange("p e m d -> p (e m d)")[:, bass.ds(e * (FB0 * D) + m * D, D)],
                                   start=(m == 0), stop=(m == FB0 - 1))
                mm.then_inc(s_yp, 1)

            def step(t, s, loads, more):
                turn_hidden(t - 1)
                hidden(t)
                output(t - 1)
                if more:
                    pe.wait_ge(s_xin[1 - s], 16 * loads)
                    rows_in(1 - s, loads)

            pe.wait_ge(s_xin[0], 16)
            rows_in(0, 1)
            hidden(0)
            pe.wait_ge(s_xin[1], 16)
            rows_in(1, 1)
            step(1, 1, 2, True)
            step(2, 0, 2, True)
            with pe.Fori(1, NT // 2 - 1) as i:
                step(2 * i + 1, 1, i + 2, True)
                step(2 * i + 2, 0, i + 2, True)
            step(NT - 2, 1, NT // 2 + 1, True)
            step(NT - 1, 0, 0, False)
            turn_hidden(NT - 1)
            output(NT - 1)
            pe.wait_ge(s_yt, NT)

            def biases0(i):
                for s in range(2):
                    if has_earlier(i):
                        pe.wait_ge(s_weT, 2 * i)
                    pe.wait_ge(s_wes, 2 * i + s + 1)
                    pe.transpose(bank[4 * s][0:E0, 0:R], wes[s][0:R, :], ident[0:R, 0:R]).then_inc(s_weTp, 1)
                for s in range(2):
                    if has_earlier(i):
                        pe.wait_ge(s_yadd, 2 * i)
                    pe.wait_ge(s_weT, 2 * i + s + 1)
                    pe.matmul(bank[4 * s + 1][0:R, 0:D], weT[s][0:E0, :], b2_t[0:E0, :], start=True, stop=False)
                    pe.matmul(bank[4 * s + 1][0:R, 0:D], ident[0:R, 0:R], grp(acc, 2 * i + s), start=False,
                              stop=True).then_inc(s_b2p, 1)

            pe.wait_ge(s_rows, 2 * NP)
            biases0(0)
            with pe.Fori(1, NP) as i:
                biases0(i)

            pe.wait_ge(s_w4, 3 * 16)
            pe.wait_ge(s_yadd, 2 * NP)

            def rows1(i):
                for s in range(2):
                    pe.wait_ge(s_h[0], i - 1 + 3 * NP)
                    pe.wait_ge(s_xn[s], i + 1 + 2 * NP)
                    for k in range(2):
                        tr = pe.transpose(bank[4][0:HW, s * PH + k * R:s * PH + (k + 1) * R], xn[s][0:R, k * HW:(k + 1) * HW],
                                          ident[0:R, 0:R])
                    tr.then_inc(s_xTp[s], 1)

            def queries_keys1(i):
                for s in range(2):
                    pe.wait_ge(s_xT[s], i + 1 + 2 * NP)
                for n in range(6):
                    if n >= 3:
                        pe.wait_ge(s_qc, 3 * i + n - 2)
                    for m in (2 * n, 2 * n + 1):
                        for k in range(2):
                            mm = pe.matmul(bank[5 + n % 3][:, (m % 2) * PH:(m % 2 + 1) * PH],
                                           w1qkv[0:HW, k, m * 128:(m + 1) * 128], xT[0:HW, k, :],
                                           start=(k == 0), stop=(k == 1))
                    mm.then_inc(s_qkp, 1)

            def values1(i, s):
                for b in range(2):
                    for k in range(2):
                        mm = pe.matmul(bank[5 + b][0:R, 0:A1 // 2], xT[0:HW, k, s * R:(s + 1) * R],
                                       w1qkv[0:HW, k, 2 * A1 + b * A1 // 2:2 * A1 + (b + 1) * A1 // 2],
                                       start=(k == 0), stop=(k == 1))
                mm.then_inc(s_vp[s], 1)

            def scores1(i, s):
                for n in range(H1):
                    hd = head_at(n)
                    mm = pe.matmul(bank[n // 3][0:R, (n % 3) * R:(n % 3 + 1) * R], qT[hd % 2][:, hd // 2, s * R:(s + 1) * R],
                                   k1T[:, hd // 2, s * R:(s + 1) * R], start=True, stop=True)
                mm.then_inc(s_sp[s], 1)

            def attend1(i, more):
                for s in range(2):
                    pe.wait_ge(s_ct[1], i + NP)
                    if has_earlier(i):
                        pe.wait_ge(s_cT[s], i)
                scores1(i, 0)
                pe.wait_ge(s_v[0], i + 1 + NP)
                pe.wait_ge(s_h[1], i + 3 * NP)
                values1(i, 1)
                if more:
                    rows1(i + 1)
                pe.wait_ge(s_sm[0], i + 1)
                scores1(i, 1)
                pe.wait_ge(s_v[1], i + 1 + NP)
                if more:
                    queries_keys1(i + 1)
                    pe.wait_ge(s_kc, 3 * i + 6)
                for s in range(2):
                    pe.wait_ge(s_exp[s], i + 1 + NP)
                    for b in range(3):
                        if s == 1:
                            pe.wait_ge(s_pt1, 6 * i + b + 1)
                        for n in range(4):
                            tr = pe.transpose(bank[5 + b][0:R, n * R:(n + 1) * R], p1[s][0:R, 4 * b + n, :], ident[0:R, 0:R])
                        tr.then_inc(s_pt1p, 1)
                    if s == 0:
                        pe.wait_ge(s_sm[1], i + 1)
                    else:
                        pe.wait_ge(s_ct[0], i + 1 + NP)
                    for n in range(H1):
                        if n % 4 == 0:
                            pe.wait_ge(s_pt1, 6 * i + 3 * s + n // 4 + 1)
                        mm = pe.matmul(bank[n // 6][0:R, (n % 6) * D1:(n % 6 + 1) * D1], pt1[s][0:R, n, :],
                                       v1[s][0:R, n * D1:(n + 1) * D1], start=True, stop=True)
                    mm.then_inc(s_op[s], 1)
                if more:
                    values1(i + 1, 0)
                for s in range(2):
                    pe.wait_ge(s_ct[s], i + 1 + NP)
                    for m in range(MB1):
                        tr = pe.transpose(turned[s][:, m // 3, (m % 3) * R:(m % 3 + 1) * R], cx[s][0:R, m * 128:(m + 1) * 128],
                                          ident[0:R, 0:R])
                    tr.then_inc(s_cTp[s], 1)
                for s in range(2):
                    pe.wait_ge(s_cT[s], i + 1)
                    if s == 1 and more:
                        pe.wait_ge(s_v[0], i + 2 + NP)
                    for m in range(MB1):
                        mm = pe.matmul(attended[s][0:R, 0:D], cT[s][:, m, :], wo1_t[:, m, :],
                                       start=(m == 0), stop=(m == MB1 - 1))
                    mm.then_inc(s_ap[s], 1)

            rows1(0)
            queries_keys1(0)
            pe.wait_ge(s_kc, 3)
            values1(0, 0)
            attend1(0, True)
            with pe.Fori(1, NP - 1) as i:
                attend1(i, True)
            attend1(NP - 1, False)
            for s in range(2):
                pe.wait_ge(s_h[s], 4 * NP)

            pe.wait_ge(s_w5, 11 * 16)
            pe.wait_ge(s_wgu, 2 * 16)

            def turn1(i):
                for s in range(2):
                    pe.wait_ge(s_xT[1], i + 3 * NP)
                    pe.wait_ge(s_xn[s], i + 1 + 3 * NP)
                    for k in range(2):
                        tr = pe.transpose(bank[4][0:HW, s * PH + k * R:s * PH + (k + 1) * R], xn[s][0:R, k * HW:(k + 1) * HW],
                                          ident[0:R, 0:R])
                    tr.then_inc(s_xTp[s], 1)

            def logits1(i):
                for s in range(2):
                    pe.wait_ge(s_lg, 2 * i + 2 * NP)
                    pe.wait_ge(s_xT[s], i + 1 + 3 * NP)
                    for k in range(2):
                        mm = pe.matmul(bank[5 + s][0:R, 0:E1], xT[0:HW, k, s * R:(s + 1) * R], rt1w_t[0:HW, k, :],
                                       start=(k == 0), stop=(k == 1))
                    mm.then_inc(s_lgp, 1)

            turn1(0)
            with pe.Fori(0, NP - 1) as i:
                turn1(i + 1)
                logits1(i)
            logits1(NP - 1)
            pe.wait_ge(s_xT[1], 4 * NP)
            pe.wait_ge(s_lg, 4 * NP)

            for s in range(2):
                pe.wait_ge(s_xTa, 2 * NP)

            def up(i, m):
                if m >= 2 or has_earlier(i):
                    pe.wait_ge(s_hid, FB1 * i + m - 1)
                for w, b in ((wg_t, 0), (wu_t, 2)):
                    for k in range(2):
                        mm = pe.matmul(bank[b + m % 2][:, 0:PH], w[0:HW, k, m * 128:(m + 1) * 128],
                                       xTall[0:HW, k, bass.ds(i * PH, PH)], start=(k == 0), stop=(k == 1))
                mm.then_inc(s_gp, 1)

            def spread_weights(i, m):
                if m >= 2 or has_earlier(i):
                    pe.wait_ge(s_hw, FB1 * i + m - 1)
                pe.matmul(bank[4 + m % 2][:, 0:PH], expert_of_hid[0:E1 + 1, m * 128:(m + 1) * 128],
                          c1T[0:E1 + 1, :], start=True, stop=True).then_inc(s_cb, 1)

            def down(i, m):
                pe.wait_ge(s_hw, FB1 * i + m + 1)
                for s in range(2):
                    mm = pe.matmul(bank[6 + s][0:R, 0:D], hidw[m % 2][:, s * R:(s + 1) * R],
                                   wd_t[:, m, :], start=False, stop=(m == FB1 - 1))
                if m == FB1 - 1:
                    mm.then_inc(s_sh, 1)

            def turn_weights(i):
                if has_earlier(i):
                    pe.wait_ge(s_hw, FB1 * i - 1)
                for s in range(2):
                    pe.wait_ge(s_wes, 2 * i + s + 1 + 2 * NP)
                    pe.transpose(bank[4][0:E1 + 1, s * R:(s + 1) * R], cs[s][0:R, :], ident[0:R, 0:R]).then_inc(s_weTp, 1)

            def experts1(i):
                earlier = has_earlier(i)
                up(i, 0)
                if earlier:
                    spread_weights(i - 1, FB1 - 1)
                    down(i - 1, FB1 - 2)
                turn_weights(i)
                up(i, 1)
                if earlier:
                    down(i - 1, FB1 - 1)
                pe.wait_ge(s_weT, i + 1 + 2 * NP)
                spread_weights(i, 0)
                up(i, 2)
                spread_weights(i, 1)
                if earlier:
                    pe.wait_ge(s_oh, 2 * i)
                for s in range(2):
                    pe.matmul(bank[6 + s][0:R, 0:D], c1T[0:E1 + 1, s * R:(s + 1) * R], bd_t[0:E1 + 1, :], start=True,
                              stop=False)
                down(i, 0)
                for m in range(3, FB1):
                    up(i, m)
                    spread_weights(i, m - 1)
                    down(i, m - 2)

            experts1(0)
            experts1(1)
            with pe.Fori(2, NP) as i:
                experts1(i)
            spread_weights(NP - 1, FB1 - 1)
            down(NP - 1, FB1 - 2)
            down(NP - 1, FB1 - 1)


def _parts(a):
    a = np.pad(a, [(0, KB * KP - FEAT)] + [(0, 0)] * (a.ndim - 1))
    return np.ascontiguousarray(a.reshape(KB, KP, *a.shape[1:]).swapaxes(0, 1))


def _patches(x):
    xh = np.zeros((NG * IPG, C_IN, SIDE + 2, SIDE + 2), np.float32)
    xh[:N_IMG, :, 1:-1, 1:-1] = x
    f = np.empty((C_IN, HALO, HALO, NG * IPG, GRID, GRID), np.float32)
    for a in range(HALO):
        for b in range(HALO):
            f[:, a, b] = xh[:, :, a:a + SIDE:PATCH, b:b + SIDE:PATCH].swapaxes(0, 1)
    f = _parts(f.reshape(FEAT, NG, R))
    return np.ascontiguousarray(f.transpose(2, 0, 1, 3)).reshape(NG, KP, KB * R)


def _shifted(w):
    w = np.asarray(w).reshape(PATCH, PATCH, NS, C_IN, -1)
    o = np.zeros((C_IN, HALO, HALO, NS, w.shape[-1]), np.float32)
    for j, (dy, dx) in enumerate(SHIFTS):
        o[:, 1 + dy:1 + dy + PATCH, 1 + dx:1 + dx + PATCH, j] = w[:, :, j].transpose(2, 0, 1, 3)
    return _parts(o.reshape(FEAT, NS, -1))


def _halves(w):
    w = np.asarray(w)
    return np.ascontiguousarray(w.reshape(2, HW, -1).swapaxes(0, 1))


def _blocks(w):
    w = np.pad(w, [(0, W1 - HID1)] + [(0, 0)] * (w.ndim - 1))
    return w.reshape(FB1, 128, *w.shape[1:]).swapaxes(0, 1)


def _tables():
    tok = np.arange(R)
    same = tok[:, None] // TOK == tok[None, :] // TOK
    later = (same & (tok[None, :] > tok[:, None])).astype(np.float32)
    earlier = (same & (tok[None, :] < tok[:, None])).astype(np.float32)
    bmask = np.where(same, 0.0, -1e30).astype(np.float32)
    cmask = np.where(same, np.where(later > 0, -10000.0, 0.0), -1e30).astype(np.float32)
    slot = np.tile(np.arange(QG), HH)
    rtab = np.where(tok[:, None] // TOK == slot[None, :] // KSEL, slot[None, :] % KSEL, -1).astype(np.float32)
    head = np.repeat(np.arange(HH), QG)
    hmask = (np.arange(HW)[:, None] // D0 == head[None, :]).astype(np.float32)

    before = (tok[:, None] < tok[None, :]).astype(np.float32)
    thr = np.broadcast_to(TS * np.arange(NTH, dtype=np.float32), (TS, NTH))
    below = np.broadcast_to((np.arange(E0)[None, :] < np.arange(E0)[:, None]).astype(np.float32), (TS, E0, E0))
    tile = np.arange(NT, dtype=np.float32).reshape(1, NT)

    n = np.arange(W1)
    expert = ((np.minimum(n // F1, E1)[None, :] == np.arange(E1 + 1)[:, None]) & (n < HID1)).astype(np.float32)

    def falling(n):
        return np.ascontiguousarray(np.broadcast_to(np.arange(n, 0, -1, dtype=np.float32), (R, n)))

    def tri(n):
        j, e = np.arange(n)[None, :], np.arange(n)[:, None]
        t = np.stack([(j > e), (j < e)], 1).astype(np.float32).reshape(1, n * 2 * n)
        return np.ascontiguousarray(np.broadcast_to(t, (R, n * 2 * n)))
    return dict(ident=np.eye(128, dtype=np.float32), before=before, thr=thr, below=below, tile=tile,
                cmask=cmask, bmask=bmask, later=later, earlier=earlier,
                rtab=rtab, hmask=hmask, order0=falling(E0), order=falling(E1), trig=tri(G1),
                expert=expert)


def kernel(**inputs):
    import concourse.bacc as _bacc
    from concourse.bass_utils import run_bass_kernel_spmd as _run

    a = {k: np.asarray(v) for k, v in inputs.items()}
    count = np.zeros((C_IN, HALO, HALO), np.float32)
    for dy, dx in SHIFTS:
        count[:, 1 + dy:1 + dy + PATCH, 1 + dx:1 + dx + PATCH] += 1
    t = _tables()
    rep = lambda v: np.ascontiguousarray(np.broadcast_to(np.asarray(v).reshape(1, -1), (R, np.asarray(v).size)))
    wqkv1 = a["L1_attn_w_qkv"].transpose(2, 1, 0, 3).reshape(D, 3 * A1)
    arrays = dict(
        x=_patches(a["x"]), tok_w=_shifted(a["L0_tok_W"]).reshape(KP, KB * NS * D),
        tok_g=_shifted(a["L0_tok_ln_gamma"])[..., 0], tok_be=_shifted(a["L0_tok_ln_beta"])[..., 0],
        tok_b=a["L0_tok_b"].reshape(1, D), tok_cnt=_parts(count.reshape(FEAT, 1)),
        wqkv=_halves(a["L0_attn_Wqkv_w"]),
        bqk=a["L0_attn_Wqkv_b"][:2 * D].reshape(4, HW).T,
        bv=rep(a["L0_attn_Wqkv_b"][2 * D:]), sel_w=_halves(a["L0_attn_sel_w"]), sel_b=rep(a["L0_attn_sel_b"]),
        temp=rep(a["L0_attn_temperature"]), wo=_halves(a["L0_attn_out_w"]), bo=rep(a["L0_attn_out_b"]),
        rt_w=_halves(a["L0_ffn_router_w"]), rt_b=rep(a["L0_ffn_router_b"]),
        w1=a["L0_ffn_w1"].reshape(E0, 2, HW, F0).transpose(0, 2, 1, 3),
        b1=a["L0_ffn_b1"].reshape(1, E0, F0),
        w2=a["L0_ffn_w2"].reshape(E0, FB0, 128, D).transpose(0, 2, 1, 3),
        b2=a["L0_ffn_b2"], gam=rep(a["L0_ffn_gamma"]), bet=rep(a["L0_ffn_beta"]),
        wqkv1=_halves(wqkv1), wo1=a["L1_attn_w_o"].reshape(MB1, 128, D).transpose(1, 0, 2),
        rt1_w=_halves(a["L1_ffn_router_w"].T), rt1_b=rep(a["L1_ffn_router_b"]), corr=rep(a["L1_ffn_corr_bias"]),
    )
    for name, g, s, b, bs in (("gate", "gWg", "sWg", "gbg", "sbg"), ("up", "gWu", "sWu", "gbu", "sbu")):
        w = np.concatenate([a["L1_ffn_" + g].transpose(1, 0, 2).reshape(D, E1 * F1), a["L1_ffn_" + s],
                            np.zeros((D, W1 - HID1), np.float32)], 1)
        arrays["w_" + name] = _halves(w)
        arrays["b_" + name] = _blocks(np.concatenate([a["L1_ffn_" + b].reshape(-1), a["L1_ffn_" + bs]]))
    wd = np.concatenate([a["L1_ffn_gWd"].reshape(E1 * F1, D), a["L1_ffn_sWd"]], 0)
    arrays["w_down"] = _blocks(wd)
    arrays["b_down"] = a["L1_ffn_gbd"]
    arrays["sb_down"] = a["L1_ffn_sbd"].reshape(1, D)
    for k, v in t.items():
        arrays[k + "_c"] = v
    nc = _bacc.Bacc("TRN2", target_bir_lowering=False, num_devices=1)
    arrays = {k: np.ascontiguousarray(v) for k, v in arrays.items()}
    args = {k: nc.dram_tensor("in_" + k, v.shape, mybir.dt.from_np(v.dtype), kind="ExternalInput").ap()
            for k, v in arrays.items()}
    args["out"] = nc.dram_tensor("out", (NG, R, D), mybir.dt.float32, kind="ExternalOutput").ap()
    vit_tower(nc, **args)
    r = _run(nc, [{"in_" + k: v for k, v in arrays.items()}], core_ids=[0])
    return r.results[0]["out"].reshape(NG * IPG, TOK, D)[:N_IMG]
```
